# Optimizing a Trainium2 kernel written in Bass

```python
import numpy as np
import jax
import jax.numpy as jnp

def _softmax(x, axis=-1):
    return jax.nn.softmax(x, axis=axis)

def _gelu(x):
    return jax.nn.gelu(x, approximate=True)

def _silu(x):
    return jax.nn.silu(x)

def _sigmoid(x):
    return jax.nn.sigmoid(x)

def _layernorm(x, axis=-1, eps=1e-05):
    m = jnp.mean(x, axis=axis, keepdims=True)
    v = jnp.var(x, axis=axis, keepdims=True)
    return (x - m) / jnp.sqrt(v + eps)

def _scatter_add(tgt, idx, src, axis=0):
    return tgt.at[idx].add(src)

def _segment_sum(src, seg, n):
    return jax.ops.segment_sum(src, seg, n)
kernel_name = 'mk_audio_tower_d2_tok_audfeat512_r4_8894b0'

def setup_inputs(seed: int=0):
    np.random.seed(seed)
    _w = jnp.asarray

    def _rec_inputs():
        import jax
        import jax.numpy as jnp
        _rk = jax.random.key(seed)
        x = 7.22013e-05 + 1.00017 * jax.random.normal(jax.random.fold_in(_rk, 1), (128, 375, 64), jnp.float32)
        return x
    x = _rec_inputs()

    def _L0_tok_setup():
        import jax, jax.numpy as jnp
        import numpy as np
        PATCH_LEN = 16
        STRIDE = 8
        D_MODEL = 128
        IN_CH = 64

        def _patch_embed(x, W, b, gamma, beta):
            B, S, C = x.shape
            n_patches = (S - PATCH_LEN) // STRIDE + 1
            idx = jnp.arange(n_patches)[:, None] * STRIDE + jnp.arange(PATCH_LEN)[None, :]
            patches = x[:, idx, :]
            patches = jnp.transpose(patches, (0, 1, 3, 2)).reshape(B, n_patches, C * PATCH_LEN)
            y = jnp.einsum('bpf,fd->bpd', patches, W) + b
            mu = jnp.mean(y, axis=-1, keepdims=True)
            var = jnp.mean(jnp.square(y - mu), axis=-1, keepdims=True)
            y = (y - mu) * jax.lax.rsqrt(var + 1e-05)
            return y * gamma + beta
        key = jax.random.key(seed)
        k1, k2, k3 = jax.random.split(key, 3)
        B, S, C = (32, 1024, IN_CH)
        x = jax.random.normal(k1, (B, S, C), dtype=jnp.float32)
        fan_in = PATCH_LEN * C
        bound = 1.0 / np.sqrt(fan_in)
        W = jax.random.uniform(k2, (fan_in, D_MODEL), minval=-bound, maxval=bound, dtype=jnp.float32)
        b = jax.random.uniform(k3, (D_MODEL,), minval=-bound, maxval=bound, dtype=jnp.float32)
        gamma = jnp.ones((D_MODEL,), dtype=jnp.float32)
        beta = jnp.zeros((D_MODEL,), dtype=jnp.float32)
        return {'x': x, 'W': W, 'b': b, 'gamma': gamma, 'beta': beta}
    _L0_tok_all = _L0_tok_setup()
    _L0_tok_in = {k: v for k, v in _L0_tok_all.items() if k in ('W', 'b', 'gamma', 'beta')}
    del _L0_tok_all

    def _L0_attn_setup():
        import jax, jax.numpy as jnp
        import numpy as np
        B_, L, D_MODEL = (8, 512, 128)
        EXPAND, D_STATE, HEADDIM, NGROUPS, D_CONV = (2, 16, 64, 1, 4)
        D_INNER = EXPAND * D_MODEL
        NHEADS = D_INNER // HEADDIM
        CONV_DIM = D_INNER + 2 * NGROUPS * D_STATE
        D_IN_PROJ = 2 * D_INNER + 2 * NGROUPS * D_STATE + NHEADS
        EPS = 1e-05

        def _mamba_params(key):
            ks = jax.random.split(key, 5)
            in_proj_w = jax.random.normal(ks[0], (D_IN_PROJ, D_MODEL), jnp.float32) * D_MODEL ** (-0.5)
            conv_w = jax.random.normal(ks[1], (CONV_DIM, 1, D_CONV), jnp.float32) * D_CONV ** (-0.5)
            conv_b = jnp.zeros((CONV_DIM,), jnp.float32)
            dt_bias = jnp.log(jnp.expm1(jax.random.uniform(ks[2], (NHEADS,), jnp.float32, 0.001, 0.1)))
            A_log = jnp.log(jax.random.uniform(ks[3], (NHEADS,), jnp.float32, 1.0, 16.0))
            Dp = jnp.ones((NHEADS,), jnp.float32)
            norm_w = jnp.ones((D_INNER,), jnp.float32)
            out_proj_w = jax.random.normal(ks[4], (D_MODEL, D_INNER), jnp.float32) * D_INNER ** (-0.5)
            return [in_proj_w, conv_w, conv_b, dt_bias, A_log, Dp, norm_w, out_proj_w]

        def _silu(v):
            return v * jax.nn.sigmoid(v)

        def _mamba2(u, in_proj_w, conv_w, conv_b, dt_bias, A_log, Dp, norm_w, out_proj_w):
            b, l, _ = u.shape
            zxbcdt = u @ in_proj_w.T
            z, xBC, dt = jnp.split(zxbcdt, [D_INNER, D_INNER + CONV_DIM], axis=-1)
            xc = jnp.transpose(xBC, (0, 2, 1))
            xc = jax.lax.conv_general_dilated(xc, conv_w, (1,), [(D_CONV - 1, 0)], feature_group_count=CONV_DIM)
            xBC = _silu(jnp.transpose(xc, (0, 2, 1)) + conv_b)
            xs, Bm, Cm = jnp.split(xBC, [D_INNER, D_INNER + NGROUPS * D_STATE], axis=-1)
            xs = xs.reshape(b, l, NHEADS, HEADDIM)
            Bm = Bm.reshape(b, l, NGROUPS, D_STATE)[:, :, 0]
            Cm = Cm.reshape(b, l, NGROUPS, D_STATE)[:, :, 0]
            dt = jax.nn.softplus(dt + dt_bias)
            A = -jnp.exp(A_log)
            dA = jnp.exp(dt * A)

            def step(h, inp):
                dA_t, dt_t, x_t, B_t, C_t = inp
                h = h * dA_t[:, :, None, None] + jnp.einsum('bh,bhp,bn->bhpn', dt_t, x_t, B_t)
                y = jnp.einsum('bhpn,bn->bhp', h, C_t)
                return (h, y)
            h0 = jnp.zeros((b, NHEADS, HEADDIM, D_STATE), u.dtype)
            seq = (jnp.moveaxis(dA, 1, 0), jnp.moveaxis(dt, 1, 0), jnp.moveaxis(xs, 1, 0), jnp.moveaxis(Bm, 1, 0), jnp.moveaxis(Cm, 1, 0))
            _, ys = jax.lax.scan(step, h0, seq)
            y = jnp.moveaxis(ys, 0, 1) + xs * Dp[None, None, :, None]
            y = y.reshape(b, l, D_INNER)
            y = y * _silu(z)
            y = y * jax.lax.rsqrt(jnp.mean(y * y, axis=-1, keepdims=True) + EPS) * norm_w
            return y @ out_proj_w.T
        key = jax.random.key(seed)
        k0, k1, k2 = jax.random.split(key, 3)
        d = {'x': jax.random.normal(k0, (B_, L, D_MODEL), jnp.float32)}
        names = ['in_proj_w', 'conv_w', 'conv_b', 'dt_bias', 'A_log', 'Dp', 'norm_w', 'out_proj_w']
        for pre, k in (('fwd_', k1), ('bwd_', k2)):
            for n, p in zip(names, _mamba_params(k)):
                d[pre + n] = p
        return d
    _L0_attn_all = _L0_attn_setup()
    _L0_attn_in = {k: v for k, v in _L0_attn_all.items() if k in ('fwd_in_proj_w', 'fwd_conv_w', 'fwd_conv_b', 'fwd_dt_bias', 'fwd_A_log', 'fwd_Dp', 'fwd_norm_w', 'fwd_out_proj_w', 'bwd_in_proj_w', 'bwd_conv_w', 'bwd_conv_b', 'bwd_dt_bias', 'bwd_A_log', 'bwd_Dp', 'bwd_norm_w', 'bwd_out_proj_w')}
    del _L0_attn_all

    def _L0_ffn_setup():
        import jax, jax.numpy as jnp
        import numpy as np
        NUM_EXPERTS = 8
        TOP_K = 2
        key = jax.random.key(seed)
        k0, k1, k2, k3, k4 = jax.random.split(key, 5)
        sl, bs, hs, ffn = (512, 2, 128, 512)
        T = sl * bs
        x = jax.random.normal(k0, (sl, bs, hs), jnp.float32)
        expert_weights = jax.random.uniform(k1, (T, TOP_K), jnp.float32)
        expert_indices = jax.random.randint(k2, (T, TOP_K), 0, NUM_EXPERTS)
        w1 = jax.random.normal(k3, (NUM_EXPERTS, hs, ffn), jnp.float32) * hs ** (-0.5)
        w2 = jax.random.normal(k4, (NUM_EXPERTS, ffn, hs), jnp.float32) * ffn ** (-0.5)
        return dict(x=x, expert_weights=expert_weights, expert_indices=expert_indices, w1=w1, w2=w2)
    _L0_ffn_all = _L0_ffn_setup()
    _L0_ffn_in = {k: v for k, v in _L0_ffn_all.items() if k in ('expert_weights', 'expert_indices', 'w1', 'w2')}
    del _L0_ffn_all

    def _L1_attn_setup():
        import jax, jax.numpy as jnp
        import numpy as np
        B, S, D_IN, UNITS = (8, 512, 128, 128)

        def _glorot(key, fan_in, fan_out):
            limit = np.sqrt(6.0 / (fan_in + fan_out)).astype(np.float32)
            return jax.random.uniform(key, (fan_in, fan_out), jnp.float32, -limit, limit)
        key = jax.random.key(seed)
        kq, kwq, kwv, kwk = jax.random.split(key, 4)
        return {'query': jax.random.normal(kq, (B, S, D_IN), jnp.float32), 'Wq': _glorot(kwq, D_IN, UNITS), 'Wv': _glorot(kwv, D_IN, UNITS), 'Wk': _glorot(kwk, D_IN, UNITS)}
    _L1_attn_all = _L1_attn_setup()
    _L1_attn_in = {k: v for k, v in _L1_attn_all.items() if k in ('Wq', 'Wv', 'Wk')}
    del _L1_attn_all

    def _L1_ffn_setup():
        import jax, jax.numpy as jnp
        import numpy as np
        H = 128
        I = 256
        E = 32
        K = 2
        key = jax.random.key(seed)
        ks = jax.random.split(key, 9)
        s = 0.02
        return {'hidden_states': jax.random.normal(ks[0], (2, 1024, H), dtype=jnp.float32), 'Wgate': jax.random.normal(ks[1], (H, E), dtype=jnp.float32) * s, 'bgate': jnp.zeros((E,), dtype=jnp.float32), 'Wg': jax.random.normal(ks[2], (E, H, I), dtype=jnp.float32) * s, 'bg': jnp.zeros((E, I), dtype=jnp.float32), 'Wu': jax.random.normal(ks[3], (E, H, I), dtype=jnp.float32) * s, 'bu': jnp.zeros((E, I), dtype=jnp.float32), 'Wd': jax.random.normal(ks[4], (E, I, H), dtype=jnp.float32) * s, 'bd': jnp.zeros((E, H), dtype=jnp.float32)}
    _L1_ffn_all = _L1_ffn_setup()
    _L1_ffn_in = {k: v for k, v in _L1_ffn_all.items() if k in ('Wgate', 'bgate', 'Wg', 'bg', 'Wu', 'bu', 'Wd', 'bd')}
    del _L1_ffn_all
    return {'x': x, 'L0_tok_W': _L0_tok_in['W'], 'L0_tok_b': _L0_tok_in['b'], 'L0_tok_gamma': _L0_tok_in['gamma'], 'L0_tok_beta': _L0_tok_in['beta'], 'L0_attn_fwd_in_proj_w': _L0_attn_in['fwd_in_proj_w'], 'L0_attn_fwd_conv_w': _L0_attn_in['fwd_conv_w'], 'L0_attn_fwd_conv_b': _L0_attn_in['fwd_conv_b'], 'L0_attn_fwd_dt_bias': _L0_attn_in['fwd_dt_bias'], 'L0_attn_fwd_A_log': _L0_attn_in['fwd_A_log'], 'L0_attn_fwd_Dp': _L0_attn_in['fwd_Dp'], 'L0_attn_fwd_norm_w': _L0_attn_in['fwd_norm_w'], 'L0_attn_fwd_out_proj_w': _L0_attn_in['fwd_out_proj_w'], 'L0_attn_bwd_in_proj_w': _L0_attn_in['bwd_in_proj_w'], 'L0_attn_bwd_conv_w': _L0_attn_in['bwd_conv_w'], 'L0_attn_bwd_conv_b': _L0_attn_in['bwd_conv_b'], 'L0_attn_bwd_dt_bias': _L0_attn_in['bwd_dt_bias'], 'L0_attn_bwd_A_log': _L0_attn_in['bwd_A_log'], 'L0_attn_bwd_Dp': _L0_attn_in['bwd_Dp'], 'L0_attn_bwd_norm_w': _L0_attn_in['bwd_norm_w'], 'L0_attn_bwd_out_proj_w': _L0_attn_in['bwd_out_proj_w'], 'L0_ffn_expert_weights': _L0_ffn_in['expert_weights'], 'L0_ffn_expert_indices': _L0_ffn_in['expert_indices'], 'L0_ffn_w1': _L0_ffn_in['w1'], 'L0_ffn_w2': _L0_ffn_in['w2'], 'L1_attn_Wq': _L1_attn_in['Wq'], 'L1_attn_Wv': _L1_attn_in['Wv'], 'L1_attn_Wk': _L1_attn_in['Wk'], 'L1_ffn_Wgate': _L1_ffn_in['Wgate'], 'L1_ffn_bgate': _L1_ffn_in['bgate'], 'L1_ffn_Wg': _L1_ffn_in['Wg'], 'L1_ffn_bg': _L1_ffn_in['bg'], 'L1_ffn_Wu': _L1_ffn_in['Wu'], 'L1_ffn_bu': _L1_ffn_in['bu'], 'L1_ffn_Wd': _L1_ffn_in['Wd'], 'L1_ffn_bd': _L1_ffn_in['bd']}

def reference(x, L0_tok_W, L0_tok_b, L0_tok_gamma, L0_tok_beta, L0_attn_fwd_in_proj_w, L0_attn_fwd_conv_w, L0_attn_fwd_conv_b, L0_attn_fwd_dt_bias, L0_attn_fwd_A_log, L0_attn_fwd_Dp, L0_attn_fwd_norm_w, L0_attn_fwd_out_proj_w, L0_attn_bwd_in_proj_w, L0_attn_bwd_conv_w, L0_attn_bwd_conv_b, L0_attn_bwd_dt_bias, L0_attn_bwd_A_log, L0_attn_bwd_Dp, L0_attn_bwd_norm_w, L0_attn_bwd_out_proj_w, L0_ffn_expert_weights, L0_ffn_expert_indices, L0_ffn_w1, L0_ffn_w2, L1_attn_Wq, L1_attn_Wv, L1_attn_Wk, L1_ffn_Wgate, L1_ffn_bgate, L1_ffn_Wg, L1_ffn_bg, L1_ffn_Wu, L1_ffn_bu, L1_ffn_Wd, L1_ffn_bd):
    import jax
    import jax.numpy as jnp

    def _L0_tok_ref(x, W, b, gamma, beta):
        import jax, jax.numpy as jnp
        import numpy as np
        PATCH_LEN = 16
        STRIDE = 8
        D_MODEL = 128
        IN_CH = 64

        def _patch_embed(x, W, b, gamma, beta):
            B, S, C = x.shape
            n_patches = (S - PATCH_LEN) // STRIDE + 1
            idx = jnp.arange(n_patches)[:, None] * STRIDE + jnp.arange(PATCH_LEN)[None, :]
            patches = x[:, idx, :]
            patches = jnp.transpose(patches, (0, 1, 3, 2)).reshape(B, n_patches, C * PATCH_LEN)
            y = jnp.einsum('bpf,fd->bpd', patches, W) + b
            mu = jnp.mean(y, axis=-1, keepdims=True)
            var = jnp.mean(jnp.square(y - mu), axis=-1, keepdims=True)
            y = (y - mu) * jax.lax.rsqrt(var + 1e-05)
            return y * gamma + beta
        return _patch_embed(x, W, b, gamma, beta)

    def _L0_attn_ref(x, fwd_in_proj_w, fwd_conv_w, fwd_conv_b, fwd_dt_bias, fwd_A_log, fwd_Dp, fwd_norm_w, fwd_out_proj_w, bwd_in_proj_w, bwd_conv_w, bwd_conv_b, bwd_dt_bias, bwd_A_log, bwd_Dp, bwd_norm_w, bwd_out_proj_w):
        import jax, jax.numpy as jnp
        import numpy as np
        B_, L, D_MODEL = (8, 512, 128)
        EXPAND, D_STATE, HEADDIM, NGROUPS, D_CONV = (2, 16, 64, 1, 4)
        D_INNER = EXPAND * D_MODEL
        NHEADS = D_INNER // HEADDIM
        CONV_DIM = D_INNER + 2 * NGROUPS * D_STATE
        D_IN_PROJ = 2 * D_INNER + 2 * NGROUPS * D_STATE + NHEADS
        EPS = 1e-05

        def _mamba_params(key):
            ks = jax.random.split(key, 5)
            in_proj_w = jax.random.normal(ks[0], (D_IN_PROJ, D_MODEL), jnp.float32) * D_MODEL ** (-0.5)
            conv_w = jax.random.normal(ks[1], (CONV_DIM, 1, D_CONV), jnp.float32) * D_CONV ** (-0.5)
            conv_b = jnp.zeros((CONV_DIM,), jnp.float32)
            dt_bias = jnp.log(jnp.expm1(jax.random.uniform(ks[2], (NHEADS,), jnp.float32, 0.001, 0.1)))
            A_log = jnp.log(jax.random.uniform(ks[3], (NHEADS,), jnp.float32, 1.0, 16.0))
            Dp = jnp.ones((NHEADS,), jnp.float32)
            norm_w = jnp.ones((D_INNER,), jnp.float32)
            out_proj_w = jax.random.normal(ks[4], (D_MODEL, D_INNER), jnp.float32) * D_INNER ** (-0.5)
            return [in_proj_w, conv_w, conv_b, dt_bias, A_log, Dp, norm_w, out_proj_w]

        def _silu(v):
            return v * jax.nn.sigmoid(v)

        def _mamba2(u, in_proj_w, conv_w, conv_b, dt_bias, A_log, Dp, norm_w, out_proj_w):
            b, l, _ = u.shape
            zxbcdt = u @ in_proj_w.T
            z, xBC, dt = jnp.split(zxbcdt, [D_INNER, D_INNER + CONV_DIM], axis=-1)
            xc = jnp.transpose(xBC, (0, 2, 1))
            xc = jax.lax.conv_general_dilated(xc, conv_w, (1,), [(D_CONV - 1, 0)], feature_group_count=CONV_DIM)
            xBC = _silu(jnp.transpose(xc, (0, 2, 1)) + conv_b)
            xs, Bm, Cm = jnp.split(xBC, [D_INNER, D_INNER + NGROUPS * D_STATE], axis=-1)
            xs = xs.reshape(b, l, NHEADS, HEADDIM)
            Bm = Bm.reshape(b, l, NGROUPS, D_STATE)[:, :, 0]
            Cm = Cm.reshape(b, l, NGROUPS, D_STATE)[:, :, 0]
            dt = jax.nn.softplus(dt + dt_bias)
            A = -jnp.exp(A_log)
            dA = jnp.exp(dt * A)

            def step(h, inp):
                dA_t, dt_t, x_t, B_t, C_t = inp
                h = h * dA_t[:, :, None, None] + jnp.einsum('bh,bhp,bn->bhpn', dt_t, x_t, B_t)
                y = jnp.einsum('bhpn,bn->bhp', h, C_t)
                return (h, y)
            h0 = jnp.zeros((b, NHEADS, HEADDIM, D_STATE), u.dtype)
            seq = (jnp.moveaxis(dA, 1, 0), jnp.moveaxis(dt, 1, 0), jnp.moveaxis(xs, 1, 0), jnp.moveaxis(Bm, 1, 0), jnp.moveaxis(Cm, 1, 0))
            _, ys = jax.lax.scan(step, h0, seq)
            y = jnp.moveaxis(ys, 0, 1) + xs * Dp[None, None, :, None]
            y = y.reshape(b, l, D_INNER)
            y = y * _silu(z)
            y = y * jax.lax.rsqrt(jnp.mean(y * y, axis=-1, keepdims=True) + EPS) * norm_w
            return y @ out_proj_w.T
        fwd = _mamba2(x, fwd_in_proj_w, fwd_conv_w, fwd_conv_b, fwd_dt_bias, fwd_A_log, fwd_Dp, fwd_norm_w, fwd_out_proj_w)
        bwd = _mamba2(x[:, ::-1], bwd_in_proj_w, bwd_conv_w, bwd_conv_b, bwd_dt_bias, bwd_A_log, bwd_Dp, bwd_norm_w, bwd_out_proj_w)
        return fwd + bwd[:, ::-1]

    def _L0_ffn_ref(x, expert_weights, expert_indices, w1, w2):
        import jax, jax.numpy as jnp
        import numpy as np
        NUM_EXPERTS = 8
        TOP_K = 2
        'Dropless MoE: sort assignments by expert, gather tokens, grouped MLP,\n            scatter-combine with top-k router weights (megablocks gather/scatter semantics).'
        in_shape = x.shape
        hs = in_shape[-1]
        x_flat = x.reshape(-1, hs)
        T = x_flat.shape[0]
        flat_ids = expert_indices.reshape(-1)
        order = jnp.argsort(flat_ids)
        bin_ids = flat_ids[order]
        token_ids = order // TOP_K
        xg = x_flat[token_ids]
        y = jnp.zeros_like(xg)
        for e in range(NUM_EXPERTS):
            h = jax.nn.gelu(xg @ w1[e], approximate=False)
            y = jnp.where((bin_ids == e)[:, None], h @ w2[e], y)
        w = expert_weights.reshape(-1)[order][:, None]
        out = jnp.zeros((T, hs), x.dtype).at[token_ids].add(w * y)
        return out.reshape(in_shape)

    def _L1_attn_ref(query, Wq, Wv, Wk):
        import jax, jax.numpy as jnp
        import numpy as np
        B, S, D_IN, UNITS = (8, 512, 128, 128)

        def _glorot(key, fan_in, fan_out):
            limit = np.sqrt(6.0 / (fan_in + fan_out)).astype(np.float32)
            return jax.random.uniform(key, (fan_in, fan_out), jnp.float32, -limit, limit)
        q = jax.nn.sigmoid(jnp.einsum('bsd,du->bsu', query, Wq))
        k = jax.nn.sigmoid(jnp.einsum('bsd,du->bsu', query, Wv))
        v = jax.nn.sigmoid(jnp.einsum('bsd,du->bsu', query, Wk))
        d_in = query.shape[-1]
        score = jnp.einsum('bqu,bku->bqk', q, k) / jnp.sqrt(jnp.float32(d_in))
        s = score.shape[1]
        masked = jnp.where(jnp.triu(jnp.ones((s, s), bool)), -jnp.inf, score)
        rest = jax.nn.softmax(masked[:, 1:, :], axis=-1)
        attn = jnp.concatenate([jnp.zeros((score.shape[0], 1, s), score.dtype), rest], axis=1)
        return jnp.einsum('bqk,bku->bqu', attn, v)

    def _L1_ffn_ref(hidden_states, Wgate, bgate, Wg, bg, Wu, bu, Wd, bd):
        import jax, jax.numpy as jnp
        import numpy as np
        H = 128
        I = 256
        E = 32
        K = 2
        B, S, Hs = hidden_states.shape
        x = hidden_states.reshape(-1, Hs)
        probs = jax.nn.softmax(x @ Wgate + bgate, axis=-1)
        router_w, sel = jax.lax.top_k(probs, K)
        comb = (jax.nn.one_hot(sel, E, dtype=x.dtype) * router_w[..., None]).sum(axis=1)

        def body(acc, xs):
            Wg_e, bg_e, Wu_e, bu_e, Wd_e, bd_e, w_e = xs
            h = jax.nn.silu(x @ Wg_e + bg_e) * (x @ Wu_e + bu_e)
            acc = acc + w_e[:, None] * (h @ Wd_e + bd_e)
            return (acc, None)
        acc0 = jnp.zeros_like(x)
        acc, _ = jax.lax.scan(body, acc0, (Wg, bg, Wu, bu, Wd, bd, comb.T))
        return acc.reshape(B, S, Hs)
    h = _L0_tok_ref(x, L0_tok_W, L0_tok_b, L0_tok_gamma, L0_tok_beta)
    h = h + _L0_attn_ref(_layernorm(h, axis=-1), L0_attn_fwd_in_proj_w, L0_attn_fwd_conv_w, L0_attn_fwd_conv_b, L0_attn_fwd_dt_bias, L0_attn_fwd_A_log, L0_attn_fwd_Dp, L0_attn_fwd_norm_w, L0_attn_fwd_out_proj_w, L0_attn_bwd_in_proj_w, L0_attn_bwd_conv_w, L0_attn_bwd_conv_b, L0_attn_bwd_dt_bias, L0_attn_bwd_A_log, L0_attn_bwd_Dp, L0_attn_bwd_norm_w, L0_attn_bwd_out_proj_w)
    h = h + _L0_ffn_ref(_layernorm(h, axis=-1), L0_ffn_expert_weights, L0_ffn_expert_indices, L0_ffn_w1, L0_ffn_w2)
    h = h + _L1_attn_ref(_layernorm(h, axis=-1), L1_attn_Wq, L1_attn_Wv, L1_attn_Wk)
    h = h + _L1_ffn_ref(_layernorm(h, axis=-1), L1_ffn_Wgate, L1_ffn_bgate, L1_ffn_Wg, L1_ffn_bg, L1_ffn_Wu, L1_ffn_bu, L1_ffn_Wd, L1_ffn_bd)
    return h

_drawn_inputs = setup_inputs


def setup_inputs(seed=0):
    import zlib

    import numpy as np

    out = dict(_drawn_inputs(seed))
    spreads = {'L0_tok_gamma': (1.0, 0.2),
     'L0_tok_beta': (0.0, 0.1),
     'L0_attn_fwd_conv_b': (0.0, 0.1),
     'L0_attn_fwd_Dp': (1.0, 0.2),
     'L0_attn_fwd_norm_w': (1.0, 0.2),
     'L0_attn_bwd_conv_b': (0.0, 0.1),
     'L0_attn_bwd_Dp': (1.0, 0.2),
     'L0_attn_bwd_norm_w': (1.0, 0.2),
     'L1_ffn_bgate': (0.0, 0.8),
     'L1_ffn_bg': (0.0, 0.8),
     'L1_ffn_bu': (0.0, 0.8),
     'L1_ffn_bd': (0.0, 0.8)}
    factors = {'L0_attn_fwd_A_log': 35.864,
     'L0_attn_bwd_dt_bias': 7.168,
     'L1_attn_Wq': 8.0,
     'L1_attn_Wv': 8.0,
     'L1_ffn_Wgate': 8.0,
     'L1_ffn_Wg': 8.0,
     'L1_ffn_Wu': 8.0,
     'L1_ffn_Wd': 8.0,
     'L0_attn_bwd_A_log': 6.18}
    for name, (base, spread) in spreads.items():
        noise = np.random.default_rng([zlib.crc32(name.encode()), seed]).standard_normal(out[name].shape)
        drawn = base * np.exp(spread * noise) if base else spread * noise
        out[name] = jnp.asarray(drawn.astype(out[name].dtype))
    for name, factor in factors.items():
        out[name] = (out[name] * factor).astype(out[name].dtype)
    return out
```

```python
import concourse.bass as bass
from concourse import mybir
from contextlib import ExitStack
import numpy as np

F32 = mybir.dt.float32
BF16 = mybir.dt.bfloat16
I32 = mybir.dt.int32
U32 = mybir.dt.uint32
ALU = mybir.AluOpType
ACT = mybir.ActivationFunctionType
AX_X = mybir.AxisListType.X

B, SEQ, CH = 128, 375, 64
BLK = 8
T = 45
NBLK = T + 1
FB = BLK * CH
D = 128
TOK = B * T
PT = 2 * T
NP = B // 2
QT = 2 * PT
NQ = B // 4
NH, HD, NS = 4, 64, 16
DI = NH * HD
EPS = 1e-5
LONGEST_DECAY = -200.0

PACK = dict(
    ident=128, later_f=PT, later_b=PT, upto_f=T, upto_b=T, gmask_f=PT, gmask_b=PT, amask=PT, tri=PT,
    iota32=32, tokw=8 * 128, tokb=1, gamma=128, beta=128, wdt=8, dtb=8, alog=8,
    wz=512, wx=5 * 128, cw=20, cb=5, dcol=4, wo=4 * 128, nw=4, wq=128, wk=128, wv=128,
    wgate=32, bgate=32, ones=2, onem=128, bcol=1,
)


def columns():
    at, out = 0, {}
    for name, n in PACK.items():
        out[name] = (at, at + n)
        at += n
    return out, at


COLS, NPACK = columns()


def at_least(eng, sem, value):
    if not isinstance(value, int) or value > 0:
        eng.wait_ge(sem, value)


def turns(eng, count, body):
    body(0)
    with eng.Fori(1, count) as i:
        body(i)


def wait_apart(eng, sem, value, passed):
    eng.wait_ge(sem, value)
    eng.sem_inc(passed, 1)


def stage_patches(nc, x, u_t, dt_dram, a_dram, h_dram, sb_pack, s_pack, load_pack):
    with ExitStack() as ctx:
        def sb(name, shape, dt=F32):
            return ctx.enter_context(nc.sbuf_tensor("pa_" + name, shape, dt))

        def sem(name):
            return ctx.enter_context(nc.semaphore("pa_" + name))

        def cst(name):
            return sb_pack[:, COLS[name][0]:COLS[name][1]]

        xin = sb("xin", [B, 4, FB])
        xt = sb("xt", [128, 4, 4, B])
        yt = sb("yt", [D, 2, B])
        st6 = sb("st6", [B, 2, 2, 6])
        mv = sb("mv", [B, 2, 2, 2])
        rs = sb("rs", [B, 2, 2])
        yn = sb("yn", [B, 2, D])
        yg = sb("yg", [B, 2, D])
        hh = sb("hh", [B, 2, D])
        uu = sb("uu", [B, 2, D])
        uc = sb("uc", [D, 2, B])
        xdt = sb("xdt", [B, T, 8])
        psx = [ctx.enter_context(nc.psum_tensor(f"pa_psx{k}", [128, 4, B], F32)) for k in range(2)]
        psy = [ctx.enter_context(nc.psum_tensor(f"pa_psy{k}", [D, 512], F32)) for k in range(2)]
        pst = [ctx.enter_context(nc.psum_tensor(f"pa_pst{k}", [B, 512], F32)) for k in range(2)]
        psu = ctx.enter_context(nc.psum_tensor("pa_psu", [D, 512], F32))
        psd = ctx.enter_context(nc.psum_tensor("pa_psd", [B, 512], F32))

        s_in = [sem(f"in{k}") for k in range(4)]
        s_xtp = sem("xtp")
        s_xt = sem("xt")
        s_y = sem("y")
        s_yt = sem("yt")
        s_ty = sem("ty")
        s_v = sem("v")
        s_tu = sem("tu")
        s_uc = sem("uc")
        s_ut = sem("ut")
        s_dt = sem("dt")
        s_r = sem("r")
        s_ve = sem("ve")
        s_wv, s_wp = sem("wv"), sem("wp")
        s_mh = sem("mh")
        mhalf = sb("mhalf", [B, 1])
        ve = sb("ve", [B, 2, 2])
        s_dtv = sem("dtv")
        s_h = [sem(f"h{k}") for k in range(2)]
        s_c = sem("c")
        s_sc = sem("sc")
        s_out = sem("out")
        NV = 8

        block = ctx.enter_context(nc.Block())
        def live(p, known, back):
            return known is None or 0 <= known - back < T

        FIRST = 4
        TURNS = (T - 2 - FIRST) // 4
        def steps(eng, step):
            for p in range(FIRST):
                step(eng, p, p % 2, p)
            with eng.Fori(0, TURNS) as i:
                for k in range(4):
                    step(eng, 4 * i + FIRST + k, (FIRST + k) % 2, None, (FIRST + k + 1) % 4)
            for p in range(FIRST + 4 * TURNS, T + 3):
                step(eng, p, p % 2, p)

        hv = h_dram.rearrange("(b t) d -> b t d", t=T)

        def x_block(b):
            return x[:, b * BLK:(b + 1) * BLK, :].rearrange("b l c -> b (l c)") if isinstance(b, int) else \
                x[:, bass.ds(b * BLK, BLK), :].rearrange("b l c -> b (l c)")

        def sp_step(sp, p, s, known, bs=None):
            if known is None or known + 3 < NBLK:
                k = (known + 3) % 4 if known is not None else (bs + 2) % 4
                at_least(sp, s_xtp, p)
                sp.dma_start(xin[:, k, :], x_block(p + 3)).then_inc(s_in[k], 16)
            if live(p, known, 1):
                q, o = p - 1, 1 - s
                sp.wait_ge(s_v, NV * q + 5)
                dst = hv[:, q, :] if isinstance(q, int) else hv[:, bass.ds(q, 1), :].rearrange("b o d -> b (o d)")
                sp.dma_start(dst, hh[:, o, :]).then_inc(s_h[o], 16)

        @block.sync
        def _(sp):
            sp.dma_start(sb_pack[:], load_pack).then_inc(s_pack, 16)
            for b in range(3):
                sp.dma_start(xin[:, b, :], x_block(b)).then_inc(s_in[b], 16)
            steps(sp, sp_step)



        def transposes(pe, b, bs, known):
            pe.wait_ge(s_in[bs], 16 * (b // 4 + 1) if known is not None else 16 * ((b >> 2) + 1))
            at_least(pe, s_xt, b - 1)
            for c in range(4):
                last = nc.tensor.transpose(psx[bs % 2][:, c, :], xin[:, bs, c * 128:(c + 1) * 128], cst("ident"))
            last.then_inc(s_xtp, 1)

        def pe_step(pe, p, s, known, bs=None):
            if live(p, known, 0):
                if known == 0:
                    pe.wait_ge(s_pack, 16)
                    transposes(pe, 0, 0, 0)
                bb = (known + 1) % 4 if known is not None else bs
                transposes(pe, p + 1, bb, known)
                pe.wait_ge(s_xt, p + 2)
                at_least(pe, s_yt, p - 1)
                for half in range(2):
                    for c in range(4):
                        last = nc.tensor.matmul(psy[s][:, 0:B], cst("tokw").rearrange("p (k d) -> p k d", k=8)[:, half * 4 + c, :],
                                                xt[:, (bb - 1 + half) % 4, c, :], start=(half + c == 0), stop=(half * 4 + c == 7))
                last.then_inc(s_y, 1)
            if live(p, known, 1):
                q = p - 1
                pe.wait_ge(s_yt, q + 1)
                at_least(pe, s_v, NV * (q - 2) + 3 if known is None or q >= 2 else 0)
                nc.tensor.transpose(pst[1 - s][:, 0:D], yt[:, 1 - s, :], cst("ident")).then_inc(s_ty, 1)
            if live(p, known, 2):
                q = p - 2
                pe.wait_ge(s_v, NV * (q + 1))
                at_least(pe, s_uc, q)
                nc.tensor.transpose(psu[:, 0:B], uu[:, s, :], cst("ident")).then_inc(s_tu, 1)
            if live(p, known, 3):
                q = p - 3
                pe.wait_ge(s_uc, q + 1)
                at_least(pe, s_dtv, q)
                nc.tensor.matmul(psd[:, 0:8], uc[:, 1 - s, :], cst("wdt"), start=True, stop=True).then_inc(s_dt, 1)

        def act_evacuate(act, b, bs):
            act.wait_ge(s_xtp, b + 1)
            at_least(act, s_y, b - 4 + 1 if isinstance(b, int) and b >= 4 or not isinstance(b, int) else 0)
            nc.scalar.activation(xt[:, bs, :, :], psx[bs % 2][:], ACT.Copy).then_inc(s_xt, 1)

        def act_step(act, p, s, known, bs=None):
            if live(p, known, 0):
                if known == 0:
                    act_evacuate(act, 0, 0)
                bb = (known + 1) % 4 if known is not None else bs
                act_evacuate(act, p + 1, bb)
                act.wait_ge(s_y, p + 1)
                at_least(act, s_ty, p - 1)
                nc.scalar.activation(yt[:, s, :], psy[s][:, 0:B], ACT.Identity, bias=cst("tokb")).then_inc(s_yt, 1)
            if live(p, known, 2):
                q = p - 2
                act.wait_ge(s_tu, q + 1)
                at_least(act, s_dt, q - 1)
                at_least(act, s_ut, q - 1)
                nc.scalar.activation(uc[:, s, :], psu[:, 0:B], ACT.Copy).then_inc(s_uc, 1)

        def pool_step(pool, p, s, known, bs=None):
            if live(p, known, 2):
                q = p - 2
                pool.wait_ge(s_uc, q + 1)
                out = u_t.rearrange("d (b t) -> d b t", t=T)
                out = out[:, :, q] if isinstance(q, int) else out[:, :, bass.ds(q, 1)].rearrange("d b o -> d (b o)")
                nc.gpsimd.tensor_copy(out, uc[:, s, :]).then_inc(s_ut, 1)
            if live(p, known, 1):
                q, o = p - 1, 1 - s
                for k, ready in ((0, 2), (1, 7)):
                    wait_apart(pool, s_v, NV * q + ready, s_wp)
                    nc.gpsimd.tensor_scalar(ve[:, o, k:k + 1], mv[:, o, k, 1:2], EPS, None, ALU.add).then_inc(s_ve, 1)
                    pool.wait_ge(s_ve, 2 * q + k + 1)
                    nc.gpsimd.tensor_tensor(rs[:, o, k:k + 1], ve[:, o, k:k + 1], mhalf[:], ALU.pow).then_inc(s_r, 1)

        def dve_step(dve, p, s, known, bs=None):
            if live(p, known, 1):
                q, o = p - 1, 1 - s
                n = [0]

                def then(ins):
                    ins.then_inc(s_v, 1)
                    n[0] += 1
                    if n[0] < NV:
                        if n[0] in (1, 6):
                            wait_apart(dve, s_v, NV * q + n[0], s_wv)
                        else:
                            dve.wait_ge(s_v, NV * q + n[0])

                dve.wait_ge(s_ty, q + 1)
                at_least(dve, s_v, NV * q if known is None or q > 0 else 0)
                then(nc.vector.bn_stats(st6[:, o, 0, :], pst[o][:, 0:D]))
                then(nc.vector.bn_aggr(mv[:, o, 0, :], st6[:, o, 0, :]))
                dve.wait_ge(s_r, 2 * q + 1)
                then(nc.vector.tensor_scalar(yn[:, o, :], pst[o][:, 0:D], mv[:, o, 0, 0:1], rs[:, o, 0:1], ALU.subtract, ALU.mult))
                then(nc.vector.tensor_tensor(yg[:, o, :], yn[:, o, :], cst("gamma"), ALU.mult))
                at_least(dve, s_h[o], 16 * ((q - o) // 2) if known is not None else 16 * ((q - o) >> 1))
                then(nc.vector.tensor_tensor(hh[:, o, :], yg[:, o, :], cst("beta"), ALU.add))
                then(nc.vector.bn_stats(st6[:, o, 1, :], hh[:, o, :]))
                then(nc.vector.bn_aggr(mv[:, o, 1, :], st6[:, o, 1, :]))
                dve.wait_ge(s_r, 2 * q + 2)
                at_least(dve, s_tu, q - 1)
                then(nc.vector.tensor_scalar(uu[:, o, :], hh[:, o, :], mv[:, o, 1, 0:1], rs[:, o, 1:2], ALU.subtract, ALU.mult))
            if live(p, known, 3):
                q = p - 3
                dve.wait_ge(s_dt, q + 1)
                out = xdt[:, q, :] if isinstance(q, int) else xdt[:, bass.ds(q, 1), :].rearrange("b o e -> b (o e)")
                nc.vector.tensor_tensor(out, psd[:, 0:8], cst("dtb"), ALU.add).then_inc(s_dtv, 1)

        @block.tensor
        def _(pe):
            steps(pe, pe_step)

        n8 = T * 8
        e, w, sl, t1 = (sb(n, [B, n8]) for n in ("e", "w", "sl", "t1"))
        al = sb("al", [B, 8])
        dtv, av = (sb(n, [B, T, 8]) for n in ("dtv", "av"))
        xf = xdt[:].rearrange("b t e -> b (t e)")

        @block.scalar
        def _(act):
            act.wait_ge(s_pack, 16)
            steps(act, act_step)
            act.wait_ge(s_c, 1)
            nc.scalar.activation(e[:], t1[:], ACT.Exp, scale=-1.0).then_inc(s_sc, 1)
            nc.scalar.activation(al[:], al[:], ACT.Exp).then_inc(s_sc, 1)
            act.wait_ge(s_c, 3)
            nc.scalar.activation(w[:], w[:], ACT.Ln).then_inc(s_sc, 1)

        @block.vector
        def _(dve):
            dve.wait_ge(s_pack, 16)
            nc.vector.tensor_scalar(al[:], cst("alog"), 88.0, None, ALU.min)
            steps(dve, dve_step)
            c = [0]

            def then(ins):
                ins.then_inc(s_c, 1)
                c[0] += 1
                dve.wait_ge(s_c, c[0])

            dve.wait_ge(s_dtv, T)
            then(nc.vector.scalar_tensor_tensor(t1[:], xf, -1.0, xf, ALU.mult, ALU.max))
            dve.wait_ge(s_sc, 2)
            then(nc.vector.tensor_scalar(sl[:], e[:], 1.0 / 7.0, -1.0 / 6.0, ALU.mult, ALU.add))
            then(nc.vector.tensor_scalar(w[:], e[:], 1.0, None, ALU.add))
            for coef in (1.0 / 5.0, -1.0 / 4.0, 1.0 / 3.0, -1.0 / 2.0, 1.0):
                then(nc.vector.tensor_tensor(sl[:], sl[:], e[:], ALU.mult))
                then(nc.vector.tensor_scalar(sl[:], sl[:], coef, None, ALU.add))
            then(nc.vector.tensor_tensor(sl[:], sl[:], e[:], ALU.mult))
            dve.wait_ge(s_sc, 3)
            then(nc.vector.tensor_tensor(w[:], w[:], sl[:], ALU.subtract))
            then(nc.vector.scalar_tensor_tensor(w[:], e[:], 0.0625, w[:], ALU.is_gt, ALU.mult))
            then(nc.vector.tensor_tensor(sl[:], sl[:], w[:], ALU.add))
            dt_flat = dtv[:].rearrange("b t e -> b (t e)")
            then(nc.vector.scalar_tensor_tensor(dt_flat, xf, 0.0, sl[:], ALU.max, ALU.add))
            for k in range(8):
                then(nc.vector.tensor_scalar(av[:, :, k], dtv[:, :, k], al[:, k:k + 1], None, ALU.mult))
            avf = av[:].rearrange("b t e -> b (t e)")
            then(nc.vector.tensor_scalar(avf, avf, -1.0, LONGEST_DECAY, ALU.mult, ALU.max))


        @block.gpsimd
        def _(pool):
            nc.gpsimd.memset(mhalf[:], -0.5).then_inc(s_mh, 1)
            pool.wait_ge(s_mh, 1)
            steps(pool, pool_step)
            pool.wait_ge(s_c, 3 + 10 + 1 + 3 + 1 + 8 + 1)
            pool.dma_start(dt_dram, dtv[:].rearrange("b t e -> b (t e)")).then_inc(s_out, 16)
            pool.dma_start(a_dram, av[:].rearrange("b t e -> b (t e)")).then_inc(s_out, 16)
            pool.wait_ge(s_out, 32)
            pool.wait_ge(s_h[0], 16 * ((T + 1) // 2))
            pool.wait_ge(s_h[1], 16 * (T // 2))
            pool.wait_ge(s_ut, T)


def stage_mamba(nc, u_t, pk, dt_dram, a_dram, h_dram, h1_dram, loads=()):
    with ExitStack() as ctx:
        def sb(name, shape, dt=F32):
            return ctx.enter_context(nc.sbuf_tensor("mb_" + name, shape, dt))

        def ps(name):
            return ctx.enter_context(nc.psum_tensor("mb_" + name, [128, 512], F32))

        def sem(name):
            return ctx.enter_context(nc.semaphore("mb_" + name))

        def cst(name, parts=128):
            return pk[0:parts, COLS[name][0]:COLS[name][1]]

        acc = sb("acc", [128, 2, 5, QT])
        th = sb("th", [128, 5, QT])
        xs = sb("xs", [128, 2, 4, QT])
        bcs = sb("bcs", [NS, 2, 4, QT])
        tz = sb("tz", [128, 2, 2, QT])
        gz = sb("gz", [128, 2, 4, QT])
        dta = sb("dta", [PT, NP, 8])
        aa = sb("aa", [PT, NP, 8])
        a2 = sb("a2", [PT, 2, 2, 2, NH, T])
        ee = sb("ee", [PT, 2, 2, NH, T])
        gm = sb("gm", [PT, 2, 2, PT])
        tt = sb("tt", [PT, 2, 2, NH, PT])
        xd = sb("xd", [PT, 2, 8, HD])
        yv = sb("yv", [128, 4, QT])
        yg = sb("yg", [128, 4, QT])
        sq = sb("sq", [128, 4, QT])
        hq = sb("hq", [PT, 2, 2, D])
        ho = sb("ho", [PT, 2, 2, D])
        hm = sb("hm", [PT, 2, D])
        var = sb("var", [PT, 2, 2])
        rr = sb("rr", [PT, 2, 2])
        mhalf = sb("mhalf", [PT, 2])
        won = sb("won", [128, 4, D])
        psx = [ps("psx0"), ps("psx1")]
        psz, pss, pst, psg, = ps("psz"), ps("pss"), ps("pst"), ps("psg")
        psy = [ps("psy0"), ps("psy1")]

        s_ld, s_k, s_mh = sem("ld"), sem("k"), sem("mh")
        s_xp = sem("xp")
        s_zp = sem("zp")
        s_t0 = sem("t0")
        s_dc = sem("dc")
        s_th = sem("th")
        s_si = sem("si")
        s_tz = sem("tz")
        s_gz = sem("gz")
        s_a2 = sem("a2")
        s_s = sem("s")
        s_e = sem("e")
        s_g = sem("g")
        s_gm = sem("gm")
        s_tt = sem("tt")
        s_xt = sem("xt")
        s_xd = sem("xd")
        s_y = sem("y")
        s_yv = sem("yv")
        s_yg = sem("yg")
        s_sq = sem("sq")
        s_o = sem("o")
        s_va = sem("va")
        s_rr = sem("rr")
        s_h = sem("h")
        s_hq = [sem("hq0"), sem("hq1")]
        s_st = [sem("st0"), sem("st1")]

        block = ctx.enter_context(nc.Block())

        FIRST = 4

        def steps(eng, turn):
            for t in range(FIRST):
                turn(t, t % 2, lambda k, t=t: 0 <= t - k < NQ)
            with eng.Fori(0, (NQ - FIRST) // 2) as i:
                for s in range(2):
                    turn(2 * i + FIRST + s, s, lambda k: True)
            for t in range(NQ, NQ + 3):
                turn(t, t % 2, lambda k, t=t: 0 <= t - k < NQ)

        def half(n, s):
            return (n - s) // 2 if isinstance(n, int) else (n - s) >> 1

        def rows(dram, n):
            v = dram.rearrange("(n j r) d -> n r j d", j=2, r=PT)
            return v[n] if isinstance(n, int) else v[bass.ds(n, 1)].rearrange("o r j d -> (o r) j d")

        flat = lambda a: a.rearrange("p k q -> p (k q)")
        GROUPS = ((0, 1), (2, 3), (4,))
        pair_cols = lambda j: slice(j * PT, (j + 1) * PT)

        @block.sync
        def _(sp):
            v = lambda a: a.rearrange("b (t e) -> (b t) e", e=8).rearrange("(p r) e -> r p e", r=PT)
            sp.dma_start(dta[:], v(dt_dram)).then_inc(s_ld, 16)
            sp.dma_start(aa[:], v(a_dram)).then_inc(s_ld, 16)

            def turn(t, s, live):
                if live(2):
                    n = t - 2
                    at_least(sp, s_h, 4 * n - 4)
                    sp.dma_start(hq[:, s], rows(h_dram, n)).then_inc(s_hq[s], 16)
                if live(0):
                    for dst, src, s_load in loads:
                        at = slice(t, t + 1) if isinstance(t, int) else bass.ds(t, 1)
                        sp.dma_start(dst(at), src(at)).then_inc(s_load, 16)
                if live(3):
                    n = t - 3
                    sp.wait_ge(s_h, 4 * n + 4)
                    sp.dma_start(rows(h1_dram, n), ho[:, 1 - s]).then_inc(s_st[1 - s], 16)

            steps(sp, turn)
            for s in range(2):
                sp.wait_ge(s_st[s], 16 * (NQ // 2))

        @block.tensor
        def _(pe):
            pe.wait_ge(s_k, 4)

            def in_proj(n, s, g):
                bank = psx[(3 * s + g) % 2]
                at_least(pe, s_dc, 18 * n + 6 * (g - 1))
                u = u_t[:, n * QT:(n + 1) * QT] if isinstance(n, int) else u_t[:, bass.ds(n * QT, QT)]
                for k in GROUPS[g]:
                    last = nc.tensor.matmul(bank[:, (k % 2) * QT:(k % 2 + 1) * QT], cst("wx")[:, k * 128:(k + 1) * 128],
                                            u, start=True, stop=True)
                last.then_inc(s_xp, 1)

            def in_proj_z(n, d):
                at_least(pe, s_gz, 2 * n + d)
                u = u_t[:, n * QT:(n + 1) * QT] if isinstance(n, int) else u_t[:, bass.ds(n * QT, QT)]
                for k in (2 * d, 2 * d + 1):
                    last = nc.tensor.matmul(psz[:, (k % 2) * QT:(k % 2 + 1) * QT], cst("wz")[:, k * 128:(k + 1) * 128],
                                            u, start=True, stop=True)
                last.then_inc(s_zp, 1)

            def exponents(n, s, j):
                m = 2 * n + j
                pe.wait_ge(s_a2, 2 * m + 2)
                at_least(pe, s_e, m)
                for d in range(2):
                    last = nc.tensor.matmul(pss[0:PT, d * 180:(d + 1) * 180], cst(("later_f", "later_b")[d], PT),
                                            a2[:, s, j, d].rearrange("k h i -> k (h i)"), start=True, stop=True)
                last.then_inc(s_s, 1)

            def transpose_x(n, s, j):
                m = 2 * n + j
                pe.wait_ge(s_si, 8 * n + 4)
                at_least(pe, s_xd, m)
                for k in range(4):
                    last = nc.tensor.transpose(pst[0:PT, k * 128:(k + 1) * 128], xs[:, s, k, pair_cols(j)], cst("ident"))
                last.then_inc(s_xt, 1)

            def b_times_c(n, s):
                pe.wait_ge(s_si, 8 * n + 8)
                at_least(pe, s_gm, n)
                at_least(pe, s_h, 4 * n - 4)
                for j in range(2):
                    for d in range(2):
                        c = pair_cols(j)
                        last = nc.tensor.matmul(psg[0:PT, (2 * j + d) * PT:(2 * j + d + 1) * PT], bcs[:, s, 2 * d, c], bcs[:, s, 2 * d + 1, c],
                                                start=True, stop=True)
                last.then_inc(s_g, 1)

            def scan(n, j):
                m = 2 * n + j
                if j == 0:
                    at_least(pe, s_yv, 4 * n)
                pe.wait_ge(s_tt, 2 * m + 2)
                pe.wait_ge(s_xd, m + 1)
                for e in range(8):
                    k = e // 2
                    last = nc.tensor.matmul(psy[k // 2][64 * (e % 2):64 * (e % 2) + 64, (k % 2) * QT + j * PT:(k % 2) * QT + (j + 1) * PT],
                                            xd[:, j, e, :], tt[:, j, e // 4, e % 4, :], start=True, stop=True)
                last.then_inc(s_y, 1)

            def out_proj(n, j, g_done):
                m = 2 * n + j
                c = pair_cols(j)
                pe.wait_ge(s_yg, n + 1)
                pe.wait_ge(s_sq, n + 1)
                at_least(pe, s_h, 2 * m)
                at_least(pe, s_gm, g_done)
                for d in range(2):
                    for k in (2 * d, 2 * d + 1):
                        nc.tensor.matmul(psg[0:PT, d * D:(d + 1) * D], yg[:, k, c], won[:, k, :],
                                         start=(k % 2 == 0), stop=(k % 2 == 1))
                    for k in (2 * d, 2 * d + 1):
                        last = nc.tensor.matmul(psg[0:PT, 2 * D + 2 * d:2 * D + 2 + 2 * d], sq[:, k, c], cst("ones"),
                                                start=(k % 2 == 0), stop=(k % 2 == 1))
                last.then_inc(s_o, 1)

            def turn(t, s, live):
                g_done = min(t - 1, NQ) if isinstance(t, int) else t - 1
                if live(3):
                    out_proj(t - 3, 0, g_done)
                if live(0):
                    in_proj(t, s, 0)
                if live(2):
                    scan(t - 2, 0)
                    scan(t - 2, 1)
                if live(1):
                    transpose_x(t - 1, 1 - s, 0)
                    exponents(t - 1, 1 - s, 0)
                if live(3):
                    out_proj(t - 3, 1, g_done)
                if live(0):
                    in_proj(t, s, 1)
                if live(1):
                    transpose_x(t - 1, 1 - s, 1)
                    exponents(t - 1, 1 - s, 1)
                if live(0):
                    in_proj_z(t, 0)
                if live(1):
                    b_times_c(t - 1, 1 - s)
                if live(0):
                    in_proj(t, s, 2)
                    in_proj_z(t, 1)

            steps(pe, turn)

        @block.scalar
        def _(act):
            def first_tap(n, s, g):
                act.wait_ge(s_xp, 3 * n + g + 1)
                at_least(act, s_si, 8 * n - 8)
                for k in GROUPS[g]:
                    nc.scalar.activation(acc[:, s, k, :], psx[(3 * s + g) % 2][:, (k % 2) * QT:(k % 2 + 1) * QT], ACT.Identity,
                                         bias=cst("cb")[:, k:k + 1], scale=cst("cw")[:, 4 * k + 3:4 * k + 4]).then_inc(s_t0, 1)

            def tanh_z(n, d):
                act.wait_ge(s_zp, 2 * n + d + 1)
                at_least(act, s_gz, 2 * n + d - 1)
                nc.scalar.activation(flat(tz[:, d]), psz[:, 0:2 * QT], ACT.Tanh, scale=0.5).then_inc(s_tz, 1)

            def tanh_x(n, s, g):
                act.wait_ge(s_dc, 18 * n + 6 * (g + 1))
                at_least(act, s_si, 8 * n)
                lo, hi = GROUPS[g][0], GROUPS[g][-1] + 1
                nc.scalar.activation(flat(th[:, lo:hi, :]), flat(acc[:, s, lo:hi, :]), ACT.Tanh, scale=0.5).then_inc(s_th, 1)

            def decays(n, j):
                m = 2 * n + j
                act.wait_ge(s_s, m + 1)
                at_least(act, s_tt, 2 * m - 2)
                nc.scalar.activation(ee[:, j].rearrange("k d h i -> k (d h i)"), pss[0:PT, 0:360], ACT.Exp).then_inc(s_e, 1)

            def turn(t, s, live):
                if live(0):
                    first_tap(t, s, 0)
                if live(1):
                    decays(t - 1, 0)
                if live(0):
                    first_tap(t, s, 1)
                    tanh_x(t, s, 0)
                if live(1):
                    decays(t - 1, 1)
                if live(2):
                    act.wait_ge(s_yg, t - 1)
                    at_least(act, s_o, 2 * (t - 2))
                    nc.scalar.activation(flat(sq[:]), flat(yg[:]), ACT.Square).then_inc(s_sq, 1)
                if live(0):
                    tanh_z(t, 0)
                    first_tap(t, s, 2)
                    tanh_x(t, s, 1)
                    tanh_z(t, 1)
                    tanh_x(t, s, 2)

            steps(act, turn)

        @block.vector
        def _(dve):
            for k in range(4):
                nc.vector.tensor_scalar(won[:, k, :], cst("wo")[:, k * D:(k + 1) * D], cst("nw")[:, k:k + 1], None, ALU.mult).then_inc(s_k, 1)
            dve.wait_ge(s_ld, 32)

            def taps(n, s, g):
                parts = ([(0, 0, 128, False), (1, 0, 128, False)], [(2, 0, 128, True), (3, 0, 128, True)],
                         [(4, 0, 64, False), (4, 64, 128, True)])[g]
                by_batch = lambda ap: ap.rearrange("p (b t) -> p b t", t=T)
                dve.wait_ge(s_t0, 5 * n + (2, 4, 5)[g])
                for back in (1, 2, 3):
                    for j, (k, lo, hi, rev) in enumerate(parts):
                        w = cst("cw")[lo:hi, 4 * k + 3 - back:4 * k + 4 - back]
                        x = by_batch(psx[(3 * s + g) % 2][lo:hi, (k % 2) * QT:(k % 2 + 1) * QT])
                        a = by_batch(acc[lo:hi, s, k, :])
                        x, a = (x[:, :, back:], a[:, :, :T - back]) if rev else (x[:, :, :T - back], a[:, :, back:])
                        if back > 1:
                            dve.wait_ge(s_dc, 18 * n + 6 * g + 2 * (back - 1) + j - 1)
                        nc.vector.scalar_tensor_tensor(a, x, w, a, ALU.mult, ALU.add).then_inc(s_dc, 1)

            def gate(n, s, d):
                dve.wait_ge(s_tz, 2 * n + d + 1)
                if d == 0:
                    at_least(dve, s_yg, n - 1)
                nc.vector.scalar_tensor_tensor(flat(gz[:, s, 2 * d:2 * d + 2]), flat(tz[:, d]),
                                               1.0, psz[:, 0:2 * QT], ALU.add, ALU.mult).then_inc(s_gz, 1)

            def silu(n, s, g):
                dve.wait_ge(s_th, 3 * n + g + 1)
                if g < 2:
                    if g == 0:
                        at_least(dve, s_yv, 4 * n - 4)
                        at_least(dve, s_xt, 2 * n - 2)
                    for k in GROUPS[g]:
                        nc.vector.scalar_tensor_tensor(xs[:, s, k, :], th[:, k, :], 1.0, acc[:, s, k, :], ALU.add, ALU.mult).then_inc(s_si, 1)
                else:
                    at_least(dve, s_g, n - 1)
                    for e in range(4):
                        p = slice(32 * e, 32 * e + NS)
                        nc.vector.scalar_tensor_tensor(bcs[:, s, e, :], th[p, 4, :], 1.0, acc[p, s, 4, :], ALU.add, ALU.mult).then_inc(s_si, 1)

            def dt_times_x(n, j):
                m = 2 * n + j
                dve.wait_ge(s_xt, m + 1)
                at_least(dve, s_y, m - 1)
                steps_dt = dta[:, m, :] if isinstance(m, int) else dta[:, bass.ds(m, 1), :].rearrange("r o e -> r (o e)")
                nc.vector.tensor_tensor(xd[:, j], pst[0:PT, :].rearrange("r (e q) -> r e q", e=8),
                                        steps_dt.unsqueeze(2).broadcast_to([PT, 8, HD]), ALU.mult).then_inc(s_xd, 1)

            def mask(n):
                dve.wait_ge(s_g, n + 1)
                at_least(dve, s_tt, 4 * n)
                masks = pk[0:PT, COLS["gmask_f"][0]:COLS["gmask_b"][1]].unsqueeze(1).broadcast_to([PT, 2, 2 * PT])
                nc.vector.tensor_tensor(gm[:].rearrange("r j d i -> r j (d i)"), psg[0:PT, 0:4 * PT].rearrange("r (j e) -> r j e", j=2),
                                        masks, ALU.mult).then_inc(s_gm, 1)

            def skip(n, s):
                dve.wait_ge(s_y, 2 * n + 2)
                at_least(dve, s_yg, n)
                for k in range(4):
                    nc.vector.scalar_tensor_tensor(yv[:, k, :], xs[:, s, k, :], cst("dcol")[:, k:k + 1],
                                                   psy[k // 2][:, (k % 2) * QT:(k % 2 + 1) * QT], ALU.mult, ALU.add).then_inc(s_yv, 1)

            def mean_square(n, j):
                m = 2 * n + j
                dve.wait_ge(s_o, m + 1)
                at_least(dve, s_rr, m - 1)
                sums = psg[0:PT, 2 * D:2 * D + 4].rearrange("r (d o) -> r d o", o=2)[:, :, 0]
                nc.vector.tensor_scalar(var[:, j, :], sums, 1.0 / DI, 16 * EPS, ALU.mult, ALU.add).then_inc(s_va, 1)

            def residual(n, s, j):
                m = 2 * n + j
                dve.wait_ge(s_rr, m + 1)
                if j == 0:
                    dve.wait_ge(s_hq[s], 16 * (half(n, s) + 1))
                    at_least(dve, s_st[s], 16 * half(n, s))
                nc.vector.scalar_tensor_tensor(hm[:, j, :], psg[0:PT, 0:D], rr[:, j, 0:1], hq[:, s, j, :],
                                               ALU.mult, ALU.add).then_inc(s_h, 1)
                dve.wait_ge(s_h, 2 * m + 1)
                nc.vector.scalar_tensor_tensor(ho[:, s, j, :], psg[0:PT, D:2 * D], rr[:, j, 1:2], hm[:, j, :],
                                               ALU.mult, ALU.add).then_inc(s_h, 1)

            def turn(t, s, live):
                if live(3):
                    mean_square(t - 3, 0)
                if live(0):
                    taps(t, s, 0)
                if live(3):
                    residual(t - 3, 1 - s, 0)
                if live(2):
                    skip(t - 2, s)
                if live(1):
                    dt_times_x(t - 1, 0)
                if live(3):
                    mean_square(t - 3, 1)
                if live(0):
                    taps(t, s, 1)
                if live(3):
                    residual(t - 3, 1 - s, 1)
                if live(1):
                    dt_times_x(t - 1, 1)
                if live(0):
                    silu(t, s, 0)
                if live(1):
                    mask(t - 1)
                if live(0):
                    gate(t, s, 0)
                    taps(t, s, 2)
                    silu(t, s, 1)
                    gate(t, s, 1)
                    silu(t, s, 2)

            steps(dve, turn)

        @block.gpsimd
        def _(pool):
            nc.gpsimd.memset(mhalf[:], -0.5).then_inc(s_mh, 1)
            pool.wait_ge(s_mh, 1)
            pool.wait_ge(s_ld, 32)

            def spread(n, s, j):
                m = 2 * n + j
                at_least(pool, s_s, m - 3)
                for d in range(2):
                    upto = cst(("upto_f", "upto_b")[d], PT).unsqueeze(1).broadcast_to([PT, NH, T])
                    av = aa[:, m, 4 * d:4 * d + 4] if isinstance(m, int) else aa[:, bass.ds(m, 1), 4 * d:4 * d + 4].rearrange("r o e -> r (o e)")
                    nc.gpsimd.tensor_tensor(a2[:, s, j, d], upto, av.unsqueeze(2).broadcast_to([PT, NH, T]), ALU.mult).then_inc(s_a2, 1)

            def weigh(n, j):
                m = 2 * n + j
                pool.wait_ge(s_e, m + 1)
                pool.wait_ge(s_gm, n + 1)
                at_least(pool, s_y, m - 1)
                for d in range(2):
                    o = tt[:, j, d].rearrange("r h (b i) -> r h b i", b=2)
                    x = ee[:, j, d].unsqueeze(2).broadcast_to([PT, NH, 2, T])
                    g = gm[:, j, d].rearrange("r (b i) -> r b i", b=2).unsqueeze(1).broadcast_to([PT, NH, 2, T])
                    nc.gpsimd.tensor_tensor(o, x, g, ALU.mult).then_inc(s_tt, 1)

            def root(n, j):
                m = 2 * n + j
                pool.wait_ge(s_va, m + 1)
                at_least(pool, s_h, 2 * m - 2)
                nc.gpsimd.tensor_tensor(rr[:, j, :], var[:, j, :], mhalf[:], ALU.pow).then_inc(s_rr, 1)

            def turn(t, s, live):
                if live(3):
                    root(t - 3, 0)
                if live(0):
                    spread(t, s, 0)
                if live(3):
                    root(t - 3, 1)
                if live(2):
                    n = t - 2
                    pool.wait_ge(s_yv, 4 * n + 4)
                    at_least(pool, s_o, 2 * n)
                    at_least(pool, s_sq, n)
                    nc.gpsimd.tensor_tensor(flat(yg[:]), flat(yv[:]), flat(gz[:, s]), ALU.mult).then_inc(s_yg, 1)
                if live(0):
                    spread(t, s, 1)
                if live(1):
                    weigh(t - 1, 0)
                    weigh(t - 1, 1)

            steps(pool, turn)


FT = 1024
FP = -(-FT // PT)
FE, FF = 8, 512
FG = 4


def stage_ffn(nc, pk, h1_dram, ew, ei, w1, w2, xs_dram):
    with ExitStack() as ctx:
        def sb(name, shape, dt=F32):
            return ctx.enter_context(nc.sbuf_tensor("ff_" + name, shape, dt))

        def ps(name):
            return ctx.enter_context(nc.psum_tensor("ff_" + name, [128, 512], F32))

        def sem(name):
            return ctx.enter_context(nc.semaphore("ff_" + name))

        ident = pk[:, COLS["ident"][0]:COLS["ident"][1]]
        NG = FP // FG
        GT = FG * PT
        KC = FF // 128
        NZ = 8
        zero = sb("zero", [128, xs_dram.shape[0] * D // 128 // NZ])
        hacc = sb("hacc", [PT, FP, D])
        st = sb("st", [PT, FP, 6])
        mv = sb("mv", [PT, FP, 2])
        ve = sb("ve", [PT, FP])
        rs = sb("rs", [PT, FP])
        mhalf = sb("mhalf", [PT, FP])
        uu = sb("uu", [PT, FP, D])
        ut = sb("ut", [D, FP * PT])
        wt = sb("wt", [PT, FP, 2])
        ix = sb("ix", [PT, FP, 2], I32)
        xf = sb("xf", [PT, FP, 2])
        part = sb("part", [PT, FE, FP, 2])
        comb = sb("comb", [PT, FE, FP])
        w1s = sb("w1s", [D, 2, FF])
        w2s = sb("w2s", [128, 2, KC, D])
        ht = sb("ht", [128, 2, KC, GT])
        psh = [ps(f"psh{c}") for c in range(KC)]
        pso = [ps("pso0"), ps("pso1")]
        psu = ps("psu")

        s_ld, s_z, s_v, s_r, s_u, s_tu, s_ut = (sem(n) for n in ("ld", "z", "v", "r", "u", "tu", "ut"))
        s_w = [sem("w0"), sem("w1")]
        s_cb = sem("cb")
        s_h = sem("h")
        s_g = sem("g")
        s_o = sem("o")
        s_a = sem("a")
        s_st = sem("st")
        block = ctx.enter_context(nc.Block())
        full = FT // PT
        rest = FT - full * PT
        h_rows = h1_dram[0:FP * PT, :].rearrange("(p r) d -> r p d", r=PT)
        UNITS = 2 * NG

        def units(eng, unit):
            def turn(i):
                for k in range(UNITS):
                    unit(eng, i, k)
            turns(eng, FE // 2, turn)

        @block.sync
        def _(sp):
            sp.dma_start(hacc[:], h_rows).then_inc(s_ld, 16)
            sp.wait_ge(s_z, 4)
            for dst, src in ((wt, ew), (ix, ei)):
                sp.dma_start(dst[:, 0:full, :], src[0:full * PT, :].rearrange("(p r) k -> r p k", r=PT)).then_inc(s_ld, 16)
                sp.dma_start(dst[0:rest, full, :], src[full * PT:FT, :]).then_inc(s_ld, 16)
            def load(i):
                for s in range(2):
                    e = 2 * i + s
                    at_least(sp, s_o, NG * 2 * i)
                    sp.dma_start(w1s[:, s, :], w1[bass.ds(e, 1)].rearrange("o d f -> (o d) f")).then_inc(s_w[s], 16)
                    sp.dma_start(w2s[:, s], w2[bass.ds(e, 1)].rearrange("o (c p) d -> (o p) c d", p=128)).then_inc(s_w[s], 16)
            turns(sp, FE // 2, load)
            spread = xs_dram.rearrange("(p q) d -> p (q d)", p=128).rearrange("p (a b) -> a p b", a=NZ)
            for k in range(NZ):
                sp.dma_start(spread[k], zero[:]).then_inc(s_st, 16)
            sp.wait_ge(s_a, FE * FP)
            sp.dma_start(h_rows, hacc[:]).then_inc(s_st, 16)
            sp.wait_ge(s_st, 16 * (NZ + 1))

        @block.gpsimd
        def _(pool):
            nc.gpsimd.memset(wt[:], 0.0).then_inc(s_z, 1)
            nc.gpsimd.memset(ix[:], 0).then_inc(s_z, 1)
            nc.gpsimd.memset(zero[:], 0.0).then_inc(s_z, 1)
            nc.gpsimd.memset(mhalf[:], -0.5).then_inc(s_z, 1)
            pool.wait_ge(s_v, 2)
            nc.gpsimd.tensor_tensor(rs[:], ve[:], mhalf[:], ALU.pow).then_inc(s_r, 1)

        @block.vector
        def _(dve):
            dve.wait_ge(s_ld, 16 * 5)
            for p in range(FP):
                last = nc.vector.bn_stats(st[:, p, :], hacc[:, p, :])
            last.then_inc(s_cb, 1)
            dve.wait_ge(s_cb, 1)
            for p in range(FP):
                last = nc.vector.bn_aggr(mv[:, p, :], st[:, p, :])
            last.then_inc(s_v, 1)
            dve.wait_ge(s_v, 1)
            nc.vector.tensor_scalar(ve[:], mv[:, :, 1], EPS, None, ALU.add).then_inc(s_v, 1)
            nc.vector.tensor_copy(xf[:], ix[:]).then_inc(s_cb, 1)
            dve.wait_ge(s_r, 1)
            for p in range(FP):
                nc.vector.tensor_scalar(uu[:, p, :], hacc[:, p, :], mv[:, p, 0:1], rs[:, p:p + 1], ALU.subtract, ALU.mult).then_inc(s_u, 1)
            dve.wait_ge(s_cb, 2)
            for e in range(FE):
                last = nc.vector.scalar_tensor_tensor(part[:, e], xf[:], float(e), wt[:], ALU.is_equal, ALU.mult)
            last.then_inc(s_cb, 1)
            dve.wait_ge(s_cb, 3)
            nc.vector.tensor_tensor(comb[:], part[:, :, :, 0], part[:, :, :, 1], ALU.add).then_inc(s_cb, 1)
            dve.wait_ge(s_cb, 4)
            dve.wait_ge(s_u, FP)

            def unit(dve, i, k):
                u, g = UNITS * i + k, k % NG
                dve.wait_ge(s_o, u + 1)
                at_least(dve, s_a, FG * u)
                for j in range(FG):
                    p = FG * g + j
                    cm = comb[:, bass.ds(2 * i + k // NG, 1), p]
                    nc.vector.scalar_tensor_tensor(hacc[:, p, :], pso[k % 2][0:PT, j * D:(j + 1) * D], cm, hacc[:, p, :],
                                                   ALU.mult, ALU.add).then_inc(s_a, 1)
            units(dve, unit)

        @block.scalar
        def _(act):
            for p in range(FP):
                act.wait_ge(s_tu, p + 1)
                nc.scalar.activation(ut[:, p * PT:(p + 1) * PT], psu[:, (p % 4) * 128:(p % 4) * 128 + PT], ACT.Copy).then_inc(s_ut, 1)

            def unit(act, i, k):
                u = UNITS * i + k
                for c in range(KC):
                    act.wait_ge(s_h, KC * u + c + 1)
                    if c == 0:
                        at_least(act, s_o, u - 1 if k else UNITS * i)
                    nc.scalar.activation(ht[:, k % 2, c, :], psh[c][:, 0:GT], ACT.Gelu).then_inc(s_g, 1)
            units(act, unit)

        @block.tensor
        def _(pe):
            for p in range(FP):
                pe.wait_ge(s_u, p + 1)
                if p >= 1:
                    pe.wait_ge(s_ut, p)
                nc.tensor.transpose(psu[:, (p % 4) * 128:(p % 4) * 128 + PT], uu[:, p, :], ident[0:PT, 0:PT]).then_inc(s_tu, 1)
            pe.wait_ge(s_ut, FP)

            def up(k, u, g):
                for c in range(KC):
                    at_least(pe, s_g, KC * (u - 1) + c + 1 if k else KC * u)
                    nc.tensor.matmul(psh[c][:, 0:GT], w1s[:, k // NG, c * 128:(c + 1) * 128], ut[:, g * GT:(g + 1) * GT],
                                     start=True, stop=True).then_inc(s_h, 1)

            def down(k, u):
                pe.wait_ge(s_g, KC * (u + 1))
                at_least(pe, s_a, FG * (u - 1) if k else FG * u)
                for j in range(FG):
                    for c in range(KC):
                        last = nc.tensor.matmul(pso[k % 2][0:PT, j * D:(j + 1) * D], ht[:, k % 2, c, j * PT:(j + 1) * PT],
                                                w2s[:, k // NG, c, :], start=(c == 0), stop=(c == KC - 1))
                last.then_inc(s_o, 1)

            def turn(i):
                for k in range(UNITS):
                    u = UNITS * i + k
                    if k % NG == 0:
                        pe.wait_ge(s_w[k // NG], 32 * (i + 1))
                    up(k, u, k % NG)
                    if k:
                        down(k - 1, u - 1)
                down(UNITS - 1, UNITS * i + UNITS - 1)
            turns(pe, FE // 2, turn)


E2, K2 = 32, 2
SLOTS = 128
NBL = -(-TOK * K2 // SLOTS) + E2 - 1
TINY = 1e-30


def stage_attention(nc, pk, h_in, h_out, x_all, oh, dm, ssum):
    with ExitStack() as ctx:
        def sb(name, shape, dt=F32):
            return ctx.enter_context(nc.sbuf_tensor("at_" + name, shape, dt))

        def ps(name):
            return ctx.enter_context(nc.psum_tensor("at_" + name, [128, 512], F32))

        def sem(name):
            return ctx.enter_context(nc.semaphore("at_" + name))

        def cst(name, parts=128):
            return pk[0:parts, COLS[name][0]:COLS[name][1]]

        hq = sb("hq", [PT, 4, 2, D])
        st = sb("st", [PT, 2, 2, 2, 6])
        mv = sb("mv", [PT, 2, 2, 2, 2])
        ve = sb("ve", [PT, 2, 2, 2])
        rs = sb("rs", [PT, 2, 2, 2])
        mhalf = sb("mhalf", [PT, 2])
        uu = sb("uu", [PT, 2, 2, D])
        ut = sb("ut", [D, 2, QT])
        tqk = sb("tqk", [128, 2, QT])
        tv = sb("tv", [PT, 2, D])
        qk = sb("qk", [128, 2, 2, QT])
        vv = sb("vv", [PT, 2, 2, D + 2])
        ee = sb("ee", [PT, 2, 2, PT])
        pp = sb("pp", [PT, 2, 2, PT])
        den = sb("den", [PT, 2, 2])
        rd = sb("rd", [PT, 2, 2])
        h3 = sb("h3", [PT, 2, 2, D])
        xc = sb("xc", [PT, 2, 2, D])
        xt = sb("xt", [D, 2, QT])
        lg = sb("lg", [PT, 2, 2, E2])
        m8 = sb("m8", [PT, 2, 2, 8])
        i8 = sb("i8", [PT, 2, 2, 8], U32)
        f8 = sb("f8", [PT, 2, 2, 8])
        ld = sb("ld", [PT, 2, 2, E2])
        le = sb("le", [PT, 2, 2, E2])
        psu, psqk, psv, pss, pso, psx, psl = (ps(n) for n in ("psu", "psqk", "psv", "pss", "pso", "psx", "psl"))

        s_k = sem("k")
        s_hq = [sem(f"hq{k}") for k in range(4)]
        s_va = sem("va")
        s_ra = sem("ra")
        s_u = sem("u")
        s_tu, s_ut = sem("tu"), sem("ut")
        s_pq, s_pv = sem("pq"), sem("pv")
        s_tq, s_tv = sem("tq"), sem("tv")
        s_q, s_vv = sem("q"), sem("vv")
        s_s, s_e, s_p, s_o = sem("s"), sem("e"), sem("p"), sem("o")
        s_d = sem("d")
        s_h = sem("h")
        s_vb = sem("vb")
        s_rb = sem("rb")
        s_x = sem("x")
        s_xa = sem("xa")
        s_tx, s_xt, s_l = sem("tx"), sem("xt"), sem("l")
        s_m = sem("m")
        s_le = sem("le")
        s_st = [sem("st0"), sem("st1")]
        s_pe1 = sem("pe1")
        s_wv = sem("wv")

        block = ctx.enter_context(nc.Block())

        FIRST = 8

        def steps(eng, turn):
            for t in range(FIRST):
                turn(t, t % 4, lambda k, t=t: 0 <= t - k < NQ)
            with eng.Fori(0, (NQ - FIRST) // 4) as i:
                for r in range(4):
                    turn(4 * i + FIRST + r, r, lambda k: True)
            for t in range(NQ, NQ + 5):
                turn(t, t % 4, lambda k, t=t: 0 <= t - k < NQ)

        def rounds(n, r, of):
            shift = {2: 1, 4: 2}[of]
            return (n - r) >> shift

        def rows(dram, n):
            v = dram.rearrange("(n j r) d -> n r j d", j=2, r=PT)
            return v[n] if isinstance(n, int) else v[bass.ds(n, 1)].rearrange("o r j d -> (o r) j d")

        def pair_rows(a, n):
            return a[:, 2 * n:2 * n + 2] if isinstance(n, int) else a[:, bass.ds(2 * n, 2)]

        flat = lambda a: a.rearrange("p k q -> p (k q)")
        pair_cols = lambda j: slice(j * PT, (j + 1) * PT)

        @block.sync
        def _(sp):
            def load(n, r):
                at_least(sp, s_h, 2 * n - 6)
                sp.dma_start(hq[:, r], rows(h_in, n)).then_inc(s_hq[r], 16)

            def turn(t, r, live):
                if live(-1):
                    load(t + 1, (r + 1) % 4)
                if live(3):
                    n, s = t - 3, (r - 3) % 2
                    sp.wait_ge(s_h, 2 * n + 2)
                    sp.dma_start(rows(h_out, n), h3[:, s]).then_inc(s_st[s], 16)

            load(0, 0)
            for t in range(FIRST):
                turn(t, t % 4, lambda k, t=t: 0 <= t - k < NQ)
            with sp.Fori(0, (NQ - FIRST) // 4 - 1) as i:
                for r in range(4):
                    turn(4 * i + FIRST + r, r, lambda k: True)
            for t in range(NQ - 4, NQ + 5):
                turn(t, t % 4, lambda k, t=t: 0 <= t - k < NQ)
            for s in range(2):
                sp.wait_ge(s_st[s], 16 * (NQ // 2))

        @block.tensor
        def _(pe):
            def transpose_u(n, s):
                pe.wait_ge(s_u, 2 * n + 2)
                at_least(pe, s_ut, n)
                for j in range(2):
                    last = nc.tensor.transpose(psu[:, pair_cols(j)], uu[:, s, j, :], cst("ident", PT)[:, 0:PT])
                last.then_inc(s_tu, 1)

            def project(n, s):
                pe.wait_ge(s_ut, n + 1)
                at_least(pe, s_tq, n)
                for k, w in enumerate(("wq", "wk")):
                    last = nc.tensor.matmul(psqk[:, k * QT:(k + 1) * QT], cst(w), ut[:, s, :], start=True, stop=True)
                last.then_inc(s_pq, 1)
                at_least(pe, s_tv, n)
                for j in range(2):
                    last = nc.tensor.matmul(psv[0:PT, j * D:(j + 1) * D], ut[:, s, pair_cols(j)], cst("wv"), start=True, stop=True)
                last.then_inc(s_pv, 1)

            def scores(n, s):
                pe.wait_ge(s_q, n + 1)
                at_least(pe, s_e, n)
                for j in range(2):
                    c = pair_cols(j)
                    last = nc.tensor.matmul(pss[0:PT, c], qk[:, s, 1, c], qk[:, s, 0, c], start=True, stop=True)
                last.then_inc(s_s, 1)

            def weighted_sum(n, s):
                pe.wait_ge(s_p, n + 1)
                pe.wait_ge(s_vv, n + 1)
                at_least(pe, s_h, 2 * n)
                for j in range(2):
                    last = nc.tensor.matmul(pso[0:PT, j * (D + 2):(j + 1) * (D + 2)], pp[:, s, j, :], vv[:, s, j, :], start=True, stop=True)
                last.then_inc(s_o, 1)

            def transpose_x(n, s):
                pe.wait_ge(s_x, 2 * n + 2)
                at_least(pe, s_xt, n)
                for j in range(2):
                    last = nc.tensor.transpose(psx[:, pair_cols(j)], xc[:, s, j, :], cst("ident", PT)[:, 0:PT])
                last.then_inc(s_tx, 1)

            def logits(n, s):
                pe.wait_ge(s_xt, n + 1)
                at_least(pe, s_m, 11 * n - 10)
                for j in range(2):
                    last = nc.tensor.matmul(psl[0:PT, j * E2:(j + 1) * E2], xt[:, s, pair_cols(j)], cst("wgate"), start=True, stop=True)
                last.then_inc(s_l, 1)

            def turn(t, r, live):
                s = r % 2
                if live(2):
                    scores(t - 2, s)
                if live(1):
                    transpose_u(t - 1, 1 - s)
                if live(4):
                    transpose_x(t - 4, s)
                if live(1):
                    project(t - 1, 1 - s)
                if live(4):
                    logits(t - 4, s)
                if live(2):
                    weighted_sum(t - 2, s)

            steps(pe, turn)

        @block.scalar
        def _(act):
            def turn(t, r, live):
                s = r % 2
                if live(1):
                    n = t - 1
                    act.wait_ge(s_tu, n + 1)
                    at_least(act, s_pv, n - 1)
                    nc.scalar.activation(ut[:, 1 - s, :], psu[:, 0:QT], ACT.Copy).then_inc(s_ut, 1)
                if live(2):
                    n = t - 2
                    act.wait_ge(s_s, n + 1)
                    at_least(act, s_p, n - 1)
                    nc.scalar.activation(flat(ee[:, s]), pss[0:PT, 0:2 * PT], ACT.Exp, scale=float(D) ** -0.5).then_inc(s_e, 1)
                if live(4):
                    n = t - 4
                    act.wait_ge(s_tx, n + 1)
                    at_least(act, s_l, n - 1)
                    nc.scalar.activation(xt[:, s, :], psx[:, 0:QT], ACT.Copy).then_inc(s_xt, 1)
                if live(1):
                    n = t - 1
                    act.wait_ge(s_pq, n + 1)
                    at_least(act, s_q, n)
                    nc.scalar.activation(flat(tqk[:]), psqk[:, 0:2 * QT], ACT.Tanh, scale=0.5).then_inc(s_tq, 1)
                    act.wait_ge(s_pv, n + 1)
                    at_least(act, s_vv, n)
                    nc.scalar.activation(flat(tv[:]), psv[0:PT, 0:2 * D], ACT.Tanh, scale=0.5).then_inc(s_tv, 1)
                if live(5):
                    n = t - 5
                    act.wait_ge(s_m, 11 * n + 6)
                    at_least(act, s_m, 11 * (n - 1))
                    nc.scalar.activation(le[:, 1 - s], ld[:, 1 - s], ACT.Exp).then_inc(s_le, 1)

            steps(act, turn)

        @block.vector
        def _(dve):
            for s in range(2):
                for j in range(2):
                    nc.vector.memset(vv[:, s, j, D:D + 2], 1.0).then_inc(s_k, 1)

            def stats(x, which, s, s_v):
                for j in range(2):
                    nc.vector.bn_stats(st[:, which, s, j, :], x[:, j, :]).then_inc(s_v, 1)

            def mean_var(which, n, s, s_v):
                for j in range(2):
                    wait_apart(dve, s_v, 5 * n + j + 1, s_wv)
                    nc.vector.bn_aggr(mv[:, which, s, j, :], st[:, which, s, j, :]).then_inc(s_v, 1)

            def add_eps(which, n, s, s_v):
                dve.wait_ge(s_v, 5 * n + 4)
                nc.vector.tensor_scalar(ve[:, which, s, :], mv[:, which, s, :, 1], EPS, None, ALU.add).then_inc(s_v, 1)

            def normed(x, which, s, out, s_out):
                for j in range(2):
                    nc.vector.tensor_scalar(out[:, j, :], x[:, j, :], mv[:, which, s, j, 0:1], rs[:, which, s, j:j + 1],
                                            ALU.subtract, ALU.mult).then_inc(s_out, 1)

            def turn(t, r, live):
                s = r % 2
                o = pso[0:PT, 0:2 * (D + 2)].rearrange("r (j c) -> r j c", j=2)
                n, q, e = t, t - 3, t - 5
                s1 = 1 - s
                if live(0):
                    dve.wait_ge(s_hq[r], 16 * (rounds(n, r, 4) + 1))
                    at_least(dve, s_u, 2 * n - 2)
                    stats(hq[:, r], 0, s, s_va)
                if live(3):
                    dve.wait_ge(s_o, q + 1)
                    at_least(dve, s_h, 2 * q - 2)
                    nc.vector.tensor_scalar(den[:, s1, :], o[:, :, D], TINY, None, ALU.max).then_inc(s_d, 1)
                if live(5):
                    dve.wait_ge(s_l, e + 1)
                    at_least(dve, s_le, e - 1)
                    bg = cst("bgate", PT).unsqueeze(1).broadcast_to([PT, 2, E2])
                    nc.vector.tensor_tensor(lg[:, s1], psl[0:PT, 0:2 * E2].rearrange("r (j e) -> r j e", j=2), bg, ALU.add).then_inc(s_m, 1)
                if live(0):
                    mean_var(0, n, s, s_va)
                if live(3):
                    dve.wait_ge(s_d, 2 * q + 1)
                    nc.vector.reciprocal(rd[:, s1, :], den[:, s1, :]).then_inc(s_d, 1)
                if live(5):
                    wait_apart(dve, s_m, 11 * e + 1, s_wv)
                    for j in range(2):
                        nc.vector.max(m8[:, s1, j, :], lg[:, s1, j, :]).then_inc(s_m, 1)
                if live(0):
                    add_eps(0, n, s, s_va)
                if live(3):
                    dve.wait_ge(s_d, 2 * q + 2)
                    at_least(dve, s_st[s1], 16 * rounds(q, s1, 2))
                    at_least(dve, s_x, 2 * q - 2)
                    for j in range(2):
                        nc.vector.scalar_tensor_tensor(h3[:, s1, j, :], o[:, j, 0:D], rd[:, s1, j:j + 1], hq[:, (r - 3) % 4, j, :], ALU.mult, ALU.add).then_inc(s_h, 1)
                if live(5):
                    wait_apart(dve, s_m, 11 * e + 3, s_wv)
                    for j in range(2):
                        nc.vector.max_index(i8[:, s1, j, :], m8[:, s1, j, :], lg[:, s1, j, :]).then_inc(s_m, 1)
                    nc.vector.tensor_tensor(ld[:, s1], lg[:, s1], m8[:, s1, :, 0:1].broadcast_to([PT, 2, E2]), ALU.subtract).then_inc(s_m, 1)
                if live(3):
                    wait_apart(dve, s_h, 2 * q + 2, s_wv)
                    stats(h3[:, s1], 1, s1, s_vb)
                if live(5):
                    dve.wait_ge(s_m, 11 * e + 5)
                    nc.vector.tensor_copy(f8[:, s1], i8[:, s1]).then_inc(s_m, 1)
                if live(0):
                    dve.wait_ge(s_ra, n + 1)
                    at_least(dve, s_tu, n - 1)
                    normed(hq[:, r], 0, s, uu[:, s], s_u)
                if live(3):
                    mean_var(1, q, s1, s_vb)
                if live(5):
                    dve.wait_ge(s_m, 11 * e + 7)
                    io = cst("iota32", PT).unsqueeze(1).broadcast_to([PT, 2, E2])
                    for k in range(2):
                        nc.vector.tensor_tensor(pair_rows(oh[k], e), io, f8[:, s1, :, k:k + 1].broadcast_to([PT, 2, E2]), ALU.is_equal).then_inc(s_m, 1)
                if live(3):
                    add_eps(1, q, s1, s_vb)
                if live(5):
                    nc.vector.tensor_tensor(pair_rows(dm, e), m8[:, s1, :, 1], m8[:, s1, :, 0], ALU.subtract).then_inc(s_m, 1)
                if live(1):
                    dve.wait_ge(s_tq, t)
                    at_least(dve, s_s, t - 2)
                    nc.vector.tensor_scalar(qk[:, s1], tqk[:], 0.5, 0.5, ALU.mult, ALU.add).then_inc(s_q, 1)
                    dve.wait_ge(s_tv, t)
                    at_least(dve, s_o, t - 2)
                    nc.vector.tensor_scalar(vv[:, s1, :, 0:D], tv[:], 0.5, 0.5, ALU.mult, ALU.add).then_inc(s_vv, 1)
                if live(3):
                    dve.wait_ge(s_rb, q + 1)
                    at_least(dve, s_tx, q - 1)
                    at_least(dve, s_xa, q - 1)
                    normed(h3[:, s1], 1, s1, xc[:, s1], s_x)
                if live(5):
                    dve.wait_ge(s_le, e + 1)
                    nc.vector.tensor_reduce(pair_rows(ssum, e), le[:, s1], AX_X, ALU.add).then_inc(s_m, 1)

            steps(dve, turn)

        @block.gpsimd
        def _(pool):
            nc.gpsimd.memset(mhalf[:], -0.5).then_inc(s_pe1, 1)
            pool.wait_ge(s_pe1, 1)
            pool.wait_ge(s_k, 4)

            def root(which, n, s, s_v, s_out, s_r):
                pool.wait_ge(s_v, 5 * n + 5)
                at_least(pool, s_out, 2 * n - 2)
                nc.gpsimd.tensor_tensor(rs[:, which, s, :], ve[:, which, s, :], mhalf[:], ALU.pow).then_inc(s_r, 1)

            def turn(t, r, live):
                s = r % 2
                if live(4):
                    pool.wait_ge(s_x, 2 * (t - 4) + 2)
                    nc.gpsimd.tensor_copy(pair_rows(x_all, t - 4), xc[:, s]).then_inc(s_xa, 1)
                if live(0):
                    root(0, t, s, s_va, s_u, s_ra)
                if live(2):
                    n = t - 2
                    pool.wait_ge(s_e, n + 1)
                    at_least(pool, s_o, n - 1)
                    nc.gpsimd.tensor_tensor(pp[:, s], ee[:, s], cst("amask", PT).unsqueeze(1).broadcast_to([PT, 2, PT]), ALU.mult).then_inc(s_p, 1)
                if live(3):
                    root(1, t - 3, 1 - s, s_vb, s_x, s_rb)

            steps(pool, turn)


F2 = 256
FC = F2 // 128
WB = 2 * F2 + D


def stage_plan(nc, pk, oh, pos, eb, brow, bias_in, bias_dram, s_bias):
    with ExitStack() as ctx:
        def sb(name, shape, dt=F32):
            return ctx.enter_context(nc.sbuf_tensor("pl_" + name, shape, dt))

        def sem(name):
            return ctx.enter_context(nc.semaphore("pl_" + name))

        def cst(name, parts=128):
            return pk[0:parts, COLS[name][0]:COLS[name][1]]

        NT = NP * E2
        cnt = sb("cnt", [PT, NP, E2])
        tot = sb("tot", [PT, NP, E2])
        ca = sb("ca", [PT, NP, E2])
        cb = sb("cb", [PT, NP, E2])
        prod = [cnt, tot]
        posf = [sb(f"posf{k}", [PT, NP]) for k in range(2)]
        sl = sb("sl", [PT, E2])
        n_e = sb("ne", [128, E2])
        n_i = sb("ni", [128, E2], I32)
        nb_i = sb("nbi", [128, E2], I32)
        en = [sb(f"en{k}", [128, E2]) for k in range(2)]
        nb = sb("nb", [128, E2])
        base = sb("base", [128, E2])
        le = sb("le", [128, E2])
        ebf = sb("ebf", [128, 1])
        bf = sb("bf", [E2, WB])
        bh = [sb(f"bh{k}", [E2, WB], BF16) for k in range(3)]
        br = [sb(f"br{k}", [E2, WB]) for k in range(2)]
        banks = [ctx.enter_context(nc.psum_tensor(f"pl_ps{k}", [128, 512], F32)) for k in range(8)]

        s_ld, s_c, s_tot, s_tri, s_ev, s_cn, s_row, s_b, s_end = (sem(n) for n in ("ld", "c", "tot", "tri", "ev", "cn", "row", "b", "end"))
        block = ctx.enter_context(nc.Block())
        flat = lambda a: a.rearrange("r p e -> r (p e)")
        C0 = 2

        @block.sync
        def _(sp):
            for lo, src in zip((0, F2, 2 * F2), bias_in):
                sp.dma_start(bf[:, lo:lo + src.shape[1]], src).then_inc(s_ld, 16)
            sp.wait_ge(s_b, 6)
            for k in range(3):
                sp.dma_start(bias_dram[:, k, :], bh[k][:]).then_inc(s_bias, 16)
            sp.wait_ge(s_bias, 48)

        @block.tensor
        def _(pe):
            pe.wait_ge(s_c, 1)
            for q in range(4):
                nc.tensor.matmul(banks[q][:], cst("onem", PT), flat(cnt[:])[:, q * 512:(q + 1) * 512], start=True, stop=True).then_inc(s_tot, 1)
            for q in range(4):
                last = nc.tensor.matmul(banks[4 + q][0:PT, :], cst("tri", PT), flat(cnt[:])[:, q * 512:(q + 1) * 512], start=True, stop=True)
            last.then_inc(s_tri, 1)
            pe.wait_ge(s_end, 1)
            nc.tensor.matmul(banks[0][0:1, 0:128], ebf[:], cst("ident"), start=True, stop=True).then_inc(s_row, 1)

        @block.scalar
        def _(act):
            for q in range(4):
                act.wait_ge(s_tot, q + 1)
                nc.scalar.activation(flat(tot[:])[:, q * 512:(q + 1) * 512], banks[q][0:PT, :], ACT.Copy).then_inc(s_ev, 1)

        @block.gpsimd
        def _(pool):
            pool.wait_ge(s_ld, 48)
            nc.gpsimd.tensor_copy(bh[0][:], bf[:]).then_inc(s_b, 1)
            pool.wait_ge(s_b, 1)
            nc.gpsimd.tensor_tensor(br[0][:], bf[:], bh[0][:], ALU.subtract).then_inc(s_b, 1)
            pool.wait_ge(s_b, 2)
            nc.gpsimd.tensor_copy(bh[1][:], br[0][:]).then_inc(s_b, 1)
            pool.wait_ge(s_b, 3)
            nc.gpsimd.tensor_tensor(br[1][:], br[0][:], bh[1][:], ALU.subtract).then_inc(s_b, 1)
            pool.wait_ge(s_b, 4)
            nc.gpsimd.tensor_copy(bh[2][:], br[1][:]).then_inc(s_b, 2)

        @block.vector
        def _(dve):
            c = [0]

            def then(ins):
                ins.then_inc(s_c, 1)
                c[0] += 1
                dve.wait_ge(s_c, c[0])

            then(nc.vector.tensor_tensor(cnt[:], oh[0], oh[1], ALU.add))
            dve.wait_ge(s_ev, 4)
            src, dst = tot, ca
            step = 1
            then(nc.vector.memset(ca[:, 0:1, :], 0.0))
            then(nc.vector.tensor_copy(ca[:, 1:, :], tot[:, :NP - 1, :]))
            src, dst = ca, cb
            while step < NP:
                then(nc.vector.tensor_copy(dst[:, :step, :], src[:, :step, :]))
                then(nc.vector.tensor_tensor(dst[:, step:, :], src[:, step:, :], src[:, :NP - step, :], ALU.add))
                src, dst = dst, src
                step *= 2
            dve.wait_ge(s_tot, 4)
            sums = [b_[:].rearrange("r (p e) -> r e p", e=E2) for b_ in banks[:4]]
            part = [ebf, None]
            for q in range(4):
                then(nc.vector.tensor_reduce(en[q % 2][:], sums[q], AX_X, ALU.add))
                then(nc.vector.tensor_copy(n_e[:], en[0][:]) if q == 0 else nc.vector.tensor_tensor(n_e[:], n_e[:], en[q % 2][:], ALU.add))
            then(nc.vector.tensor_scalar(n_e[:], n_e[:], float(SLOTS - 1), None, ALU.add))
            then(nc.vector.tensor_copy(n_i[:], n_e[:]))
            then(nc.vector.tensor_scalar(nb_i[:], n_i[:], SLOTS.bit_length() - 1, None, ALU.logical_shift_right))
            then(nc.vector.tensor_copy(nb[:], nb_i[:]))
            a, b = nb, en[0]
            other = en[1]
            step = 1
            while step < E2:
                then(nc.vector.tensor_copy(b[:, :step], a[:, :step]))
                then(nc.vector.tensor_tensor(b[:, step:], a[:, step:], a[:, :E2 - step], ALU.add))
                a, b = b, (other if b is en[0] else en[0])
                step *= 2
            then(nc.vector.tensor_tensor(base[:], a[:], nb[:], ALU.subtract))
            then(nc.vector.tensor_scalar(base[:], base[:], float(SLOTS), None, ALU.mult))
            then(nc.vector.tensor_scalar(le[:], a[:], brow, None, ALU.is_le))
            then(nc.vector.tensor_reduce(ebf[:], le[:], AX_X, ALU.add))
            nc.vector.tensor_scalar(ebf[:], ebf[:], float(E2 - 1), None, ALU.min).then_inc(s_end, 1)
            dve.wait_ge(s_tri, 1)
            for q in range(4):
                sl4 = slice(q * NP // 4, (q + 1) * NP // 4)
                then(nc.vector.tensor_tensor(dst[:, sl4, :], src[:, sl4, :], banks[4 + q][0:PT, :].rearrange("r (p e) -> r p e", e=E2), ALU.add))
            then(nc.vector.tensor_tensor(src[:], dst[:], base[0:PT, :].unsqueeze(1).broadcast_to([PT, NP, E2]), ALU.add))
            for k in range(2):
                then(nc.vector.tensor_tensor(prod[k][:], src[:], oh[k], ALU.mult))
            for k in range(2):
                then(nc.vector.tensor_reduce(posf[k][:], prod[k][:], AX_X, ALU.add))
            for k in range(2):
                then(nc.vector.tensor_copy(pos[k], posf[k][:]))
            dve.wait_ge(s_row, 1)
            then(nc.vector.tensor_copy(eb, banks[0][0:1, 0:128]))


def stage_experts(nc, pk, x_all, pos, eb, dm, ssum, wgu, wd, bias_dram, xs_dram, ys_dram, h3_dram, out_dram, s_w, n_w):
    with ExitStack() as ctx:
        def sb(name, shape, dt=F32):
            return ctx.enter_context(nc.sbuf_tensor("ex_" + name, shape, dt))

        def ps(name):
            return ctx.enter_context(nc.psum_tensor("ex_" + name, [128, 512], F32))

        def sem(name):
            return ctx.enter_context(nc.semaphore("ex_" + name))

        def cst(name, parts=128):
            return pk[0:parts, COLS[name][0]:COLS[name][1]]

        RING = 4
        xb = sb("xb", [SLOTS, RING, D])
        bb = sb("bb", [3, RING, WB], BF16)
        one3 = sb("one3", [3, SLOTS], BF16)
        xt = sb("xt", [D, 2, SLOTS])
        sg = sb("sg", [SLOTS, 2, F2])
        hh = sb("hh", [SLOTS, 2, F2])
        ht = sb("ht", [128, 2, FC, SLOTS])
        yb = sb("yb", [SLOTS, 2, D])
        pw = sb("pw", [PT, 2, NP])
        pw2 = sb("pw2", [PT, NP])
        y1 = sb("y1", [PT, 4, D])
        y2 = sb("y2", [PT, 4, D])
        hq = sb("hq", [PT, 4, D])
        ha = sb("ha", [PT, 4, D])
        ho = sb("ho", [PT, 4, D])
        psx = ps("psx")
        psg = [ps("psg0"), ps("psg1")]
        psh = [ps("psh0"), ps("psh1")]
        psy = [ps("psy0"), ps("psy1")]

        s_sc = sem("sc")
        s_k = sem("k")
        s_x = [sem(f"x{k}") for k in range(RING)]
        s_tx, s_xt, s_g, s_sg, s_hh, s_th, s_ht, s_y, s_yb = (sem(n) for n in ("tx", "xt", "g", "sg", "hh", "th", "ht", "y", "yb"))
        s_st = [sem("st0"), sem("st1")]
        s_pw = sem("pw")
        s_ga = [sem(f"ga{k}") for k in range(4)]
        s_hq = [sem(f"hq{k}") for k in range(4)]
        s_bi = [sem(f"bi{k}") for k in range(RING)]
        s_a = sem("a")
        s_out = [sem(f"out{k}") for k in range(4)]

        block = ctx.enter_context(nc.Block())
        PEEL = 5
        TURNS = (NBL - 3 - PEEL) // RING
        REST = PEEL + RING * TURNS

        def steps(eng, step):
            for n in range(PEEL):
                step(eng, n, n % RING, n)
            with eng.Fori(0, TURNS) as i:
                for k in range(RING):
                    step(eng, RING * i + PEEL + k, (PEEL + k) % RING, None)
            for n in range(REST, NBL + 3):
                step(eng, n, n % RING, n)

        def live(known, back):
            return known is None or 0 <= known - back < NBL

        def rows(dram, n):
            v = dram.rearrange("(n s) d -> n s d", s=SLOTS)
            return v[n] if isinstance(n, int) else v[bass.ds(n, 1)].rearrange("o s d -> (o s) d")

        def expert(eng, n):
            return eng.value_load(eb[0:1, n:n + 1] if isinstance(n, int) else eb[0:1, bass.ds(n, 1)], min_val=0, max_val=E2 - 1)

        pairs = h3_dram.rearrange("(p r) d -> p r d", r=PT)
        outs = out_dram.rearrange("(p r) d -> p r d", r=PT)

        @block.gpsimd
        def _(pool):
            nc.gpsimd.memset(one3[:], 1.0).then_inc(s_k, 1)
            for p in range(NP):
                for k in range(K2):
                    pool.indirect_dma_start(xs_dram, bass.IndirectOffsetOnAxis(ap=pos[k][:, p:p + 1], axis=0),
                                            x_all[:, p, :], None).then_inc(s_sc, 16)
            for s in range(2):
                pool.wait_ge(s_st[s], 16 * ((NBL + 1 - s) // 2))
            for p in range(NP):
                s = p % 4
                if p >= 4:
                    pool.wait_ge(s_a, 2 * (p - 3))
                for k, y in enumerate((y1, y2)):
                    pool.indirect_dma_start(y[:, s, :], None, ys_dram, bass.IndirectOffsetOnAxis(ap=pos[k][:, p:p + 1], axis=0)).then_inc(s_ga[s], 16)

        @block.sync
        def _(sp):
            def load_x(m, s):
                sp.dma_start(xb[:, s, :], rows(xs_dram, m)).then_inc(s_x[s], 16)

            def load_bias(m, s):
                e = expert(sp, m)
                sp.dma_start(bb[:, s, :], bias_dram[bass.ds(e, 1)].rearrange("o k w -> (o k) w")).then_inc(s_bi[s], 16)

            sp.wait_ge(s_sc, 16 * K2 * NP)
            for m in range(3):
                load_x(m, m)
            load_bias(0, 0)

            def step(sp, n, s, known):
                if known is None or known + 3 < NBL:
                    at_least(sp, s_tx, n)
                    load_x(n + 3, (s + 3) % RING)
                if known is None or known + 1 < NBL:
                    at_least(sp, s_y, n - 2)
                    load_bias(n + 1, (s + 1) % RING)
                if known is None or 0 <= known - 4:
                    b = n - 4
                    sp.wait_ge(s_yb, b + 1)
                    sp.dma_start(rows(ys_dram, b), yb[:, s % 2, :]).then_inc(s_st[s % 2], 16)

            steps(sp, step)
            b = NBL - 1
            sp.wait_ge(s_yb, b + 1)
            sp.dma_start(rows(ys_dram, b), yb[:, b % 2, :]).then_inc(s_st[b % 2], 16)
            def turn(i):
                for s in range(4):
                    p = 4 * i + s
                    at_least(sp, s_a, 8 * i)
                    sp.dma_start(hq[:, s, :], pairs[bass.ds(p, 1)].rearrange("o r d -> (o r) d")).then_inc(s_hq[s], 16)
                for s in range(4):
                    p = 4 * i + s
                    sp.wait_ge(s_a, 2 * p + 2)
                    sp.dma_start(outs[bass.ds(p, 1)].rearrange("o r d -> (o r) d"), ho[:, s, :]).then_inc(s_out[s], 16)
            turns(sp, NP // 4, turn)
            for s in range(4):
                sp.wait_ge(s_out[s], 16 * (NP // 4))

        @block.tensor
        def _(pe):
            pe.wait_ge(s_w, n_w)
            pe.wait_ge(s_k, 1)

            def step(pe, n, s, known):
                if live(known, 0):
                    pe.wait_ge(s_x[s], 16 * (n // RING + 1) if known is not None else 16 * ((n >> 2) + 1))
                    at_least(pe, s_xt, n)
                    nc.tensor.transpose(psx[:, 0:SLOTS], xb[:, s, :], cst("ident")).then_inc(s_tx, 1)
                if live(known, 1):
                    b, r = n - 1, (s - 1) % RING
                    e = expert(pe, b)
                    pe.wait_ge(s_xt, b + 1)
                    pe.wait_ge(s_bi[r], 16 * (b // RING + 1) if known is not None else 16 * ((b >> 2) + 1))
                    at_least(pe, s_hh, b - 1)
                    nc.tensor.matmul(psg[r % 2][:], xt[:, r % 2, :], wgu[:, bass.ds(e, 1), :].rearrange("p o f -> p (o f)"), start=True, stop=False)
                    nc.tensor.matmul(psg[r % 2][:], one3[:], bb[:, r, 0:2 * F2], start=False, stop=True).then_inc(s_g, 1)
                if live(known, 2):
                    b, r = n - 2, (s - 2) % RING
                    pe.wait_ge(s_hh, b + 1)
                    at_least(pe, s_ht, b - 1)
                    for c in range(FC):
                        last = nc.tensor.transpose(psh[r % 2][:, c * SLOTS:(c + 1) * SLOTS], hh[:, r % 2, c * 128:(c + 1) * 128], cst("ident"))
                    last.then_inc(s_th, 1)
                if live(known, 3):
                    b, r = n - 3, (s - 3) % RING
                    e = expert(pe, b)
                    pe.wait_ge(s_ht, b + 1)
                    at_least(pe, s_yb, b - 1)
                    for c in range(FC):
                        nc.tensor.matmul(psy[r % 2][:, 0:D], ht[:, r % 2, c, :], wd[:, bass.ds(e, 1), c, :].rearrange("p o d -> p (o d)"), start=(c == 0), stop=False)
                    nc.tensor.matmul(psy[r % 2][:, 0:D], one3[:], bb[:, r, 2 * F2:], start=False, stop=True).then_inc(s_y, 1)

            steps(pe, step)

        @block.scalar
        def _(act):
            nc.scalar.activation(pw[:, 1, :], dm, ACT.Exp).then_inc(s_pw, 1)

            def step(act, n, s, known):
                if live(known, 0):
                    act.wait_ge(s_tx, n + 1)
                    at_least(act, s_g, n - 1)
                    nc.scalar.activation(xt[:, s % 2, :], psx[:, 0:SLOTS], ACT.Copy).then_inc(s_xt, 1)
                if live(known, 1):
                    b, r = n - 1, (s - 1) % 2
                    act.wait_ge(s_g, b + 1)
                    at_least(act, s_hh, b - 1)
                    nc.scalar.activation(sg[:, r, :], psg[r][:, 0:F2], ACT.Silu).then_inc(s_sg, 1)
                if live(known, 2):
                    b, r = n - 2, s % 2
                    act.wait_ge(s_th, b + 1)
                    at_least(act, s_y, b - 1)
                    nc.scalar.activation(ht[:, r].rearrange("p c s -> p (c s)"), psh[r][:, 0:FC * SLOTS], ACT.Copy).then_inc(s_ht, 1)

            steps(act, step)

        @block.vector
        def _(dve):
            nc.vector.reciprocal(pw[:, 0, :], ssum).then_inc(s_pw, 1)
            dve.wait_ge(s_pw, 2)
            nc.vector.tensor_tensor(pw2[:], pw[:, 1, :], pw[:, 0, :], ALU.mult).then_inc(s_pw, 1)

            def step(dve, n, s, known):
                if live(known, 1):
                    b, r = n - 1, (s - 1) % 2
                    dve.wait_ge(s_sg, b + 1)
                    at_least(dve, s_th, b - 1)
                    nc.vector.tensor_tensor(hh[:, r, :], sg[:, r, :], psg[r][:, F2:2 * F2], ALU.mult).then_inc(s_hh, 1)
                if live(known, 3):
                    b, r = n - 3, (s - 3) % 2
                    dve.wait_ge(s_y, b + 1)
                    at_least(dve, s_st[r], 16 * (b // 2) if known is not None else 16 * ((b - r) >> 1))
                    nc.vector.tensor_copy(yb[:, r, :], psy[r][:, 0:D]).then_inc(s_yb, 1)

            steps(dve, step)
            dve.wait_ge(s_pw, 3)
            def turn(i):
                for s in range(4):
                    p = 4 * i + s
                    dve.wait_ge(s_ga[s], 32 * (i + 1))
                    dve.wait_ge(s_hq[s], 16 * (i + 1))
                    nc.vector.scalar_tensor_tensor(ha[:, s, :], y1[:, s, :], pw[:, 0, bass.ds(p, 1)], hq[:, s, :], ALU.mult, ALU.add).then_inc(s_a, 1)
                    dve.wait_ge(s_a, 2 * p + 1)
                    at_least(dve, s_out[s], 16 * i)
                    nc.vector.scalar_tensor_tensor(ho[:, s, :], y2[:, s, :], pw2[:, bass.ds(p, 1)], ha[:, s, :], ALU.mult, ALU.add).then_inc(s_a, 1)
            turns(dve, NP // 4, turn)


def bass_audio_tower_kernel(nc, x, small, e_w, e_i, w1, w2, wg, wu, wd_, bg, bu, bd, out):
    def dram(name, shape, dt=F32):
        return nc.dram_tensor(name, shape, dt, kind="Internal").ap()

    h0, h1, h3 = (dram(n, [TOK, D]) for n in ("h0", "h1", "h3"))
    dt_dram, a_dram = (dram(n, [B, T * 8]) for n in ("steps_dt", "steps_a"))
    xs_dram, ys_dram = (dram(n, [NBL * SLOTS, D]) for n in ("slots_x", "slots_y"))
    bias_dram = dram("bias_parts", [E2, 3, WB], BF16)

    with ExitStack() as ctx:
        def sb(name, shape, dt=F32):
            return ctx.enter_context(nc.sbuf_tensor(name, shape, dt))

        s_pack, s_bias, s_w = (ctx.enter_context(nc.semaphore(n)) for n in ("s_pack", "s_bias", "s_w"))
        pk = sb("pk", [128, NPACK])
        wgu = sb("wgu", [D, E2, 2 * F2])
        wd = sb("wd", [128, E2, FC, D])
        pos = [sb(f"pos{k}", [PT, NP], I32) for k in range(K2)]
        eb = sb("eb", [1, 128], I32)
        dm = sb("dm", [PT, NP])
        ssum = sb("ssum", [PT, NP])
        loads = [
            (lambda e: wgu[:, e, 0:F2], lambda e: wg[e].rearrange("o d f -> d o f"), s_w),
            (lambda e: wgu[:, e, F2:2 * F2], lambda e: wu[e].rearrange("o d f -> d o f"), s_w),
            (lambda e: wd[:, e].rearrange("p o c d -> p (o c) d"), lambda e: wd_[e].rearrange("o (c p) d -> p (o c) d", p=128), s_w),
        ]
        with nc.sbuf_tensor("u_t", [D, TOK], F32) as u_t:
            stage_patches(nc, x, u_t[:], dt_dram, a_dram, h0, pk, s_pack, small)
            stage_mamba(nc, u_t[:], pk, dt_dram, a_dram, h0, h1, loads)
        stage_ffn(nc, pk, h1, e_w, e_i, w1, w2, xs_dram)
        with nc.sbuf_tensor("x_all", [PT, NP, D], F32) as x_all:
            with nc.sbuf_tensor("oh0", [PT, NP, E2], F32) as oh0, nc.sbuf_tensor("oh1", [PT, NP, E2], F32) as oh1:
                stage_attention(nc, pk, h1, h3, x_all[:], [oh0[:], oh1[:]], dm[:], ssum[:])
                stage_plan(nc, pk, [oh0[:], oh1[:]], [p[:] for p in pos], eb[:], pk[:, COLS["bcol"][0]:COLS["bcol"][1]],
                           (bg, bu, bd), bias_dram, s_bias)
            stage_experts(nc, pk, x_all[:], [p[:] for p in pos], eb[:], dm[:], ssum[:], wgu[:], wd[:], bias_dram, xs_dram, ys_dram,
                          h3, out.rearrange("b t d -> (b t) d"), s_w, 16 * len(loads) * NQ)



def pack(i):
    f = np.float32
    r = np.arange(PT); b, t = r // T, r % T
    same = b[:, None] == b[None]
    tt = np.arange(T)
    p = {}
    p["ident"] = np.eye(128)
    p["later_f"] = same & (t[:, None] > t[None]); p["later_b"] = same & (t[:, None] < t[None])
    p["upto_f"] = t[:, None] <= tt[None]; p["upto_b"] = t[:, None] >= tt[None]
    p["gmask_f"] = 0.25 * (same & (t[:, None] <= t[None])); p["gmask_b"] = 0.25 * (same & (t[:, None] >= t[None]))
    p["amask"] = same & (t[:, None] < t[None])
    p["tri"] = r[:, None] < r[None]
    p["iota32"] = np.broadcast_to(np.arange(32), (128, 32))
    p["bcol"] = np.arange(128)[:, None]
    p["ones"] = np.ones((128, 2)); p["onem"] = np.ones((128, 128))
    p["tokw"] = i["L0_tok_W"].reshape(64, 2, 8, 128).transpose(1, 2, 0, 3).reshape(8, 128, 128).transpose(1, 0, 2).reshape(128, 1024)
    p["tokb"] = i["L0_tok_b"][:, None]
    row = lambda a: np.broadcast_to(a[None], (128, a.size))
    p["gamma"] = row(i["L0_tok_gamma"]); p["beta"] = row(i["L0_tok_beta"])
    m = lambda d, n: np.asarray(i[f"L0_attn_{d}_{n}"])
    wi = {d: m(d, "in_proj_w") for d in ("fwd", "bwd")}
    both = lambda n: np.concatenate([m("fwd", n), m("bwd", n)])
    p["wdt"] = np.concatenate([wi["fwd"][544:], wi["bwd"][544:]]).T
    p["dtb"] = row(both("dt_bias")); p["alog"] = row(both("A_log"))
    p["wz"] = np.concatenate([wi["fwd"][:256], wi["bwd"][:256]]).T
    def tiles(a):
        n = a["fwd"].shape[1]
        bc = np.zeros((128, n), f)
        bc[0:16], bc[32:48], bc[64:80], bc[96:112] = a["fwd"][256:272], a["fwd"][272:], a["bwd"][256:272], a["bwd"][272:]
        return [a["fwd"][:128], a["fwd"][128:256], a["bwd"][:128], a["bwd"][128:256], bc]
    p["wx"] = np.concatenate([w.T for w in tiles({d: wi[d][256:544] for d in wi})], 1)
    p["cw"] = np.stack(tiles({d: m(d, "conv_w")[:, 0] for d in wi}), 1).reshape(128, 20)
    p["cb"] = np.stack(tiles({d: m(d, "conv_b")[:, None] for d in wi}), 1).reshape(128, 5)
    p["dcol"] = np.repeat(both("Dp"), 64).reshape(4, 128).T
    p["wo"] = np.concatenate([m("fwd", "out_proj_w"), m("bwd", "out_proj_w")], 1).T.reshape(4, 128, 128).transpose(1, 0, 2).reshape(128, 512)
    p["nw"] = both("norm_w").reshape(4, 128).T
    p["wq"], p["wk"], p["wv"] = i["L1_attn_Wq"], i["L1_attn_Wv"], i["L1_attn_Wk"]
    p["wgate"] = i["L1_ffn_Wgate"]; p["bgate"] = row(i["L1_ffn_bgate"])
    out = np.zeros((128, NPACK), f)
    for n, a in p.items():
        c = COLS[n]; a = np.asarray(a); out[:a.shape[0], c[0]:c[1]] = a
    return out


_L = "L1_ffn_"
_AS_THEY_ARE = ["L0_ffn_expert_weights", "L0_ffn_expert_indices", "L0_ffn_w1", "L0_ffn_w2",
                _L + "Wg", _L + "Wu", _L + "Wd", _L + "bg", _L + "bu", _L + "bd"]


def kernel(**inputs):
    import concourse.bacc as bacc
    from concourse.bass_utils import run_bass_kernel_spmd as run

    nc = bacc.Bacc("TRN2", target_bir_lowering=False, num_devices=1)
    arrays, args = {}, []
    given = {n: np.ascontiguousarray(a) for n, a in inputs.items()}
    for name, a in [("x", given["x"]), ("small", pack(given))] + [(n, given[n]) for n in _AS_THEY_ARE]:
        arrays[f"in_{name}"] = a
        args.append(nc.dram_tensor(f"in_{name}", a.shape, mybir.dt.from_np(a.dtype), kind="ExternalInput").ap())
    out = nc.dram_tensor("out", (B, T, D), F32, kind="ExternalOutput").ap()
    bass_audio_tower_kernel(nc, *args, out)
    return run(nc, [arrays], core_ids=[0]).results[0]["out"]
```

```python
import concourse.bass as bass
from concourse import mybir
from contextlib import ExitStack
import numpy as np

F32 = mybir.dt.float32
BF16 = mybir.dt.bfloat16
I32 = mybir.dt.int32
U32 = mybir.dt.uint32
ALU = mybir.AluOpType
ACT = mybir.ActivationFunctionType
AX_X = mybir.AxisListType.X

B, SEQ, CH = 128, 375, 64
BLK = 8
T = 45
NBLK = T + 1
FB = BLK * CH
D = 128
TOK = B * T
PT = 2 * T
NP = B // 2
QT = 2 * PT
NQ = B // 4
NH, HD, NS = 4, 64, 16
DI = NH * HD
EPS = 1e-5
LONGEST_DECAY = -200.0

PACK = dict(
    ident=128, later_f=PT, later_b=PT, upto_f=T, upto_b=T, gmask_f=PT, gmask_b=PT, amask=PT, tri=PT,
    iota32=32, tokw=8 * 128, tokb=1, gamma=128, beta=128, wdt=8, dtb=8, alog=8,
    wz=512, wx=5 * 128, cw=20, cb=5, dcol=4, wo=4 * 128, nw=4, wq=128, wk=128, wv=128,
    wgate=32, bgate=32, ones=2, onem=128, bcol=1, tokid=4 * NQ, block0=128,
)


def columns():
    at, out = 0, {}
    for name, n in PACK.items():
        out[name] = (at, at + n)
        at += n
    return out, at


COLS, NPACK = columns()


def at_least(eng, sem, value):
    if not isinstance(value, int) or value > 0:
        eng.wait_ge(sem, value)


def turns(eng, count, body):
    body(0)
    with eng.Fori(1, count) as i:
        body(i)


def wait_apart(eng, sem, value, passed):
    eng.wait_ge(sem, value)
    eng.sem_inc(passed, 1)


def stage_patches(nc, x, u_t, dt_dram, a_dram, h_dram, sb_pack, s_pack, load_pack):
    with ExitStack() as ctx:
        def sb(name, shape, dt=F32):
            return ctx.enter_context(nc.sbuf_tensor("pa_" + name, shape, dt))

        def sem(name):
            return ctx.enter_context(nc.semaphore("pa_" + name))

        def cst(name):
            return sb_pack[:, COLS[name][0]:COLS[name][1]]

        xin = sb("xin", [B, 4, FB])
        xt = sb("xt", [128, 4, 4, B])
        yt = sb("yt", [D, 2, B])
        st6 = sb("st6", [B, 2, 2, 6])
        mv = sb("mv", [B, 2, 2, 2])
        ve = sb("ve", [B, 2, 2])
        rs = sb("rs", [B, 2, 2])
        mhalf = sb("mhalf", [B, 2])
        yn = sb("yn", [B, 2, D])
        yg = sb("yg", [B, 2, D])
        hh = sb("hh", [B, 2, D])
        uu = sb("uu", [B, 2, D])
        uc = sb("uc", [D, 2, B])
        xdt = sb("xdt", [B, T, 8])
        n8 = T * 8
        e, w, sl, t1 = (sb(n, [B, n8]) for n in ("e", "w", "sl", "t1"))
        al = sb("al", [B, 8])
        dtv, av = (sb(n, [B, T, 8]) for n in ("dtv", "av"))
        xf = xdt[:].rearrange("b t e -> b (t e)")
        psx = [ctx.enter_context(nc.psum_tensor(f"pa_psx{k}", [128, 4, B], F32)) for k in range(2)]
        psy = [ctx.enter_context(nc.psum_tensor(f"pa_psy{k}", [D, 512], F32)) for k in range(2)]
        pst = [ctx.enter_context(nc.psum_tensor(f"pa_pst{k}", [B, 512], F32)) for k in range(2)]
        psu = ctx.enter_context(nc.psum_tensor("pa_psu", [D, 512], F32))
        psd = ctx.enter_context(nc.psum_tensor("pa_psd", [B, 512], F32))

        s_in = [sem(f"in{k}") for k in range(4)]
        s_xtp = sem("xtp")
        s_xt = sem("xt")
        s_y = sem("y")
        s_yt = sem("yt")
        s_ty = sem("ty")
        s_n = [sem("n1"), sem("n2")]
        s_ve = sem("ve")
        s_r = sem("r")
        s_yn, s_yg, s_hh, s_uu = (sem(n) for n in ("yn", "yg", "hh", "uu"))
        s_tu = sem("tu")
        s_uc = sem("uc")
        s_ut = sem("ut")
        s_dt = sem("dt")
        s_dtv = sem("dtv")
        s_wv = sem("wv")
        s_mh = sem("mh")
        s_h = [sem(f"h{k}") for k in range(2)]
        s_c = sem("c")
        s_sc = sem("sc")
        s_out = sem("out")

        block = ctx.enter_context(nc.Block())

        FIRST = 8
        TURNS = (NBLK - 4 - FIRST) // 4
        LAST = T + 7

        def steps(eng, step):
            def one(p):
                step(p, p % 4, lambda k: 0 <= p - k < T, lambda k: p + k < NBLK)

            for p in range(FIRST):
                one(p)
            with eng.Fori(0, TURNS) as i:
                for r in range(4):
                    step(4 * i + FIRST + r, r, lambda k: True, lambda k: True)
            for p in range(FIRST + 4 * TURNS, LAST):
                one(p)

        hv = h_dram.rearrange("(b t) d -> b t d", t=T)

        @block.sync
        def _(sp):
            def load_block(b, r):
                src = x[:, b * BLK:(b + 1) * BLK, :] if isinstance(b, int) else x[:, bass.ds(b * BLK, BLK), :]
                sp.dma_start(xin[:, r, :], src.rearrange("b l c -> b (l c)")).then_inc(s_in[r], 16)

            def step(p, r, live, more):
                s = r % 2
                if more(4):
                    at_least(sp, s_xtp, p + 1)
                    load_block(p + 4, r)
                if live(2):
                    q = p - 2
                    sp.wait_ge(s_hh, q + 1)
                    dst = hv[:, q, :] if isinstance(q, int) else hv[:, bass.ds(q, 1), :].rearrange("b o d -> b (o d)")
                    sp.dma_start(dst, hh[:, s, :]).then_inc(s_h[s], 16)

            load_block(0, 0)
            sp.dma_start(sb_pack[:], load_pack).then_inc(s_pack, 16)
            for b in range(1, 4):
                load_block(b, b)
            steps(sp, step)
            sp.wait_ge(s_c, 1 + 1 + 2 + 6 + 3 + 1)
            sp.dma_start(dt_dram, dtv[:].rearrange("b t e -> b (t e)")).then_inc(s_out, 16)
            sp.wait_ge(s_c, 1 + 1 + 2 + 6 + 3 + 1 + 2)
            sp.dma_start(a_dram, av[:].rearrange("b t e -> b (t e)")).then_inc(s_out, 16)
            sp.wait_ge(s_out, 32)
            sp.wait_ge(s_h[0], 16 * ((T + 1) // 2))
            sp.wait_ge(s_h[1], 16 * (T // 2))

        @block.tensor
        def _(pe):
            def transpose_block(b, r):
                pe.wait_ge(s_in[r], 16 * (((b - r) >> 2) + 1))
                at_least(pe, s_xt, b - 1)
                for c in range(4):
                    last = nc.tensor.transpose(psx[r % 2][:, c, :], xin[:, r, c * 128:(c + 1) * 128], cst("ident"))
                last.then_inc(s_xtp, 1)

            def step(p, r, live, more):
                s = r % 2
                if live(0):
                    pe.wait_ge(s_xt, p + 2)
                    at_least(pe, s_yt, p - 1)
                    w = cst("tokw").rearrange("p (k d) -> p k d", k=8)
                    for k in range(8):
                        last = nc.tensor.matmul(psy[s][:, 0:B], w[:, k, :], xt[:, (r + k // 4) % 4, k % 4, :], start=(k == 0), stop=(k == 7))
                    last.then_inc(s_y, 1)
                if more(2):
                    transpose_block(p + 2, (r + 2) % 4)
                if live(1):
                    q = p - 1
                    pe.wait_ge(s_yt, q + 1)
                    at_least(pe, s_yn, q - 1)
                    nc.tensor.transpose(pst[1 - s][:, 0:D], yt[:, 1 - s, :], cst("ident")).then_inc(s_ty, 1)
                if live(5):
                    q = p - 5
                    pe.wait_ge(s_uu, q + 1)
                    at_least(pe, s_uc, q)
                    nc.tensor.transpose(psu[:, 0:B], uu[:, 1 - s, :], cst("ident")).then_inc(s_tu, 1)
                if live(6):
                    q = p - 6
                    pe.wait_ge(s_uc, q + 1)
                    at_least(pe, s_dtv, q)
                    nc.tensor.matmul(psd[:, 0:8], uc[:, s, :], cst("wdt"), start=True, stop=True).then_inc(s_dt, 1)

            pe.wait_ge(s_pack, 16)
            transpose_block(0, 0)
            transpose_block(1, 1)
            steps(pe, step)

        @block.scalar
        def _(act):
            def evacuate(b, r):
                act.wait_ge(s_xtp, b + 1)
                at_least(act, s_y, b - 3)
                nc.scalar.activation(xt[:, r, :, :], psx[r % 2][:], ACT.Copy).then_inc(s_xt, 1)

            def step(p, r, live, more):
                s = r % 2
                if live(0):
                    act.wait_ge(s_y, p + 1)
                    at_least(act, s_ty, p - 1)
                    nc.scalar.activation(yt[:, s, :], psy[s][:, 0:B], ACT.Identity, bias=cst("tokb")).then_inc(s_yt, 1)
                if more(2):
                    evacuate(p + 2, (r + 2) % 4)
                if live(5):
                    q = p - 5
                    act.wait_ge(s_tu, q + 1)
                    at_least(act, s_dt, q - 1)
                    at_least(act, s_ut, q - 1)
                    nc.scalar.activation(uc[:, 1 - s, :], psu[:, 0:B], ACT.Copy).then_inc(s_uc, 1)

            act.wait_ge(s_pack, 16)
            evacuate(0, 0)
            evacuate(1, 1)
            steps(act, step)
            act.wait_ge(s_c, 2)
            nc.scalar.activation(e[:], t1[:], ACT.Exp, scale=-1.0).then_inc(s_sc, 1)
            nc.scalar.activation(al[:], al[:], ACT.Exp).then_inc(s_sc, 1)
            act.wait_ge(s_c, 3)
            nc.scalar.activation(w[:], w[:], ACT.Ln).then_inc(s_sc, 1)

        @block.vector
        def _(dve):
            def step(p, r, live, more):
                s = r % 2
                if live(7):
                    q = p - 7
                    dve.wait_ge(s_dt, q + 1)
                    out = xdt[:, q, :] if isinstance(q, int) else xdt[:, bass.ds(q, 1), :].rearrange("b o e -> b (o e)")
                    nc.vector.tensor_tensor(out, psd[:, 0:8], cst("dtb"), ALU.add).then_inc(s_dtv, 1)
                if live(3):
                    dve.wait_ge(s_hh, p - 2)
                    nc.vector.bn_stats(st6[:, 1 - s, 1, :], hh[:, 1 - s, :]).then_inc(s_n[1], 1)
                if live(1):
                    wait_apart(dve, s_ty, p, s_wv)
                    nc.vector.bn_stats(st6[:, 1 - s, 0, :], pst[1 - s][:, 0:D]).then_inc(s_n[0], 1)
                if live(2):
                    dve.wait_ge(s_r, p - 1)
                    nc.vector.tensor_scalar(yn[:, s, :], pst[s][:, 0:D], mv[:, s, 0, 0:1], rs[:, s, 0:1], ALU.subtract, ALU.mult).then_inc(s_yn, 1)
                if live(4):
                    if not live(2):
                        dve.wait_ge(s_r, p - 1)
                    at_least(dve, s_tu, p - 5)
                    nc.vector.tensor_scalar(uu[:, s, :], hh[:, s, :], mv[:, s, 1, 0:1], rs[:, s, 1:2], ALU.subtract, ALU.mult).then_inc(s_uu, 1)
                if live(3):
                    wait_apart(dve, s_n[1], 2 * (p - 3) + 1, s_wv)
                    nc.vector.bn_aggr(mv[:, 1 - s, 1, :], st6[:, 1 - s, 1, :]).then_inc(s_n[1], 1)
                if live(2):
                    dve.wait_ge(s_yn, p - 1)
                    nc.vector.tensor_tensor(yg[:, s, :], yn[:, s, :], cst("gamma"), ALU.mult).then_inc(s_yg, 1)
                if live(1):
                    wait_apart(dve, s_n[0], 2 * (p - 1) + 1, s_wv)
                    nc.vector.bn_aggr(mv[:, 1 - s, 0, :], st6[:, 1 - s, 0, :]).then_inc(s_n[0], 1)
                if live(1) or live(3):
                    norms = slice(0 if live(1) else 1, 2 if live(3) else 1)
                    if live(1):
                        dve.wait_ge(s_n[0], 2 * p)
                    if live(3):
                        dve.wait_ge(s_n[1], 2 * p - 4)
                    at_least(dve, s_r, p - 2)
                    nc.vector.tensor_scalar(ve[:, 1 - s, norms], mv[:, 1 - s, norms, 1], EPS, None, ALU.add).then_inc(s_ve, 1)
                if live(2):
                    dve.wait_ge(s_yg, p - 1)
                    at_least(dve, s_uu, p - 3)
                    at_least(dve, s_h[s], 16 * ((p - 2 - s) >> 1))
                    nc.vector.tensor_tensor(hh[:, s, :], yg[:, s, :], cst("beta"), ALU.add).then_inc(s_hh, 1)
                elif live(4):
                    dve.wait_ge(s_uu, p - 3)

            dve.wait_ge(s_pack, 16)
            nc.vector.tensor_scalar(al[:], cst("alog"), 88.0, None, ALU.min).then_inc(s_c, 1)
            steps(dve, step)
            c = [1]

            def then(ins):
                ins.then_inc(s_c, 1)
                c[0] += 1
                dve.wait_ge(s_c, c[0])

            dve.wait_ge(s_dtv, T)
            then(nc.vector.scalar_tensor_tensor(t1[:], xf, -1.0, xf, ALU.mult, ALU.max))
            dve.wait_ge(s_sc, 2)
            then(nc.vector.tensor_scalar(w[:], e[:], 1.0, None, ALU.add))
            then(nc.vector.tensor_scalar(sl[:], e[:], 1.0 / 7.0, None, ALU.mult))
            for coef in (-1.0 / 6.0, 1.0 / 5.0, -1.0 / 4.0, 1.0 / 3.0, -1.0 / 2.0, 1.0):
                then(nc.vector.scalar_tensor_tensor(sl[:], sl[:], coef, e[:], ALU.add, ALU.mult))
            dve.wait_ge(s_sc, 3)
            then(nc.vector.tensor_tensor(w[:], w[:], sl[:], ALU.subtract))
            then(nc.vector.scalar_tensor_tensor(w[:], e[:], 0.0625, w[:], ALU.is_gt, ALU.mult))
            then(nc.vector.tensor_tensor(sl[:], sl[:], w[:], ALU.add))
            dt_flat = dtv[:].rearrange("b t e -> b (t e)")
            then(nc.vector.scalar_tensor_tensor(dt_flat, xf, 0.0, sl[:], ALU.max, ALU.add))
            then(nc.vector.scalar_tensor_tensor(av[:], dtv[:], -1.0, al[:].unsqueeze(1).broadcast_to([B, T, 8]), ALU.mult, ALU.mult))
            avf = av[:].rearrange("b t e -> b (t e)")
            then(nc.vector.tensor_scalar(avf, avf, LONGEST_DECAY, None, ALU.max))

        @block.gpsimd
        def _(pool):
            def step(p, r, live, more):
                s = r % 2
                if live(1) or live(3):
                    norms = slice(0 if live(1) else 1, 2 if live(3) else 1)
                    pool.wait_ge(s_ve, p)
                    at_least(pool, s_yn, min(p - 2, T) if isinstance(p, int) else p - 2)
                    at_least(pool, s_uu, p - 4)
                    nc.gpsimd.tensor_tensor(rs[:, 1 - s, norms], ve[:, 1 - s, norms], mhalf[:, norms], ALU.pow).then_inc(s_r, 1)
                if live(6):
                    q = p - 6
                    pool.wait_ge(s_uc, q + 1)
                    out = u_t.rearrange("d (b t) -> d b t", t=T)
                    out = out[:, :, q] if isinstance(q, int) else out[:, :, bass.ds(q, 1)].rearrange("d b o -> d (b o)")
                    nc.gpsimd.tensor_copy(out, uc[:, s, :]).then_inc(s_ut, 1)

            nc.gpsimd.memset(mhalf[:], -0.5).then_inc(s_mh, 1)
            pool.wait_ge(s_mh, 1)
            steps(pool, step)
            pool.wait_ge(s_ut, T)


def stage_mamba(nc, u_t, pk, dt_dram, a_dram, h_dram, h1_dram, loads=()):
    with ExitStack() as ctx:
        def sb(name, shape, dt=F32):
            return ctx.enter_context(nc.sbuf_tensor("mb_" + name, shape, dt))

        def ps(name):
            return ctx.enter_context(nc.psum_tensor("mb_" + name, [128, 512], F32))

        def sem(name):
            return ctx.enter_context(nc.semaphore("mb_" + name))

        def cst(name, parts=128):
            return pk[0:parts, COLS[name][0]:COLS[name][1]]

        acc = sb("acc", [128, 2, 5, QT])
        th = sb("th", [128, 5, QT])
        xs = sb("xs", [128, 2, 4, QT])
        bcs = sb("bcs", [NS, 2, 4, QT])
        tz = sb("tz", [128, 2, 2, QT])
        gz = sb("gz", [128, 2, 4, QT])
        dta = sb("dta", [PT, NP, 8])
        aa = sb("aa", [PT, NP, 8])
        a2 = sb("a2", [PT, 2, 2, 2, NH, T])
        ee = sb("ee", [PT, 2, 2, NH, T])
        gm = sb("gm", [PT, 2, 2, PT])
        tt = sb("tt", [PT, 2, 2, NH, PT])
        xd = sb("xd", [PT, 2, 8, HD])
        yv = sb("yv", [128, 4, QT])
        yg = sb("yg", [128, 4, QT])
        sq = sb("sq", [128, 4, QT])
        hq = sb("hq", [PT, 2, 2, D])
        ho = sb("ho", [PT, 2, 2, D])
        hm = sb("hm", [PT, 2, D])
        var = sb("var", [PT, 2, 2])
        rr = sb("rr", [PT, 2, 2])
        mhalf = sb("mhalf", [PT, 2])
        won = sb("won", [128, 4, D])
        psx = [ps("psx0"), ps("psx1")]
        psz, pss, pst, psg, = ps("psz"), ps("pss"), ps("pst"), ps("psg")
        psy = [ps("psy0"), ps("psy1")]

        s_ld, s_k, s_mh = sem("ld"), sem("k"), sem("mh")
        s_xp = sem("xp")
        s_zp = sem("zp")
        s_t0 = sem("t0")
        s_dc = sem("dc")
        s_th = sem("th")
        s_si = sem("si")
        s_tz = sem("tz")
        s_gz = sem("gz")
        s_a2 = sem("a2")
        s_s = sem("s")
        s_e = sem("e")
        s_g = sem("g")
        s_gm = sem("gm")
        s_tt = sem("tt")
        s_xt = sem("xt")
        s_xd = sem("xd")
        s_y = sem("y")
        s_yv = sem("yv")
        s_yg = sem("yg")
        s_sq = sem("sq")
        s_o = sem("o")
        s_va = sem("va")
        s_rr = sem("rr")
        s_h = sem("h")
        s_hq = [sem("hq0"), sem("hq1")]
        s_st = [sem("st0"), sem("st1")]

        block = ctx.enter_context(nc.Block())

        FIRST = 4

        def steps(eng, turn):
            for t in range(FIRST):
                turn(t, t % 2, lambda k, t=t: 0 <= t - k < NQ)
            with eng.Fori(0, (NQ - FIRST) // 2) as i:
                for s in range(2):
                    turn(2 * i + FIRST + s, s, lambda k: True)
            for t in range(NQ, NQ + 3):
                turn(t, t % 2, lambda k, t=t: 0 <= t - k < NQ)

        def half(n, s):
            return (n - s) // 2 if isinstance(n, int) else (n - s) >> 1

        def rows(dram, n):
            v = dram.rearrange("(n j r) d -> n r j d", j=2, r=PT)
            return v[n] if isinstance(n, int) else v[bass.ds(n, 1)].rearrange("o r j d -> (o r) j d")

        flat = lambda a: a.rearrange("p k q -> p (k q)")
        GROUPS = ((0, 1), (2, 3), (4,))
        pair_cols = lambda j: slice(j * PT, (j + 1) * PT)

        @block.sync
        def _(sp):
            v = lambda a: a.rearrange("b (t e) -> (b t) e", e=8).rearrange("(p r) e -> r p e", r=PT)
            sp.dma_start(dta[:], v(dt_dram)).then_inc(s_ld, 16)
            sp.dma_start(aa[:], v(a_dram)).then_inc(s_ld, 16)

            def turn(t, s, live):
                if live(2):
                    n = t - 2
                    at_least(sp, s_h, 4 * n - 4)
                    sp.dma_start(hq[:, s], rows(h_dram, n)).then_inc(s_hq[s], 16)
                if live(0):
                    for dst, src, s_load in loads:
                        at = slice(t, t + 1) if isinstance(t, int) else bass.ds(t, 1)
                        sp.dma_start(dst(at), src(at)).then_inc(s_load, 16)
                if live(3):
                    n = t - 3
                    sp.wait_ge(s_h, 4 * n + 4)
                    sp.dma_start(rows(h1_dram, n), ho[:, 1 - s]).then_inc(s_st[1 - s], 16)

            steps(sp, turn)
            for s in range(2):
                sp.wait_ge(s_st[s], 16 * (NQ // 2))

        @block.tensor
        def _(pe):
            pe.wait_ge(s_k, 4)

            def in_proj(n, s, g):
                bank = psx[(3 * s + g) % 2]
                at_least(pe, s_dc, 18 * n + 6 * (g - 1))
                u = u_t[:, n * QT:(n + 1) * QT] if isinstance(n, int) else u_t[:, bass.ds(n * QT, QT)]
                for k in GROUPS[g]:
                    last = nc.tensor.matmul(bank[:, (k % 2) * QT:(k % 2 + 1) * QT], cst("wx")[:, k * 128:(k + 1) * 128],
                                            u, start=True, stop=True)
                last.then_inc(s_xp, 1)

            def in_proj_z(n, d):
                at_least(pe, s_gz, 2 * n + d)
                u = u_t[:, n * QT:(n + 1) * QT] if isinstance(n, int) else u_t[:, bass.ds(n * QT, QT)]
                for k in (2 * d, 2 * d + 1):
                    last = nc.tensor.matmul(psz[:, (k % 2) * QT:(k % 2 + 1) * QT], cst("wz")[:, k * 128:(k + 1) * 128],
                                            u, start=True, stop=True)
                last.then_inc(s_zp, 1)

            def exponents(n, s, j):
                m = 2 * n + j
                pe.wait_ge(s_a2, 2 * m + 2)
                at_least(pe, s_e, m)
                for d in range(2):
                    last = nc.tensor.matmul(pss[0:PT, d * 180:(d + 1) * 180], cst(("later_f", "later_b")[d], PT),
                                            a2[:, s, j, d].rearrange("k h i -> k (h i)"), start=True, stop=True)
                last.then_inc(s_s, 1)

            def transpose_x(n, s, j):
                m = 2 * n + j
                pe.wait_ge(s_si, 8 * n + 4)
                at_least(pe, s_xd, m)
                for k in range(4):
                    last = nc.tensor.transpose(pst[0:PT, k * 128:(k + 1) * 128], xs[:, s, k, pair_cols(j)], cst("ident"))
                last.then_inc(s_xt, 1)

            def b_times_c(n, s):
                pe.wait_ge(s_si, 8 * n + 8)
                at_least(pe, s_gm, n)
                at_least(pe, s_h, 4 * n - 4)
                for j in range(2):
                    for d in range(2):
                        c = pair_cols(j)
                        last = nc.tensor.matmul(psg[0:PT, (2 * j + d) * PT:(2 * j + d + 1) * PT], bcs[:, s, 2 * d, c], bcs[:, s, 2 * d + 1, c],
                                                start=True, stop=True)
                last.then_inc(s_g, 1)

            def scan(n, j):
                m = 2 * n + j
                if j == 0:
                    at_least(pe, s_yv, 4 * n)
                pe.wait_ge(s_tt, 2 * m + 2)
                pe.wait_ge(s_xd, m + 1)
                for e in range(8):
                    k = e // 2
                    last = nc.tensor.matmul(psy[k // 2][64 * (e % 2):64 * (e % 2) + 64, (k % 2) * QT + j * PT:(k % 2) * QT + (j + 1) * PT],
                                            xd[:, j, e, :], tt[:, j, e // 4, e % 4, :], start=True, stop=True)
                last.then_inc(s_y, 1)

            def out_proj(n, j, g_done):
                m = 2 * n + j
                c = pair_cols(j)
                pe.wait_ge(s_yg, n + 1)
                pe.wait_ge(s_sq, n + 1)
                at_least(pe, s_h, 2 * m)
                at_least(pe, s_gm, g_done)
                for d in range(2):
                    for k in (2 * d, 2 * d + 1):
                        nc.tensor.matmul(psg[0:PT, d * D:(d + 1) * D], yg[:, k, c], won[:, k, :],
                                         start=(k % 2 == 0), stop=(k % 2 == 1))
                    for k in (2 * d, 2 * d + 1):
                        last = nc.tensor.matmul(psg[0:PT, 2 * D + 2 * d:2 * D + 2 + 2 * d], sq[:, k, c], cst("ones"),
                                                start=(k % 2 == 0), stop=(k % 2 == 1))
                last.then_inc(s_o, 1)

            def turn(t, s, live):
                g_done = min(t - 1, NQ) if isinstance(t, int) else t - 1
                if live(0):
                    in_proj(t, s, 0)
                if live(3):
                    out_proj(t - 3, 0, g_done)
                if live(0):
                    in_proj(t, s, 1)
                if live(2):
                    scan(t - 2, 0)
                    scan(t - 2, 1)
                if live(1):
                    transpose_x(t - 1, 1 - s, 0)
                    exponents(t - 1, 1 - s, 0)
                if live(3):
                    out_proj(t - 3, 1, g_done)
                if live(0):
                    in_proj_z(t, 0)
                if live(1):
                    transpose_x(t - 1, 1 - s, 1)
                    exponents(t - 1, 1 - s, 1)
                    b_times_c(t - 1, 1 - s)
                if live(0):
                    in_proj(t, s, 2)
                    in_proj_z(t, 1)

            steps(pe, turn)

        @block.scalar
        def _(act):
            def first_tap(n, s, g):
                act.wait_ge(s_xp, 3 * n + g + 1)
                at_least(act, s_si, 8 * n - 8)
                for k in GROUPS[g]:
                    nc.scalar.activation(acc[:, s, k, :], psx[(3 * s + g) % 2][:, (k % 2) * QT:(k % 2 + 1) * QT], ACT.Identity,
                                         bias=cst("cb")[:, k:k + 1], scale=cst("cw")[:, 4 * k + 3:4 * k + 4]).then_inc(s_t0, 1)

            def tanh_z(n, d):
                act.wait_ge(s_zp, 2 * n + d + 1)
                at_least(act, s_gz, 2 * n + d - 1)
                nc.scalar.activation(flat(tz[:, d]), psz[:, 0:2 * QT], ACT.Tanh, scale=0.5).then_inc(s_tz, 1)

            def tanh_x(n, s, g):
                act.wait_ge(s_dc, 18 * n + 6 * (g + 1))
                at_least(act, s_si, 8 * n)
                lo, hi = GROUPS[g][0], GROUPS[g][-1] + 1
                nc.scalar.activation(flat(th[:, lo:hi, :]), flat(acc[:, s, lo:hi, :]), ACT.Tanh, scale=0.5).then_inc(s_th, 1)

            def decays(n, j):
                m = 2 * n + j
                act.wait_ge(s_s, m + 1)
                at_least(act, s_tt, 2 * m - 2)
                nc.scalar.activation(ee[:, j].rearrange("k d h i -> k (d h i)"), pss[0:PT, 0:360], ACT.Exp).then_inc(s_e, 1)

            def gate_squares(n):
                act.wait_ge(s_yg, n + 1)
                at_least(act, s_o, 2 * n)
                nc.scalar.activation(flat(sq[:]), flat(yg[:]), ACT.Square).then_inc(s_sq, 1)

            def turn(t, s, live):
                if live(0):
                    first_tap(t, s, 0)
                    first_tap(t, s, 1)
                    tanh_x(t, s, 0)
                if live(1):
                    decays(t - 1, 0)
                if live(0):
                    tanh_x(t, s, 1)
                if live(2):
                    gate_squares(t - 2)
                if live(0):
                    tanh_z(t, 0)
                if live(1):
                    decays(t - 1, 1)
                if live(0):
                    first_tap(t, s, 2)
                    tanh_z(t, 1)
                    tanh_x(t, s, 2)

            steps(act, turn)

        @block.vector
        def _(dve):
            for k in range(4):
                nc.vector.tensor_scalar(won[:, k, :], cst("wo")[:, k * D:(k + 1) * D], cst("nw")[:, k:k + 1], None, ALU.mult).then_inc(s_k, 1)
            dve.wait_ge(s_ld, 32)

            def taps(n, s, g):
                parts = ([(0, 0, 128, False), (1, 0, 128, False)], [(2, 0, 128, True), (3, 0, 128, True)],
                         [(4, 0, 64, False), (4, 64, 128, True)])[g]
                by_batch = lambda ap: ap.rearrange("p (b t) -> p b t", t=T)
                dve.wait_ge(s_t0, 5 * n + (2, 4, 5)[g])
                for back in (1, 2, 3):
                    for j, (k, lo, hi, rev) in enumerate(parts):
                        w = cst("cw")[lo:hi, 4 * k + 3 - back:4 * k + 4 - back]
                        x = by_batch(psx[(3 * s + g) % 2][lo:hi, (k % 2) * QT:(k % 2 + 1) * QT])
                        a = by_batch(acc[lo:hi, s, k, :])
                        x, a = (x[:, :, back:], a[:, :, :T - back]) if rev else (x[:, :, :T - back], a[:, :, back:])
                        if back > 1:
                            dve.wait_ge(s_dc, 18 * n + 6 * g + 2 * (back - 1) + j - 1)
                        nc.vector.scalar_tensor_tensor(a, x, w, a, ALU.mult, ALU.add).then_inc(s_dc, 1)

            def gate(n, s, d):
                dve.wait_ge(s_tz, 2 * n + d + 1)
                if d == 0:
                    at_least(dve, s_yg, n - 1)
                nc.vector.scalar_tensor_tensor(flat(gz[:, s, 2 * d:2 * d + 2]), flat(tz[:, d]),
                                               1.0, psz[:, 0:2 * QT], ALU.add, ALU.mult).then_inc(s_gz, 1)

            def silu(n, s, g):
                dve.wait_ge(s_th, 3 * n + g + 1)
                if g < 2:
                    if g == 0:
                        at_least(dve, s_yv, 4 * n - 4)
                        at_least(dve, s_xt, 2 * n - 2)
                    for k in GROUPS[g]:
                        nc.vector.scalar_tensor_tensor(xs[:, s, k, :], th[:, k, :], 1.0, acc[:, s, k, :], ALU.add, ALU.mult).then_inc(s_si, 1)
                else:
                    at_least(dve, s_g, n - 1)
                    for e in range(4):
                        p = slice(32 * e, 32 * e + NS)
                        nc.vector.scalar_tensor_tensor(bcs[:, s, e, :], th[p, 4, :], 1.0, acc[p, s, 4, :], ALU.add, ALU.mult).then_inc(s_si, 1)

            def dt_times_x(n, j):
                m = 2 * n + j
                dve.wait_ge(s_xt, m + 1)
                at_least(dve, s_y, m - 1)
                steps_dt = dta[:, m, :] if isinstance(m, int) else dta[:, bass.ds(m, 1), :].rearrange("r o e -> r (o e)")
                nc.vector.tensor_tensor(xd[:, j], pst[0:PT, :].rearrange("r (e q) -> r e q", e=8),
                                        steps_dt.unsqueeze(2).broadcast_to([PT, 8, HD]), ALU.mult).then_inc(s_xd, 1)

            def mask(n):
                dve.wait_ge(s_g, n + 1)
                at_least(dve, s_tt, 4 * n)
                masks = pk[0:PT, COLS["gmask_f"][0]:COLS["gmask_b"][1]].unsqueeze(1).broadcast_to([PT, 2, 2 * PT])
                nc.vector.tensor_tensor(gm[:].rearrange("r j d i -> r j (d i)"), psg[0:PT, 0:4 * PT].rearrange("r (j e) -> r j e", j=2),
                                        masks, ALU.mult).then_inc(s_gm, 1)

            def skip(n, s):
                dve.wait_ge(s_y, 2 * n + 2)
                at_least(dve, s_yg, n)
                for k in range(4):
                    nc.vector.scalar_tensor_tensor(yv[:, k, :], xs[:, s, k, :], cst("dcol")[:, k:k + 1],
                                                   psy[k // 2][:, (k % 2) * QT:(k % 2 + 1) * QT], ALU.mult, ALU.add).then_inc(s_yv, 1)

            def mean_square(n, j):
                m = 2 * n + j
                dve.wait_ge(s_o, m + 1)
                at_least(dve, s_rr, m - 1)
                sums = psg[0:PT, 2 * D:2 * D + 4].rearrange("r (d o) -> r d o", o=2)[:, :, 0]
                nc.vector.tensor_scalar(var[:, j, :], sums, 1.0 / DI, 16 * EPS, ALU.mult, ALU.add).then_inc(s_va, 1)

            def residual(n, s, j):
                m = 2 * n + j
                dve.wait_ge(s_rr, m + 1)
                if j == 0:
                    dve.wait_ge(s_hq[s], 16 * (half(n, s) + 1))
                    at_least(dve, s_st[s], 16 * half(n, s))
                nc.vector.scalar_tensor_tensor(hm[:, j, :], psg[0:PT, 0:D], rr[:, j, 0:1], hq[:, s, j, :],
                                               ALU.mult, ALU.add).then_inc(s_h, 1)
                dve.wait_ge(s_h, 2 * m + 1)
                nc.vector.scalar_tensor_tensor(ho[:, s, j, :], psg[0:PT, D:2 * D], rr[:, j, 1:2], hm[:, j, :],
                                               ALU.mult, ALU.add).then_inc(s_h, 1)

            def turn(t, s, live):
                if live(0):
                    taps(t, s, 0)
                if live(3):
                    mean_square(t - 3, 0)
                if live(0):
                    taps(t, s, 1)
                if live(3):
                    residual(t - 3, 1 - s, 0)
                if live(2):
                    skip(t - 2, s)
                if live(1):
                    dt_times_x(t - 1, 0)
                if live(3):
                    mean_square(t - 3, 1)
                if live(0):
                    silu(t, s, 0)
                if live(3):
                    residual(t - 3, 1 - s, 1)
                if live(1):
                    dt_times_x(t - 1, 1)
                    mask(t - 1)
                if live(0):
                    silu(t, s, 1)
                    gate(t, s, 0)
                    taps(t, s, 2)
                    gate(t, s, 1)
                    silu(t, s, 2)

            steps(dve, turn)

        @block.gpsimd
        def _(pool):
            nc.gpsimd.memset(mhalf[:], -0.5).then_inc(s_mh, 1)
            pool.wait_ge(s_mh, 1)
            pool.wait_ge(s_ld, 32)

            def spread(n, s, j):
                m = 2 * n + j
                at_least(pool, s_s, m - 3)
                for d in range(2):
                    upto = cst(("upto_f", "upto_b")[d], PT).unsqueeze(1).broadcast_to([PT, NH, T])
                    av = aa[:, m, 4 * d:4 * d + 4] if isinstance(m, int) else aa[:, bass.ds(m, 1), 4 * d:4 * d + 4].rearrange("r o e -> r (o e)")
                    nc.gpsimd.tensor_tensor(a2[:, s, j, d], upto, av.unsqueeze(2).broadcast_to([PT, NH, T]), ALU.mult).then_inc(s_a2, 1)

            def weigh(n, j):
                m = 2 * n + j
                pool.wait_ge(s_e, m + 1)
                pool.wait_ge(s_gm, n + 1)
                at_least(pool, s_y, m - 1)
                for d in range(2):
                    o = tt[:, j, d].rearrange("r h (b i) -> r h b i", b=2)
                    x = ee[:, j, d].unsqueeze(2).broadcast_to([PT, NH, 2, T])
                    g = gm[:, j, d].rearrange("r (b i) -> r b i", b=2).unsqueeze(1).broadcast_to([PT, NH, 2, T])
                    nc.gpsimd.tensor_tensor(o, x, g, ALU.mult).then_inc(s_tt, 1)

            def root(n, j):
                m = 2 * n + j
                pool.wait_ge(s_va, m + 1)
                at_least(pool, s_h, 2 * m - 2)
                nc.gpsimd.tensor_tensor(rr[:, j, :], var[:, j, :], mhalf[:], ALU.pow).then_inc(s_rr, 1)

            def turn(t, s, live):
                if live(3):
                    root(t - 3, 0)
                if live(0):
                    spread(t, s, 0)
                if live(3):
                    root(t - 3, 1)
                if live(2):
                    n = t - 2
                    pool.wait_ge(s_yv, 4 * n + 4)
                    at_least(pool, s_o, 2 * n)
                    at_least(pool, s_sq, n)
                    nc.gpsimd.tensor_tensor(flat(yg[:]), flat(yv[:]), flat(gz[:, s]), ALU.mult).then_inc(s_yg, 1)
                if live(0):
                    spread(t, s, 1)
                if live(1):
                    weigh(t - 1, 0)
                    weigh(t - 1, 1)

            steps(pool, turn)


FT = 1024
FP = -(-FT // PT)
FE, FF = 8, 512
FG = 4


def stage_ffn(nc, pk, h1_dram, ew, ei, w1, w2):
    with ExitStack() as ctx:
        def sb(name, shape, dt=F32):
            return ctx.enter_context(nc.sbuf_tensor("ff_" + name, shape, dt))

        def ps(name):
            return ctx.enter_context(nc.psum_tensor("ff_" + name, [128, 512], F32))

        def sem(name):
            return ctx.enter_context(nc.semaphore("ff_" + name))

        ident = pk[:, COLS["ident"][0]:COLS["ident"][1]]
        NG = FP // FG
        GT = FG * PT
        KC = FF // 128
        hacc = sb("hacc", [PT, FP, D])
        st = sb("st", [PT, FP, 6])
        mv = sb("mv", [PT, FP, 2])
        ve = sb("ve", [PT, FP])
        rs = sb("rs", [PT, FP])
        mhalf = sb("mhalf", [PT, FP])
        uu = sb("uu", [PT, FP, D])
        ut = sb("ut", [D, FP * PT])
        wt = sb("wt", [PT, FP, 2])
        ix = sb("ix", [PT, FP, 2], I32)
        xf = sb("xf", [PT, FP, 2])
        part = sb("part", [PT, FE, FP, 2])
        comb = sb("comb", [PT, FE, FP])
        w1s = sb("w1s", [D, 2, FF])
        w2s = sb("w2s", [128, 2, KC, D])
        ht = sb("ht", [128, 2, KC, GT])
        psh = [ps(f"psh{c}") for c in range(KC)]
        pso = [ps("pso0"), ps("pso1")]
        psu = ps("psu")

        s_ld, s_z, s_v, s_r, s_u, s_tu, s_ut = (sem(n) for n in ("ld", "z", "v", "r", "u", "tu", "ut"))
        s_w = [sem("w0"), sem("w1")]
        s_cb = sem("cb")
        s_h = sem("h")
        s_g = sem("g")
        s_o = sem("o")
        s_a = sem("a")
        s_st = sem("st")
        block = ctx.enter_context(nc.Block())
        full = FT // PT
        rest = FT - full * PT
        h_rows = h1_dram[0:FP * PT, :].rearrange("(p r) d -> r p d", r=PT)
        UNITS = 2 * NG

        def units(eng, unit):
            def turn(i):
                for k in range(UNITS):
                    unit(eng, i, k)
            turns(eng, FE // 2, turn)

        @block.sync
        def _(sp):
            sp.dma_start(hacc[:], h_rows).then_inc(s_ld, 16)
            sp.wait_ge(s_z, 3)
            for dst, src in ((wt, ew), (ix, ei)):
                sp.dma_start(dst[:, 0:full, :], src[0:full * PT, :].rearrange("(p r) k -> r p k", r=PT)).then_inc(s_ld, 16)
                sp.dma_start(dst[0:rest, full, :], src[full * PT:FT, :]).then_inc(s_ld, 16)
            def load(i):
                for s in range(2):
                    e = 2 * i + s
                    at_least(sp, s_o, NG * 2 * i)
                    sp.dma_start(w1s[:, s, :], w1[bass.ds(e, 1)].rearrange("o d f -> (o d) f")).then_inc(s_w[s], 16)
                    sp.dma_start(w2s[:, s], w2[bass.ds(e, 1)].rearrange("o (c p) d -> (o p) c d", p=128)).then_inc(s_w[s], 16)
            turns(sp, FE // 2, load)
            sp.wait_ge(s_a, FE * FP)
            sp.dma_start(h_rows, hacc[:]).then_inc(s_st, 16)
            sp.wait_ge(s_st, 16)

        @block.gpsimd
        def _(pool):
            nc.gpsimd.memset(wt[:], 0.0).then_inc(s_z, 1)
            nc.gpsimd.memset(ix[:], 0).then_inc(s_z, 1)
            nc.gpsimd.memset(mhalf[:], -0.5).then_inc(s_z, 1)
            pool.wait_ge(s_v, 2)
            nc.gpsimd.tensor_tensor(rs[:], ve[:], mhalf[:], ALU.pow).then_inc(s_r, 1)

        @block.vector
        def _(dve):
            dve.wait_ge(s_ld, 16 * 5)
            for p in range(FP):
                last = nc.vector.bn_stats(st[:, p, :], hacc[:, p, :])
            last.then_inc(s_cb, 1)
            dve.wait_ge(s_cb, 1)
            for p in range(FP):
                last = nc.vector.bn_aggr(mv[:, p, :], st[:, p, :])
            last.then_inc(s_v, 1)
            dve.wait_ge(s_v, 1)
            nc.vector.tensor_scalar(ve[:], mv[:, :, 1], EPS, None, ALU.add).then_inc(s_v, 1)
            nc.vector.tensor_copy(xf[:], ix[:]).then_inc(s_cb, 1)
            dve.wait_ge(s_r, 1)
            for p in range(FP):
                nc.vector.tensor_scalar(uu[:, p, :], hacc[:, p, :], mv[:, p, 0:1], rs[:, p:p + 1], ALU.subtract, ALU.mult).then_inc(s_u, 1)
            dve.wait_ge(s_cb, 2)
            for e in range(FE):
                last = nc.vector.scalar_tensor_tensor(part[:, e], xf[:], float(e), wt[:], ALU.is_equal, ALU.mult)
            last.then_inc(s_cb, 1)
            dve.wait_ge(s_cb, 3)
            nc.vector.tensor_tensor(comb[:], part[:, :, :, 0], part[:, :, :, 1], ALU.add).then_inc(s_cb, 1)
            dve.wait_ge(s_cb, 4)
            dve.wait_ge(s_u, FP)

            def unit(dve, i, k):
                u, g = UNITS * i + k, k % NG
                dve.wait_ge(s_o, u + 1)
                at_least(dve, s_a, FG * u)
                for j in range(FG):
                    p = FG * g + j
                    cm = comb[:, bass.ds(2 * i + k // NG, 1), p]
                    nc.vector.scalar_tensor_tensor(hacc[:, p, :], pso[k % 2][0:PT, j * D:(j + 1) * D], cm, hacc[:, p, :],
                                                   ALU.mult, ALU.add).then_inc(s_a, 1)
            units(dve, unit)

        @block.scalar
        def _(act):
            for p in range(FP):
                act.wait_ge(s_tu, p + 1)
                nc.scalar.activation(ut[:, p * PT:(p + 1) * PT], psu[:, (p % 4) * 128:(p % 4) * 128 + PT], ACT.Copy).then_inc(s_ut, 1)

            def unit(act, i, k):
                u = UNITS * i + k
                for c in range(KC):
                    act.wait_ge(s_h, KC * u + c + 1)
                    if c == 0:
                        at_least(act, s_o, u - 1 if k else UNITS * i)
                    nc.scalar.activation(ht[:, k % 2, c, :], psh[c][:, 0:GT], ACT.Gelu).then_inc(s_g, 1)
            units(act, unit)

        @block.tensor
        def _(pe):
            for p in range(FP):
                pe.wait_ge(s_u, p + 1)
                if p >= 1:
                    pe.wait_ge(s_ut, p)
                nc.tensor.transpose(psu[:, (p % 4) * 128:(p % 4) * 128 + PT], uu[:, p, :], ident[0:PT, 0:PT]).then_inc(s_tu, 1)
            pe.wait_ge(s_ut, FP)

            def up(k, u, g):
                for c in range(KC):
                    at_least(pe, s_g, KC * (u - 1) + c + 1 if k else KC * u)
                    nc.tensor.matmul(psh[c][:, 0:GT], w1s[:, k // NG, c * 128:(c + 1) * 128], ut[:, g * GT:(g + 1) * GT],
                                     start=True, stop=True).then_inc(s_h, 1)

            def down(k, u):
                pe.wait_ge(s_g, KC * (u + 1))
                at_least(pe, s_a, FG * (u - 1) if k else FG * u)
                for j in range(FG):
                    for c in range(KC):
                        last = nc.tensor.matmul(pso[k % 2][0:PT, j * D:(j + 1) * D], ht[:, k % 2, c, j * PT:(j + 1) * PT],
                                                w2s[:, k // NG, c, :], start=(c == 0), stop=(c == KC - 1))
                last.then_inc(s_o, 1)

            def turn(i):
                for k in range(UNITS):
                    u = UNITS * i + k
                    if k % NG == 0:
                        pe.wait_ge(s_w[k // NG], 32 * (i + 1))
                    up(k, u, k % NG)
                    if k:
                        down(k - 1, u - 1)
                down(UNITS - 1, UNITS * i + UNITS - 1)
            turns(pe, FE // 2, turn)


E2, K2 = 32, 2
SLOTS = 128
NBL = -(-TOK * K2 // SLOTS) + E2 - 1
TINY = 1e-30
ROOM = -(-TOK // SLOTS) + 1
EMPTY = E2 * ROOM
XW = D + 1
SPARE = NBL * SLOTS


def stage_attention(nc, pk, h_in, h3_all, xs_dram, base, dm, ssum, s_sc):
    with ExitStack() as ctx:
        def sb(name, shape, dt=F32):
            return ctx.enter_context(nc.sbuf_tensor("at_" + name, shape, dt))

        def ps(name):
            return ctx.enter_context(nc.psum_tensor("at_" + name, [128, 512], F32))

        def sem(name):
            return ctx.enter_context(nc.semaphore("at_" + name))

        def cst(name, parts=128):
            return pk[0:parts, COLS[name][0]:COLS[name][1]]

        hq = sb("hq", [PT, 4, 2, D])
        st = sb("st", [PT, 2, 2, 2, 6])
        mv = sb("mv", [PT, 2, 2, 2, 2])
        ve = sb("ve", [PT, 2, 2, 2])
        rs = sb("rs", [PT, 2, 2, 2])
        mhalf = sb("mhalf", [PT, 2])
        uu = sb("uu", [PT, 2, 2, D])
        ut = sb("ut", [D, 2, QT])
        tqk = sb("tqk", [128, 2, QT])
        tv = sb("tv", [PT, 2, D])
        qk = sb("qk", [128, 2, 2, QT])
        vv = sb("vv", [PT, 2, 2, D + 2])
        ee = sb("ee", [PT, 2, 2, PT])
        pp = sb("pp", [PT, 2, 2, PT])
        den = sb("den", [PT, 2, 2])
        rd = sb("rd", [PT, 2, 2])
        xc = sb("xc", [PT, 2, 2, D])
        copies = sb("copies", [PT, 4, 2, 2, XW])
        oh = sb("oh", [PT, 2, 2, 2, E2])
        cnt = sb("cnt", [PT, 2, 2, E2])
        nxt = sb("nxt", [PT, 2, E2])
        prod = sb("prod", [PT, 4, E2])
        posf = sb("posf", [PT, 4])
        pos = [[sb(f"pos{s}{k}", [PT, 1], I32) for k in range(4)] for s in range(2)]
        xt = sb("xt", [D, 2, QT])
        lg = sb("lg", [PT, 2, 2, E2])
        m8 = sb("m8", [PT, 2, 2, 8])
        i8 = sb("i8", [PT, 2, 2, 8], U32)
        f8 = sb("f8", [PT, 2, 2, 8])
        ld = sb("ld", [PT, 2, 2, E2])
        le = sb("le", [PT, 2, 2, E2])
        psu, psqk, psv, pss, pso, psx, psl = (ps(n) for n in ("psu", "psqk", "psv", "pss", "pso", "psx", "psl"))
        psc = ps("psc")

        s_k = sem("k")
        s_hq = [sem(f"hq{k}") for k in range(4)]
        s_va = sem("va")
        s_ra = sem("ra")
        s_u = sem("u")
        s_tu, s_ut = sem("tu"), sem("ut")
        s_pq, s_pv = sem("pq"), sem("pv")
        s_tq, s_tv = sem("tq"), sem("tv")
        s_q, s_vv = sem("q"), sem("vv")
        s_s, s_e, s_p, s_o = sem("s"), sem("e"), sem("p"), sem("o")
        s_d = sem("d")
        s_h = sem("h")
        s_vb = sem("vb")
        s_rb = sem("rb")
        s_x = sem("x")
        s_xa = sem("xa")
        s_pc = sem("pc")
        s_b = sem("b")
        s_tx, s_xt, s_l = sem("tx"), sem("xt"), sem("l")
        s_m = sem("m")
        s_le = sem("le")
        s_wv, s_wp = sem("wv"), sem("wp")

        block = ctx.enter_context(nc.Block())

        FIRST = 8
        LAST = 7
        MS = 12

        def steps(eng, turn):
            for t in range(FIRST):
                turn(t, t % 4, lambda k, t=t: 0 <= t - k < NQ)
            with eng.Fori(0, (NQ - FIRST) // 4) as i:
                for r in range(4):
                    turn(4 * i + FIRST + r, r, lambda k: True)
            for t in range(NQ, NQ + LAST):
                turn(t, t % 4, lambda k, t=t: 0 <= t - k < NQ)

        def rounds(n, r, of):
            shift = {2: 1, 4: 2}[of]
            return (n - r) >> shift

        def rows(dram, n):
            v = dram.rearrange("(n j r) d -> n r j d", j=2, r=PT)
            return v[n] if isinstance(n, int) else v[bass.ds(n, 1)].rearrange("o r j d -> (o r) j d")

        def pair_rows(a, n):
            return a[:, 2 * n:2 * n + 2] if isinstance(n, int) else a[:, bass.ds(2 * n, 2)]

        flat = lambda a: a.rearrange("p k q -> p (k q)")
        pair_cols = lambda j: slice(j * PT, (j + 1) * PT)

        @block.sync
        def _(sp):
            def load(n, r):
                at_least(sp, s_h, 2 * n - 6)
                sp.dma_start(hq[:, r], rows(h_in, n)).then_inc(s_hq[r], 16)

            def turn(t, r, live):
                if live(-1):
                    load(t + 1, (r + 1) % 4)

            load(0, 0)
            for t in range(FIRST):
                turn(t, t % 4, lambda k, t=t: 0 <= t - k < NQ)
            with sp.Fori(0, (NQ - FIRST) // 4 - 1) as i:
                for r in range(4):
                    turn(4 * i + FIRST + r, r, lambda k: True)
            for t in range(NQ - 4, NQ):
                turn(t, t % 4, lambda k, t=t: 0 <= t - k < NQ)
            for s in range(4):
                sp.wait_ge(s_sc[s], 64 * (NQ // 4))

        @block.tensor
        def _(pe):
            def transpose_u(n, s):
                pe.wait_ge(s_u, 2 * n + 2)
                at_least(pe, s_ut, n)
                for j in range(2):
                    last = nc.tensor.transpose(psu[:, pair_cols(j)], uu[:, s, j, :], cst("ident", PT)[:, 0:PT])
                last.then_inc(s_tu, 1)

            def project(n, s):
                pe.wait_ge(s_ut, n + 1)
                at_least(pe, s_tq, n)
                for k, w in enumerate(("wq", "wk")):
                    last = nc.tensor.matmul(psqk[:, k * QT:(k + 1) * QT], cst(w), ut[:, s, :], start=True, stop=True)
                last.then_inc(s_pq, 1)
                at_least(pe, s_tv, n)
                for j in range(2):
                    last = nc.tensor.matmul(psv[0:PT, j * D:(j + 1) * D], ut[:, s, pair_cols(j)], cst("wv"), start=True, stop=True)
                last.then_inc(s_pv, 1)

            def scores(n, s):
                pe.wait_ge(s_q, n + 1)
                at_least(pe, s_e, n)
                for j in range(2):
                    c = pair_cols(j)
                    last = nc.tensor.matmul(pss[0:PT, c], qk[:, s, 1, c], qk[:, s, 0, c], start=True, stop=True)
                last.then_inc(s_s, 1)

            def weighted_sum(n, s):
                pe.wait_ge(s_p, n + 1)
                pe.wait_ge(s_vv, n + 1)
                at_least(pe, s_h, 2 * n)
                for j in range(2):
                    last = nc.tensor.matmul(pso[0:PT, j * (D + 2):(j + 1) * (D + 2)], pp[:, s, j, :], vv[:, s, j, :], start=True, stop=True)
                last.then_inc(s_o, 1)

            def transpose_x(n, s):
                pe.wait_ge(s_x, 2 * n + 2)
                at_least(pe, s_xt, n)
                for j in range(2):
                    last = nc.tensor.transpose(psx[:, pair_cols(j)], xc[:, s, j, :], cst("ident", PT)[:, 0:PT])
                last.then_inc(s_tx, 1)

            def logits(n, s):
                pe.wait_ge(s_xt, n + 1)
                at_least(pe, s_m, MS * n - 10)
                for j in range(2):
                    last = nc.tensor.matmul(psl[0:PT, j * E2:(j + 1) * E2], xt[:, s, pair_cols(j)], cst("wgate"), start=True, stop=True)
                last.then_inc(s_l, 1)

            def counts(n, s):
                pe.wait_ge(s_m, MS * n + 11)
                at_least(pe, s_b, 8 * (n - 1) + 2)
                c = lambda j: psc[0:PT, j * E2:(j + 1) * E2]
                nc.tensor.matmul(c(0), cst("tri", PT), cnt[:, s, 0, :], start=True, stop=True)
                nc.tensor.matmul(c(1), cst("tri", PT), cnt[:, s, 1, :], start=True, stop=False)
                nc.tensor.matmul(c(1), cst("onem", PT)[:, 0:PT], cnt[:, s, 0, :], start=False, stop=True)
                for j in range(2):
                    last = nc.tensor.matmul(psc[:, 2 * E2:3 * E2], cst("onem", PT), cnt[:, s, j, :], start=(j == 0), stop=(j == 1))
                last.then_inc(s_pc, 1)

            def turn(t, r, live):
                s = r % 2
                if live(2):
                    scores(t - 2, s)
                if live(6):
                    counts(t - 6, s)
                if live(1):
                    transpose_u(t - 1, 1 - s)
                if live(4):
                    transpose_x(t - 4, s)
                if live(1):
                    project(t - 1, 1 - s)
                if live(4):
                    logits(t - 4, s)
                if live(2):
                    weighted_sum(t - 2, s)

            steps(pe, turn)

        @block.scalar
        def _(act):
            def turn(t, r, live):
                s = r % 2
                if live(1):
                    n = t - 1
                    act.wait_ge(s_tu, n + 1)
                    at_least(act, s_pv, n - 1)
                    nc.scalar.activation(ut[:, 1 - s, :], psu[:, 0:QT], ACT.Copy).then_inc(s_ut, 1)
                if live(2):
                    n = t - 2
                    act.wait_ge(s_s, n + 1)
                    at_least(act, s_p, n - 1)
                    nc.scalar.activation(flat(ee[:, s]), pss[0:PT, 0:2 * PT], ACT.Exp, scale=float(D) ** -0.5).then_inc(s_e, 1)
                if live(4):
                    n = t - 4
                    act.wait_ge(s_tx, n + 1)
                    at_least(act, s_l, n - 1)
                    nc.scalar.activation(xt[:, s, :], psx[:, 0:QT], ACT.Copy).then_inc(s_xt, 1)
                if live(1):
                    n = t - 1
                    act.wait_ge(s_pq, n + 1)
                    at_least(act, s_q, n)
                    nc.scalar.activation(flat(tqk[:]), psqk[:, 0:2 * QT], ACT.Tanh, scale=0.5).then_inc(s_tq, 1)
                    act.wait_ge(s_pv, n + 1)
                    at_least(act, s_vv, n)
                    nc.scalar.activation(flat(tv[:]), psv[0:PT, 0:2 * D], ACT.Tanh, scale=0.5).then_inc(s_tv, 1)
                if live(4):
                    n = t - 4
                    at_least(act, s_sc[r], 64 * rounds(n, r, 4))
                    nc.scalar.activation(copies[:, r, :, :, 0:D], xc[:, s].unsqueeze(1).broadcast_to([PT, 2, 2, D]), ACT.Copy).then_inc(s_xa, 1)
                    ids = cst("tokid", PT).rearrange("r (k m) -> r k m", k=2)
                    ids = ids[:, :, 2 * n:2 * n + 2] if isinstance(n, int) else ids[:, :, bass.ds(2 * n, 2)]
                    nc.scalar.activation(copies[:, r, :, :, D], ids, ACT.Copy).then_inc(s_xa, 1)
                if live(5):
                    n = t - 5
                    act.wait_ge(s_m, MS * n + 6)
                    at_least(act, s_m, MS * (n - 1))
                    nc.scalar.activation(le[:, 1 - s], ld[:, 1 - s], ACT.Exp).then_inc(s_le, 1)

            steps(act, turn)

        @block.vector
        def _(dve):
            for s in range(2):
                for j in range(2):
                    nc.vector.memset(vv[:, s, j, D:D + 2], 1.0).then_inc(s_k, 1)
            nc.vector.tensor_scalar(base, cst("iota32"), float(ROOM * SLOTS), None, ALU.mult).then_inc(s_k, 1)

            def stats(x, which, s, s_v):
                for j in range(2):
                    nc.vector.bn_stats(st[:, which, s, j, :], x(j)).then_inc(s_v, 1)

            def mean_var(which, n, s, s_v):
                for j in range(2):
                    wait_apart(dve, s_v, 5 * n + j + 1, s_wv)
                    nc.vector.bn_aggr(mv[:, which, s, j, :], st[:, which, s, j, :]).then_inc(s_v, 1)

            def add_eps(which, n, s, s_v):
                dve.wait_ge(s_v, 5 * n + 4)
                nc.vector.tensor_scalar(ve[:, which, s, :], mv[:, which, s, :, 1], EPS, None, ALU.add).then_inc(s_v, 1)

            def normed(x, which, s, out, s_out):
                for j in range(2):
                    nc.vector.tensor_scalar(out[:, j, :], x(j), mv[:, which, s, j, 0:1], rs[:, which, s, j:j + 1],
                                            ALU.subtract, ALU.mult).then_inc(s_out, 1)

            def turn(t, r, live):
                s = r % 2
                o = pso[0:PT, 0:2 * (D + 2)].rearrange("r (j c) -> r j c", j=2)
                n, q, e = t, t - 3, t - 5
                s1 = 1 - s
                h3 = lambda j: h3_all[:, q + q + j, :] if isinstance(q, int) else h3_all[:, bass.ds(2 * q + j, 1), :].rearrange("r o d -> r (o d)")
                c = t - 6
                if live(0):
                    dve.wait_ge(s_hq[r], 16 * (rounds(n, r, 4) + 1))
                    at_least(dve, s_u, 2 * n - 2)
                    stats(lambda j: hq[:, r, j, :], 0, s, s_va)
                if live(3):
                    dve.wait_ge(s_o, q + 1)
                    at_least(dve, s_h, 2 * q - 2)
                    nc.vector.tensor_scalar(den[:, s1, :], o[:, :, D], TINY, None, ALU.max).then_inc(s_d, 1)
                if live(5):
                    dve.wait_ge(s_l, e + 1)
                    at_least(dve, s_le, e - 1)
                    bg = cst("bgate", PT).unsqueeze(1).broadcast_to([PT, 2, E2])
                    nc.vector.tensor_tensor(lg[:, s1], psl[0:PT, 0:2 * E2].rearrange("r (j e) -> r j e", j=2), bg, ALU.add).then_inc(s_m, 1)
                if live(0):
                    mean_var(0, n, s, s_va)
                if live(6):
                    dve.wait_ge(s_pc, c + 1)
                    nc.vector.tensor_tensor(nxt[:], psc[0:PT, 0:2 * E2].rearrange("r (j e) -> r j e", j=2),
                                            base[0:PT, :].unsqueeze(1).broadcast_to([PT, 2, E2]), ALU.add).then_inc(s_b, 1)
                if live(3):
                    dve.wait_ge(s_d, 2 * q + 1)
                    nc.vector.reciprocal(rd[:, s1, :], den[:, s1, :]).then_inc(s_d, 1)
                if live(5):
                    wait_apart(dve, s_m, MS * e + 1, s_wv)
                    for j in range(2):
                        nc.vector.max(m8[:, s1, j, :], lg[:, s1, j, :]).then_inc(s_m, 1)
                if live(6):
                    dve.wait_ge(s_b, 8 * c + 1)
                    nc.vector.tensor_tensor(base, base, psc[:, 2 * E2:3 * E2], ALU.add).then_inc(s_b, 1)
                    nc.vector.tensor_tensor(prod[:].rearrange("r (k j) e -> r k (j e)", k=2), oh[:, s].rearrange("r k j e -> r k (j e)"),
                                            nxt[:].rearrange("r j e -> r (j e)").unsqueeze(1).broadcast_to([PT, 2, 2 * E2]), ALU.mult).then_inc(s_b, 1)
                if live(0):
                    add_eps(0, n, s, s_va)
                if live(3):
                    dve.wait_ge(s_d, 2 * q + 2)
                    for j in range(2):
                        nc.vector.scalar_tensor_tensor(h3(j), o[:, j, 0:D], rd[:, s1, j:j + 1], hq[:, (r - 3) % 4, j, :], ALU.mult, ALU.add).then_inc(s_h, 1)
                if live(5):
                    wait_apart(dve, s_m, MS * e + 3, s_wv)
                    for j in range(2):
                        nc.vector.max_index(i8[:, s1, j, :], m8[:, s1, j, :], lg[:, s1, j, :]).then_inc(s_m, 1)
                    nc.vector.tensor_tensor(ld[:, s1], lg[:, s1], m8[:, s1, :, 0:1].broadcast_to([PT, 2, E2]), ALU.subtract).then_inc(s_m, 1)
                if live(3):
                    wait_apart(dve, s_h, 2 * q + 2, s_wv)
                    stats(h3, 1, s1, s_vb)
                if live(5):
                    dve.wait_ge(s_m, MS * e + 5)
                    nc.vector.tensor_copy(f8[:, s1], i8[:, s1]).then_inc(s_m, 1)
                if live(0):
                    dve.wait_ge(s_ra, n + 1)
                    at_least(dve, s_tu, n - 1)
                    normed(lambda j: hq[:, r, j, :], 0, s, uu[:, s], s_u)
                if live(3):
                    mean_var(1, q, s1, s_vb)
                if live(5):
                    dve.wait_ge(s_m, MS * e + 7)
                    io = cst("iota32", PT).unsqueeze(1).broadcast_to([PT, 2, E2])
                    for k in range(2):
                        nc.vector.tensor_tensor(oh[:, s1, k], io, f8[:, s1, :, k:k + 1].broadcast_to([PT, 2, E2]), ALU.is_equal).then_inc(s_m, 1)
                if live(3):
                    add_eps(1, q, s1, s_vb)
                if live(5):
                    nc.vector.tensor_tensor(pair_rows(dm, e), m8[:, s1, :, 1], m8[:, s1, :, 0], ALU.subtract).then_inc(s_m, 1)
                    dve.wait_ge(s_m, MS * e + 9)
                    nc.vector.tensor_tensor(cnt[:, s1], oh[:, s1, 0], oh[:, s1, 1], ALU.add).then_inc(s_m, 1)
                if live(6):
                    dve.wait_ge(s_b, 8 * c + 3)
                    nc.vector.tensor_reduce(posf[:], prod[:], AX_X, ALU.add).then_inc(s_b, 1)
                if live(1):
                    dve.wait_ge(s_tq, t)
                    at_least(dve, s_s, t - 2)
                    nc.vector.tensor_scalar(qk[:, s1], tqk[:], 0.5, 0.5, ALU.mult, ALU.add).then_inc(s_q, 1)
                    dve.wait_ge(s_tv, t)
                    at_least(dve, s_o, t - 2)
                    nc.vector.tensor_scalar(vv[:, s1, :, 0:D], tv[:], 0.5, 0.5, ALU.mult, ALU.add).then_inc(s_vv, 1)
                if live(6):
                    dve.wait_ge(s_b, 8 * c + 4)
                    at_least(dve, s_sc[(r - 8) % 4], 64 * rounds(c - 2, (r - 8) % 4, 4) + 64 if not isinstance(c, int) or c >= 2 else 0)
                    for k in range(4):
                        nc.vector.tensor_copy(pos[s][k][:], posf[:, k:k + 1]).then_inc(s_b, 1)
                if live(3):
                    dve.wait_ge(s_rb, q + 1)
                    at_least(dve, s_tx, q - 1)
                    at_least(dve, s_xa, 2 * q - 2)
                    normed(h3, 1, s1, xc[:, s1], s_x)
                if live(5):
                    dve.wait_ge(s_le, e + 1)
                    nc.vector.tensor_reduce(pair_rows(ssum, e), le[:, s1], AX_X, ALU.add).then_inc(s_m, 1)

            steps(dve, turn)

        @block.gpsimd
        def _(pool):
            nc.gpsimd.memset(mhalf[:], -0.5).then_inc(s_k, 1)
            pool.wait_ge(s_k, 6)

            def root(which, n, s, s_v, s_out, s_r):
                pool.wait_ge(s_v, 5 * n + 5)
                at_least(pool, s_out, 2 * n - 2)
                nc.gpsimd.tensor_tensor(rs[:, which, s, :], ve[:, which, s, :], mhalf[:], ALU.pow).then_inc(s_r, 1)

            def turn(t, r, live):
                s = r % 2

                def send(*which):
                    if live(7):
                        if 0 in which:
                            pool.wait_ge(s_b, 8 * (t - 7) + 8)
                            wait_apart(pool, s_xa, 2 * (t - 7) + 2, s_wp)
                        for k in which:
                            pool.indirect_dma_start(xs_dram, bass.IndirectOffsetOnAxis(ap=pos[1 - s][k][:], axis=0),
                                                    copies[:, (r + 1) % 4, k // 2, k % 2, :], None).then_inc(s_sc[(r + 1) % 4], 16)

                send(0, 1)
                if live(0):
                    root(0, t, s, s_va, s_u, s_ra)
                if live(2):
                    n = t - 2
                    pool.wait_ge(s_e, n + 1)
                    at_least(pool, s_o, n - 1)
                    nc.gpsimd.tensor_tensor(pp[:, s], ee[:, s], cst("amask", PT).unsqueeze(1).broadcast_to([PT, 2, PT]), ALU.mult).then_inc(s_p, 1)
                send(2)
                if live(3):
                    root(1, t - 3, 1 - s, s_vb, s_x, s_rb)
                send(3)

            steps(pool, turn)


F2 = 256
FC = F2 // 128
WB = 2 * F2 + D


def stage_plan(nc, pk, base, slot_rows, bias_in, bias_dram, xs_dram, s_bias):
    with ExitStack() as ctx:
        def sb(name, shape, dt=F32):
            return ctx.enter_context(nc.sbuf_tensor("pl_" + name, shape, dt))

        def sem(name):
            return ctx.enter_context(nc.semaphore("pl_" + name))

        def cst(name, parts=128):
            return pk[0:parts, COLS[name][0]:COLS[name][1]]

        n_e = sb("ne", [128, E2])
        n_i = sb("ni", [128, E2], I32)
        nb_i = sb("nbi", [128, E2], I32)
        en = [sb(f"en{k}", [128, E2]) for k in range(2)]
        nb = sb("nb", [128, E2])
        le = sb("le", [128, E2])
        first = sb("first", [128, E2])
        ebf = sb("ebf", [128, 1])
        fbf = sb("fbf", [128, 1])
        abf = sb("abf", [128, 1])
        open_slots = sb("open_slots", [SLOTS, XW])
        bf = sb("bf", [E2, WB])
        bh = [sb(f"bh{k}", [E2, WB], BF16) for k in range(3)]
        br = [sb(f"br{k}", [E2, WB]) for k in range(2)]
        psr = ctx.enter_context(nc.psum_tensor("pl_psr", [128, 512], F32))

        s_ld, s_c, s_z, s_row, s_b, s_ee, s_ea = (sem(n) for n in ("ld", "c", "z", "row", "b", "ee", "ea"))
        s_tail = [sem(f"tail{k}") for k in range(2)]
        block = ctx.enter_context(nc.Block())
        NB = slice(0, 128)
        PLACES = slice(128, 256)
        NEXT = slice(256, 256 + E2)

        def fill(eng, experts, s_tail):
            eng.wait_ge(s_z, 3)
            for e in experts:
                row = eng.value_load(slot_rows[0:1, NEXT.start + e:NEXT.start + e + 1], min_val=0, max_val=EMPTY * SLOTS - SLOTS)
                eng.dma_start(xs_dram[bass.ds(row, SLOTS), :], open_slots[:]).then_inc(s_tail, 16)
            eng.wait_ge(s_tail, 16 * len(experts))

        @block.sync
        def _(sp):
            for lo, src in zip((0, F2, 2 * F2), bias_in):
                sp.dma_start(bf[:, lo:lo + src.shape[1]], src).then_inc(s_ld, 16)
            fill(sp, range(0, E2, 2), s_tail[0])
            sp.wait_ge(s_b, 6)
            for k in range(3):
                sp.dma_start(bias_dram[:, k, :], bh[k][:]).then_inc(s_bias, 16)
            sp.dma_start(xs_dram[EMPTY * SLOTS:(EMPTY + 1) * SLOTS, :], open_slots[:]).then_inc(s_bias, 16)
            sp.wait_ge(s_bias, 64)

        @block.scalar
        def _(act):
            fill(act, range(1, E2, 2), s_tail[1])

        @block.tensor
        def _(pe):
            pe.wait_ge(s_ee, 1)
            nc.tensor.matmul(psr[0:1, 0:128], ebf[:], cst("ident"), start=True, stop=True)
            pe.wait_ge(s_ea, 1)
            nc.tensor.matmul(psr[0:1, 128:256], abf[:], cst("ident"), start=True, stop=True).then_inc(s_row, 1)

        @block.gpsimd
        def _(pool):
            nc.gpsimd.memset(open_slots[:, 0:D], 0.0).then_inc(s_z, 1)
            nc.gpsimd.memset(open_slots[:, D:XW], -1.0).then_inc(s_z, 1)
            pool.wait_ge(s_ld, 48)
            nc.gpsimd.tensor_copy(bh[0][:], bf[:]).then_inc(s_b, 1)
            pool.wait_ge(s_b, 1)
            nc.gpsimd.tensor_tensor(br[0][:], bf[:], bh[0][:], ALU.subtract).then_inc(s_b, 1)
            pool.wait_ge(s_b, 2)
            nc.gpsimd.tensor_copy(bh[1][:], br[0][:]).then_inc(s_b, 1)
            pool.wait_ge(s_b, 3)
            nc.gpsimd.tensor_tensor(br[1][:], br[0][:], bh[1][:], ALU.subtract).then_inc(s_b, 1)
            pool.wait_ge(s_b, 4)
            nc.gpsimd.tensor_copy(bh[2][:], br[1][:]).then_inc(s_b, 2)

        @block.vector
        def _(dve):
            c = [0]

            def then(ins):
                ins.then_inc(s_c, 1)
                c[0] += 1
                dve.wait_ge(s_c, c[0])

            nc.vector.tensor_copy(slot_rows[0:1, NEXT], base[0:1, :]).then_inc(s_z, 1)
            then(nc.vector.scalar_tensor_tensor(n_e[:], cst("iota32"), -float(ROOM * SLOTS), base, ALU.mult, ALU.add))
            then(nc.vector.tensor_scalar(n_e[:], n_e[:], float(SLOTS - 1), None, ALU.add))
            then(nc.vector.tensor_copy(n_i[:], n_e[:]))
            then(nc.vector.tensor_scalar(nb_i[:], n_i[:], SLOTS.bit_length() - 1, None, ALU.logical_shift_right))
            then(nc.vector.tensor_copy(nb[:], nb_i[:]))
            a, b = nb, en[0]
            other = en[1]
            step = 1
            while step < E2:
                then(nc.vector.tensor_copy(b[:, :step], a[:, :step]))
                then(nc.vector.tensor_tensor(b[:, step:], a[:, step:], a[:, :E2 - step], ALU.add))
                a, b = b, (other if b is en[0] else en[0])
                step *= 2
            then(nc.vector.tensor_scalar(le[:], a[:], cst("bcol"), None, ALU.is_le))
            then(nc.vector.tensor_reduce(ebf[:], le[:], AX_X, ALU.add))
            then(nc.vector.tensor_tensor(first[:], le[:], nb[:], ALU.mult))
            then(nc.vector.tensor_reduce(fbf[:], first[:], AX_X, ALU.add))
            then(nc.vector.scalar_tensor_tensor(abf[:], ebf[:], float(ROOM), cst("bcol"), ALU.mult, ALU.add))
            then(nc.vector.tensor_tensor(abf[:], abf[:], fbf[:], ALU.subtract))
            nc.vector.tensor_scalar(abf[:], abf[:], float(EMPTY), None, ALU.min).then_inc(s_ea, 1)
            nc.vector.tensor_scalar(ebf[:], ebf[:], float(E2 - 1), None, ALU.min).then_inc(s_ee, 1)
            dve.wait_ge(s_row, 1)
            then(nc.vector.tensor_copy(slot_rows[0:1, 0:256], psr[0:1, 0:256]))


def stage_experts(nc, pk, h3_all, slot_rows, dm, ssum, wgu, wd, bias_dram, xs_dram, ys_dram, out_dram, s_w, n_w, s_st):
    with ExitStack() as ctx:
        def sb(name, shape, dt=F32):
            return ctx.enter_context(nc.sbuf_tensor("ex_" + name, shape, dt))

        def ps(name):
            return ctx.enter_context(nc.psum_tensor("ex_" + name, [128, 512], F32))

        def sem(name):
            return ctx.enter_context(nc.semaphore("ex_" + name))

        def cst(name, parts=128):
            return pk[0:parts, COLS[name][0]:COLS[name][1]]

        RING = 4
        CP = 8
        xb = sb("xb", [SLOTS, RING, XW])
        rows_to = [sb(f"rows_to{k}", [SLOTS, 1], I32) for k in range(RING)]
        bb = sb("bb", [3, RING, WB], BF16)
        one3 = sb("one3", [3, SLOTS], BF16)
        spares = sb("spares", [SLOTS, 128])
        xt = sb("xt", [D, 2, SLOTS])
        sg = sb("sg", [SLOTS, 2, F2])
        hh = sb("hh", [SLOTS, 2, F2])
        ht = sb("ht", [128, 2, FC, SLOTS])
        yb = sb("yb", [SLOTS, RING, D])
        pw = sb("pw", [PT, 2, NP])
        pw2 = sb("pw2", [PT, NP])
        yy = sb("yy", [PT, 2, 2, CP, D])
        ha = sb("ha", [PT, 2, CP, D])
        ho = sb("ho", [PT, 2, CP, D])
        psx = ps("psx")
        psg = [ps("psg0"), ps("psg1")]
        psh = [ps("psh0"), ps("psh1")]
        psy = [ps("psy0"), ps("psy1")]

        s_k = sem("k")
        s_x = [sem(f"x{k}") for k in range(RING)]
        s_tx, s_xt, s_g, s_sg, s_hh, s_th, s_ht, s_y, s_yb = (sem(n) for n in ("tx", "xt", "g", "sg", "hh", "th", "ht", "y", "yb"))
        s_to = sem("to")
        s_pw = sem("pw")
        s_wp = sem("wp")
        s_yy = [sem(f"yy{k}") for k in range(2)]
        s_bi = [sem(f"bi{k}") for k in range(RING)]
        s_a = sem("a")
        s_out = [sem(f"out{k}") for k in range(2)]

        block = ctx.enter_context(nc.Block())
        PEEL = 5
        TURNS = (NBL - 3 - PEEL) // RING
        REST = PEEL + RING * TURNS

        def steps(eng, step):
            for n in range(PEEL):
                step(eng, n, n % RING, n)
            with eng.Fori(0, TURNS) as i:
                for k in range(RING):
                    step(eng, RING * i + PEEL + k, (PEEL + k) % RING, None)
            for n in range(REST, NBL + 3):
                step(eng, n, n % RING, n)

        def live(known, back):
            return known is None or 0 <= known - back < NBL

        def rows(dram, n):
            v = dram.rearrange("(n s) d -> n s d", s=SLOTS)
            return v[n] if isinstance(n, int) else v[bass.ds(n, 1)].rearrange("o s d -> (o s) d")

        def of_block(eng, at, n, most):
            return eng.value_load(slot_rows[0:1, at + n:at + n + 1] if isinstance(n, int) else slot_rows[0:1, bass.ds(n + at, 1)], min_val=0, max_val=most)

        def expert(eng, n):
            return of_block(eng, 0, n, E2 - 1)

        results = ys_dram[SPARE:SPARE + 2 * TOK].rearrange("(k p r) d -> r k p d", k=2, r=PT)
        outs = out_dram.rearrange("(p r) d -> r p d", r=PT)

        @block.gpsimd
        def _(pool):
            nc.gpsimd.memset(one3[:], 1.0).then_inc(s_k, 1)

            def step(pool, n, s, known):
                if live(known, 3):
                    b, r = n - 3, (s - 3) % RING
                    pool.wait_ge(s_to, b + 1)
                    wait_apart(pool, s_yb, b + 1, s_wp)
                    pool.indirect_dma_start(ys_dram, bass.IndirectOffsetOnAxis(ap=rows_to[r][:], axis=0), yb[:, r, :], None).then_inc(s_st[r], 16)

            steps(pool, step)
            for r in range(RING):
                pool.wait_ge(s_st[r], 16 * ((NBL + RING - 1 - r) // RING))
            pool.sem_inc(s_k, 1)

        @block.sync
        def _(sp):
            def load_x(m, s):
                place = of_block(sp, 128, m, EMPTY)
                sp.dma_start(xb[:, s, :], rows(xs_dram, place)).then_inc(s_x[s], 16)

            def load_bias(m, s):
                e = expert(sp, m)
                sp.dma_start(bb[:, s, :], bias_dram[bass.ds(e, 1)].rearrange("o k w -> (o k) w")).then_inc(s_bi[s], 16)

            for m in range(3):
                load_x(m, m)
            load_bias(0, 0)

            def step(sp, n, s, known):
                if known is None or known + 3 < NBL:
                    at_least(sp, s_tx, n)
                    at_least(sp, s_to, n)
                    load_x(n + 3, (s + 3) % RING)
                if known is None or known + 1 < NBL:
                    at_least(sp, s_y, n - 2)
                    load_bias(n + 1, (s + 1) % RING)

            steps(sp, step)
            sp.wait_ge(s_k, 2)

            def load_results(q, s):
                for k in range(K2):
                    src = results[:, k, q * CP:(q + 1) * CP, :] if isinstance(q, int) else results[:, k, bass.ds(q * CP, CP), :]
                    sp.dma_start(yy[:, s, k], src).then_inc(s_yy[s], 16)

            for q in range(2):
                load_results(q, q)
            for q in range(NP // CP):
                s = q % 2
                sp.wait_ge(s_a, 2 * CP * (q + 1))
                sp.dma_start(outs[:, q * CP:(q + 1) * CP, :], ho[:, s]).then_inc(s_out[s], 16)
                if q + 2 < NP // CP:
                    load_results(q + 2, s)
            for s in range(2):
                sp.wait_ge(s_out[s], 16 * (NP // CP // 2))

        @block.tensor
        def _(pe):
            pe.wait_ge(s_w, n_w)
            pe.wait_ge(s_k, 1)

            def step(pe, n, s, known):
                if live(known, 1):
                    b, r = n - 1, (s - 1) % RING
                    e = expert(pe, b)
                    pe.wait_ge(s_xt, b + 1)
                    pe.wait_ge(s_bi[r], 16 * (b // RING + 1) if known is not None else 16 * ((b >> 2) + 1))
                    at_least(pe, s_hh, b - 1)
                    nc.tensor.matmul(psg[r % 2][:], xt[:, r % 2, :], wgu[:, bass.ds(e, 1), :].rearrange("p o f -> p (o f)"), start=True, stop=False)
                    nc.tensor.matmul(psg[r % 2][:], one3[:], bb[:, r, 0:2 * F2], start=False, stop=True).then_inc(s_g, 1)
                if live(known, 3):
                    b, r = n - 3, (s - 3) % RING
                    e = expert(pe, b)
                    pe.wait_ge(s_ht, b + 1)
                    at_least(pe, s_yb, b - 1)
                    for c in range(FC):
                        nc.tensor.matmul(psy[r % 2][:, 0:D], ht[:, r % 2, c, :], wd[:, bass.ds(e, 1), c, :].rearrange("p o d -> p (o d)"), start=(c == 0), stop=False)
                    nc.tensor.matmul(psy[r % 2][:, 0:D], one3[:], bb[:, r, 2 * F2:], start=False, stop=True).then_inc(s_y, 1)
                if live(known, 0):
                    pe.wait_ge(s_x[s], 16 * (n // RING + 1) if known is not None else 16 * ((n >> 2) + 1))
                    at_least(pe, s_xt, n)
                    nc.tensor.transpose(psx[:, 0:SLOTS], xb[:, s, 0:D], cst("ident")).then_inc(s_tx, 1)
                if live(known, 2):
                    b, r = n - 2, (s - 2) % RING
                    pe.wait_ge(s_hh, b + 1)
                    at_least(pe, s_ht, b - 1)
                    for c in range(FC):
                        last = nc.tensor.transpose(psh[r % 2][:, c * SLOTS:(c + 1) * SLOTS], hh[:, r % 2, c * 128:(c + 1) * 128], cst("ident"))
                    last.then_inc(s_th, 1)

            steps(pe, step)

        @block.scalar
        def _(act):
            nc.scalar.activation(pw[:, 1, :], dm, ACT.Exp).then_inc(s_pw, 1)

            def step(act, n, s, known):
                if live(known, 1):
                    b, r = n - 1, (s - 1) % 2
                    act.wait_ge(s_g, b + 1)
                    at_least(act, s_hh, b - 1)
                    nc.scalar.activation(sg[:, r, :], psg[r][:, 0:F2], ACT.Silu).then_inc(s_sg, 1)
                if live(known, 0):
                    act.wait_ge(s_tx, n + 1)
                    at_least(act, s_g, n - 1)
                    nc.scalar.activation(xt[:, s % 2, :], psx[:, 0:SLOTS], ACT.Copy).then_inc(s_xt, 1)
                if live(known, 2):
                    b, r = n - 2, s % 2
                    act.wait_ge(s_th, b + 1)
                    at_least(act, s_y, b - 1)
                    nc.scalar.activation(ht[:, r].rearrange("p c s -> p (c s)"), psh[r][:, 0:FC * SLOTS], ACT.Copy).then_inc(s_ht, 1)

            steps(act, step)

        @block.vector
        def _(dve):
            nc.vector.reciprocal(pw[:, 0, :], ssum).then_inc(s_pw, 1)
            nc.vector.tensor_scalar(spares[:], cst("block0"), cst("bcol"), None, ALU.add).then_inc(s_pw, 1)
            dve.wait_ge(s_pw, 3)
            nc.vector.tensor_tensor(pw2[:], pw[:, 1, :], pw[:, 0, :], ALU.mult).then_inc(s_pw, 1)

            def step(dve, n, s, known):
                if live(known, 1):
                    b, r = n - 1, (s - 1) % RING
                    dve.wait_ge(s_tx, n)
                    at_least(dve, s_st[r], 16 * (b // RING) if known is not None else 16 * ((b - r) >> 2))
                    spare = spares[:, b:b + 1] if isinstance(n, int) else spares[:, bass.ds(b, 1)]
                    nc.vector.tensor_tensor(rows_to[r][:], xb[:, r, D:XW], spare, ALU.max).then_inc(s_to, 1)
                if live(known, 3):
                    b, r = n - 3, (s - 3) % RING
                    dve.wait_ge(s_y, b + 1)
                    at_least(dve, s_st[r], 16 * (b // RING) if known is not None else 16 * ((b - r) >> 2))
                    nc.vector.tensor_copy(yb[:, r, :], psy[r % 2][:, 0:D]).then_inc(s_yb, 1)
                if live(known, 1):
                    b, r = n - 1, (s - 1) % 2
                    dve.wait_ge(s_sg, b + 1)
                    at_least(dve, s_th, b - 1)
                    nc.vector.tensor_tensor(hh[:, r, :], sg[:, r, :], psg[r][:, F2:2 * F2], ALU.mult).then_inc(s_hh, 1)

            steps(dve, step)
            dve.wait_ge(s_pw, 4)
            for q in range(NP // CP):
                s = q % 2
                dve.wait_ge(s_yy[s], 32 * (q // 2 + 1))
                at_least(dve, s_out[s], 16 * (q // 2))
                for j in range(CP):
                    p = q * CP + j
                    nc.vector.scalar_tensor_tensor(ha[:, s, j, :], yy[:, s, 0, j, :], pw[:, 0, p:p + 1], h3_all[:, p, :], ALU.mult, ALU.add).then_inc(s_a, 1)
                for j in range(CP):
                    p = q * CP + j
                    dve.wait_ge(s_a, 2 * CP * q + j + 1)
                    nc.vector.scalar_tensor_tensor(ho[:, s, j, :], yy[:, s, 1, j, :], pw2[:, p:p + 1], ha[:, s, j, :], ALU.mult, ALU.add).then_inc(s_a, 1)


def bass_audio_tower_kernel(nc, x, small, e_w, e_i, w1, w2, wg, wu, wd_, bg, bu, bd, out):
    def dram(name, shape, dt=F32):
        return nc.dram_tensor(name, shape, dt, kind="Internal").ap()

    h0, h1 = (dram(n, [TOK, D]) for n in ("h0", "h1"))
    dt_dram, a_dram = (dram(n, [B, T * 8]) for n in ("steps_dt", "steps_a"))
    xs_dram = dram("slots_x", [(EMPTY + 1) * SLOTS, XW])
    ys_dram = dram("results", [SPARE + K2 * TOK, D])
    bias_dram = dram("bias_parts", [E2, 3, WB], BF16)

    with ExitStack() as ctx:
        def sb(name, shape, dt=F32):
            return ctx.enter_context(nc.sbuf_tensor(name, shape, dt))

        s_pack, s_bias, s_w = (ctx.enter_context(nc.semaphore(n)) for n in ("s_pack", "s_bias", "s_w"))
        s_sent, s_back = ([ctx.enter_context(nc.semaphore(f"{n}{k}")) for k in range(4)] for n in ("s_sent", "s_back"))
        pk = sb("pk", [128, NPACK])
        wgu = sb("wgu", [D, E2, 2 * F2])
        wd = sb("wd", [128, E2, FC, D])
        slot_rows = sb("slot_rows", [1, 256 + E2], I32)
        base = sb("base", [128, E2])
        dm = sb("dm", [PT, NP])
        ssum = sb("ssum", [PT, NP])
        loads = [
            (lambda e: wgu[:, e, 0:F2], lambda e: wg[e].rearrange("o d f -> d o f"), s_w),
            (lambda e: wgu[:, e, F2:2 * F2], lambda e: wu[e].rearrange("o d f -> d o f"), s_w),
            (lambda e: wd[:, e].rearrange("p o c d -> p (o c) d"), lambda e: wd_[e].rearrange("o (c p) d -> p (o c) d", p=128), s_w),
        ]
        with nc.sbuf_tensor("u_t", [D, TOK], F32) as u_t:
            stage_patches(nc, x, u_t[:], dt_dram, a_dram, h0, pk, s_pack, small)
            stage_mamba(nc, u_t[:], pk, dt_dram, a_dram, h0, h1, loads)
        stage_ffn(nc, pk, h1, e_w, e_i, w1, w2)
        with nc.sbuf_tensor("h3_all", [PT, NP, D], F32) as h3_all:
            stage_attention(nc, pk, h1, h3_all[:], xs_dram, base[:], dm[:], ssum[:], s_sent)
            stage_plan(nc, pk, base[:], slot_rows, (bg, bu, bd), bias_dram, xs_dram, s_bias)
            stage_experts(nc, pk, h3_all[:], slot_rows, dm[:], ssum[:], wgu[:], wd[:], bias_dram, xs_dram, ys_dram,
                          out.rearrange("b t d -> (b t) d"), s_w, 16 * len(loads) * NQ, s_back)
def pack(i):
    f = np.float32
    r = np.arange(PT); b, t = r // T, r % T
    same = b[:, None] == b[None]
    tt = np.arange(T)
    p = {}
    p["ident"] = np.eye(128)
    p["later_f"] = same & (t[:, None] > t[None]); p["later_b"] = same & (t[:, None] < t[None])
    p["upto_f"] = t[:, None] <= tt[None]; p["upto_b"] = t[:, None] >= tt[None]
    p["gmask_f"] = 0.25 * (same & (t[:, None] <= t[None])); p["gmask_b"] = 0.25 * (same & (t[:, None] >= t[None]))
    p["amask"] = same & (t[:, None] < t[None])
    p["tri"] = r[:, None] < r[None]
    p["iota32"] = np.broadcast_to(np.arange(32), (128, 32))
    token = SPARE + np.arange(NP)[None, :] * PT + r[:, None]
    p["tokid"] = np.stack([token, token + TOK], 1).reshape(PT, 2 * NP)
    p["block0"] = np.broadcast_to(np.arange(128) * SLOTS, (128, 128))
    p["bcol"] = np.arange(128)[:, None]
    p["ones"] = np.ones((128, 2)); p["onem"] = np.ones((128, 128))
    p["tokw"] = i["L0_tok_W"].reshape(64, 2, 8, 128).transpose(1, 2, 0, 3).reshape(8, 128, 128).transpose(1, 0, 2).reshape(128, 1024)
    p["tokb"] = i["L0_tok_b"][:, None]
    row = lambda a: np.broadcast_to(a[None], (128, a.size))
    p["gamma"] = row(i["L0_tok_gamma"]); p["beta"] = row(i["L0_tok_beta"])
    m = lambda d, n: np.asarray(i[f"L0_attn_{d}_{n}"])
    wi = {d: m(d, "in_proj_w") for d in ("fwd", "bwd")}
    both = lambda n: np.concatenate([m("fwd", n), m("bwd", n)])
    p["wdt"] = np.concatenate([wi["fwd"][544:], wi["bwd"][544:]]).T
    p["dtb"] = row(both("dt_bias")); p["alog"] = row(both("A_log"))
    p["wz"] = np.concatenate([wi["fwd"][:256], wi["bwd"][:256]]).T
    def tiles(a):
        n = a["fwd"].shape[1]
        bc = np.zeros((128, n), f)
        bc[0:16], bc[32:48], bc[64:80], bc[96:112] = a["fwd"][256:272], a["fwd"][272:], a["bwd"][256:272], a["bwd"][272:]
        return [a["fwd"][:128], a["fwd"][128:256], a["bwd"][:128], a["bwd"][128:256], bc]
    p["wx"] = np.concatenate([w.T for w in tiles({d: wi[d][256:544] for d in wi})], 1)
    p["cw"] = np.stack(tiles({d: m(d, "conv_w")[:, 0] for d in wi}), 1).reshape(128, 20)
    p["cb"] = np.stack(tiles({d: m(d, "conv_b")[:, None] for d in wi}), 1).reshape(128, 5)
    p["dcol"] = np.repeat(both("Dp"), 64).reshape(4, 128).T
    p["wo"] = np.concatenate([m("fwd", "out_proj_w"), m("bwd", "out_proj_w")], 1).T.reshape(4, 128, 128).transpose(1, 0, 2).reshape(128, 512)
    p["nw"] = both("norm_w").reshape(4, 128).T
    p["wq"], p["wk"], p["wv"] = i["L1_attn_Wq"], i["L1_attn_Wv"], i["L1_attn_Wk"]
    p["wgate"] = i["L1_ffn_Wgate"]; p["bgate"] = row(i["L1_ffn_bgate"])
    out = np.zeros((128, NPACK), f)
    for n, a in p.items():
        c = COLS[n]; a = np.asarray(a); out[:a.shape[0], c[0]:c[1]] = a
    return out


_L = "L1_ffn_"
_AS_THEY_ARE = ["L0_ffn_expert_weights", "L0_ffn_expert_indices", "L0_ffn_w1", "L0_ffn_w2",
                _L + "Wg", _L + "Wu", _L + "Wd", _L + "bg", _L + "bu", _L + "bd"]


def kernel(**inputs):
    import concourse.bacc as bacc
    from concourse.bass_utils import run_bass_kernel_spmd as run

    nc = bacc.Bacc("TRN2", target_bir_lowering=False, num_devices=1)
    arrays, args = {}, []
    given = {n: np.ascontiguousarray(a) for n, a in inputs.items()}
    for name, a in [("x", given["x"]), ("small", pack(given))] + [(n, given[n]) for n in _AS_THEY_ARE]:
        arrays[f"in_{name}"] = a
        args.append(nc.dram_tensor(f"in_{name}", a.shape, mybir.dt.from_np(a.dtype), kind="ExternalInput").ap())
    out = nc.dram_tensor("out", (B, T, D), F32, kind="ExternalOutput").ap()
    bass_audio_tower_kernel(nc, *args, out)
    return run(nc, [arrays], core_ids=[0]).results[0]["out"]
```

```python
import concourse.bass as bass
from concourse import mybir
from contextlib import ExitStack
import numpy as np

F32 = mybir.dt.float32
BF16 = mybir.dt.bfloat16
I32 = mybir.dt.int32
U32 = mybir.dt.uint32
ALU = mybir.AluOpType
ACT = mybir.ActivationFunctionType
AX_X = mybir.AxisListType.X

B, CH = 128, 64
BLK = 8
T = 45
NBLK = T + 1
FB = BLK * CH
D = 128
TOK = B * T
PT = 2 * T
NP = B // 2
QT = 2 * PT
NQ = B // 4
NH, HD, NS = 4, 64, 16
DI = NH * HD
EPS = 1e-5
LONGEST_DECAY = -200.0

PACK = dict(
    ident=128, later_f=PT, later_b=PT, upto_f=T, upto_b=T, gmask_f=PT, gmask_b=PT, amask=PT, tri=PT,
    iota32=32, tokw=8 * 128, tokb=1, gamma=128, beta=128, wdt=8, dtb=8, alog=8,
    wz=512, wx=5 * 128, cw=20, cb=5, dcol=4, wo=4 * 128, nw=4, wq=128, wk=128, wv=128,
    wgate=32, bgate=32, ones=2, onem=128, bcol=1, tokid=4 * NQ, block0=128,
)


def columns():
    at, out = 0, {}
    for name, n in PACK.items():
        out[name] = (at, at + n)
        at += n
    return out, at


COLS, NPACK = columns()




def at_least(eng, sem, value):
    if not isinstance(value, int) or value > 0:
        eng.wait_ge(sem, value)


def turns(eng, count, body):
    body(0)
    with eng.Fori(1, count) as i:
        body(i)


def wait_apart(eng, sem, value, passed):
    eng.wait_ge(sem, value)
    eng.sem_inc(passed, 1)


def stage_patches(nc, x, u_t, dt_dram, a_dram, h_dram, sb_pack, s_pack, load_pack):
    with ExitStack() as ctx:
        def sb(name, shape, dt=F32):
            return ctx.enter_context(nc.sbuf_tensor("pa_" + name, shape, dt))

        def sem(name):
            return ctx.enter_context(nc.semaphore("pa_" + name))

        def cst(name):
            return sb_pack[:, COLS[name][0]:COLS[name][1]]

        xin = sb("xin", [B, 4, FB])
        xt = sb("xt", [128, 4, 4, B])
        yt = sb("yt", [D, 2, B])
        st6 = sb("st6", [B, 2, 2, 6])
        mv = sb("mv", [B, 2, 2, 2])
        ve = sb("ve", [B, 2, 2])
        rs = sb("rs", [B, 2, 2])
        mhalf = sb("mhalf", [B, 2])
        yn = sb("yn", [B, 2, D])
        yg = sb("yg", [B, 2, D])
        hh = sb("hh", [B, 2, D])
        uu = sb("uu", [B, 2, D])
        uc = sb("uc", [D, 2, B])
        xdt = sb("xdt", [B, T, 8])
        n8 = T * 8
        e, w, sl, t1 = (sb(n, [B, n8]) for n in ("e", "w", "sl", "t1"))
        al = sb("al", [B, 8])
        dtv, av = (sb(n, [B, T, 8]) for n in ("dtv", "av"))
        xf = xdt[:].rearrange("b t e -> b (t e)")
        psx = [ctx.enter_context(nc.psum_tensor(f"pa_psx{k}", [128, 4, B], F32)) for k in range(2)]
        psy = [ctx.enter_context(nc.psum_tensor(f"pa_psy{k}", [D, 512], F32)) for k in range(2)]
        pst = [ctx.enter_context(nc.psum_tensor(f"pa_pst{k}", [B, 512], F32)) for k in range(2)]
        psu = ctx.enter_context(nc.psum_tensor("pa_psu", [D, 512], F32))
        psd = ctx.enter_context(nc.psum_tensor("pa_psd", [B, 512], F32))

        s_in = [sem(f"in{k}") for k in range(4)]
        s_xtp = sem("xtp")
        s_xt = sem("xt")
        s_y = sem("y")
        s_yt = sem("yt")
        s_ty = sem("ty")
        s_n = [sem("n1"), sem("n2")]
        s_ve = sem("ve")
        s_r = sem("r")
        s_yn, s_yg, s_hh, s_uu = (sem(n) for n in ("yn", "yg", "hh", "uu"))
        s_tu = sem("tu")
        s_uc = sem("uc")
        s_ut = sem("ut")
        s_dt = sem("dt")
        s_dtv = sem("dtv")
        s_wv = sem("wv")
        s_mh = sem("mh")
        s_h = [sem(f"h{k}") for k in range(2)]
        s_c = sem("c")
        s_sc = sem("sc")
        s_out = sem("out")

        block = ctx.enter_context(nc.Block())

        FIRST = 8
        TURNS = (NBLK - 5 - FIRST) // 4
        LAST = T + 7

        def steps(eng, step):
            def one(p):
                step(p, p % 4, lambda k: 0 <= p - k < T, lambda k: p + k < NBLK)

            for p in range(FIRST):
                one(p)
            with eng.Fori(0, TURNS) as i:
                for r in range(4):
                    step(4 * i + FIRST + r, r, lambda k: True, lambda k: True)
            for p in range(FIRST + 4 * TURNS, LAST):
                one(p)

        hv = h_dram.rearrange("(b t) d -> b t d", t=T)

        @block.sync
        def _(sp):
            def load_block(b, r):
                src = x[:, b * BLK:(b + 1) * BLK, :] if isinstance(b, int) else x[:, bass.ds(b * BLK, BLK), :]
                sp.dma_start(xin[:, r, :], src.rearrange("b l c -> b (l c)")).then_inc(s_in[r], 16)

            def step(p, r, live, more):
                s = r % 2
                if more(5):
                    at_least(sp, s_xtp, p + 2)
                    load_block(p + 5, (r + 1) % 4)
                if live(2):
                    q = p - 2
                    sp.wait_ge(s_hh, q + 1)
                    dst = hv[:, q, :] if isinstance(q, int) else hv[:, bass.ds(q, 1), :].rearrange("b o d -> b (o d)")
                    sp.dma_start(dst, hh[:, s, :]).then_inc(s_h[s], 16)

            load_block(0, 0)
            sp.dma_start(sb_pack[:], load_pack).then_inc(s_pack, 16)
            for b in range(1, 4):
                load_block(b, b)
            sp.wait_ge(s_xtp, 1)
            load_block(4, 0)
            steps(sp, step)
            sp.wait_ge(s_c, 1 + 1 + 2 + 6 + 3 + 1)
            sp.dma_start(dt_dram, dtv[:].rearrange("b t e -> b (t e)")).then_inc(s_out, 16)
            sp.wait_ge(s_c, 1 + 1 + 2 + 6 + 3 + 1 + 2)
            sp.dma_start(a_dram, av[:].rearrange("b t e -> b (t e)")).then_inc(s_out, 16)
            sp.wait_ge(s_out, 32)
            sp.wait_ge(s_h[0], 16 * ((T + 1) // 2))
            sp.wait_ge(s_h[1], 16 * (T // 2))

        @block.tensor
        def _(pe):
            def transpose_block(b, r):
                pe.wait_ge(s_in[r], 16 * (((b - r) >> 2) + 1))
                at_least(pe, s_xt, b - 1)
                for c in range(4):
                    last = nc.tensor.transpose(psx[r % 2][:, c, :], xin[:, r, c * 128:(c + 1) * 128], cst("ident"))
                last.then_inc(s_xtp, 1)

            def step(p, r, live, more):
                s = r % 2
                if live(0):
                    pe.wait_ge(s_xt, p + 2)
                    at_least(pe, s_yt, p - 1)
                    w = cst("tokw").rearrange("p (k d) -> p k d", k=8)
                    for k in range(8):
                        last = nc.tensor.matmul(psy[s][:, 0:B], w[:, k, :], xt[:, (r + k // 4) % 4, k % 4, :], start=(k == 0), stop=(k == 7))
                    last.then_inc(s_y, 1)
                if more(3):
                    transpose_block(p + 3, (r + 3) % 4)
                if live(1):
                    q = p - 1
                    pe.wait_ge(s_yt, q + 1)
                    at_least(pe, s_yn, q - 1)
                    nc.tensor.transpose(pst[1 - s][:, 0:D], yt[:, 1 - s, :], cst("ident")).then_inc(s_ty, 1)
                if live(5):
                    q = p - 5
                    pe.wait_ge(s_uu, q + 1)
                    at_least(pe, s_uc, q)
                    nc.tensor.transpose(psu[:, 0:B], uu[:, 1 - s, :], cst("ident")).then_inc(s_tu, 1)
                if live(6):
                    q = p - 6
                    pe.wait_ge(s_uc, q + 1)
                    at_least(pe, s_dtv, q)
                    nc.tensor.matmul(psd[:, 0:8], uc[:, s, :], cst("wdt"), start=True, stop=True).then_inc(s_dt, 1)

            pe.wait_ge(s_pack, 16)
            transpose_block(0, 0)
            transpose_block(1, 1)
            transpose_block(2, 2)
            steps(pe, step)

        @block.scalar
        def _(act):
            def evacuate(b, r):
                act.wait_ge(s_xtp, b + 1)
                at_least(act, s_y, b - 3)
                nc.scalar.activation(xt[:, r, :, :], psx[r % 2][:], ACT.Copy).then_inc(s_xt, 1)

            def step(p, r, live, more):
                s = r % 2
                if live(0):
                    act.wait_ge(s_y, p + 1)
                    at_least(act, s_ty, p - 1)
                    nc.scalar.activation(yt[:, s, :], psy[s][:, 0:B], ACT.Identity, bias=cst("tokb")).then_inc(s_yt, 1)
                if more(3):
                    evacuate(p + 3, (r + 3) % 4)
                if live(5):
                    q = p - 5
                    act.wait_ge(s_tu, q + 1)
                    at_least(act, s_dt, q - 1)
                    at_least(act, s_ut, q - 1)
                    nc.scalar.activation(uc[:, 1 - s, :], psu[:, 0:B], ACT.Copy).then_inc(s_uc, 1)

            act.wait_ge(s_pack, 16)
            evacuate(0, 0)
            evacuate(1, 1)
            evacuate(2, 2)
            steps(act, step)
            act.wait_ge(s_c, 2)
            nc.scalar.activation(e[:], t1[:], ACT.Exp, scale=-1.0).then_inc(s_sc, 1)
            nc.scalar.activation(al[:], al[:], ACT.Exp).then_inc(s_sc, 1)
            act.wait_ge(s_c, 3)
            nc.scalar.activation(w[:], w[:], ACT.Ln).then_inc(s_sc, 1)

        @block.vector
        def _(dve):
            def step(p, r, live, more):
                s = r % 2
                if live(7):
                    q = p - 7
                    dve.wait_ge(s_dt, q + 1)
                    out = xdt[:, q, :] if isinstance(q, int) else xdt[:, bass.ds(q, 1), :].rearrange("b o e -> b (o e)")
                    nc.vector.tensor_tensor(out, psd[:, 0:8], cst("dtb"), ALU.add).then_inc(s_dtv, 1)
                if live(3):
                    dve.wait_ge(s_hh, p - 2)
                    nc.vector.bn_stats(st6[:, 1 - s, 1, :], hh[:, 1 - s, :]).then_inc(s_n[1], 1)
                if live(1):
                    wait_apart(dve, s_ty, p, s_wv)
                    nc.vector.bn_stats(st6[:, 1 - s, 0, :], pst[1 - s][:, 0:D]).then_inc(s_n[0], 1)
                if live(2):
                    dve.wait_ge(s_r, p - 1)
                    nc.vector.tensor_scalar(yn[:, s, :], pst[s][:, 0:D], mv[:, s, 0, 0:1], rs[:, s, 0:1], ALU.subtract, ALU.mult).then_inc(s_yn, 1)
                if live(4):
                    if not live(2):
                        dve.wait_ge(s_r, p - 1)
                    at_least(dve, s_tu, p - 5)
                    nc.vector.tensor_scalar(uu[:, s, :], hh[:, s, :], mv[:, s, 1, 0:1], rs[:, s, 1:2], ALU.subtract, ALU.mult).then_inc(s_uu, 1)
                if live(3):
                    wait_apart(dve, s_n[1], 2 * (p - 3) + 1, s_wv)
                    nc.vector.bn_aggr(mv[:, 1 - s, 1, :], st6[:, 1 - s, 1, :]).then_inc(s_n[1], 1)
                if live(2):
                    dve.wait_ge(s_yn, p - 1)
                    nc.vector.tensor_tensor(yg[:, s, :], yn[:, s, :], cst("gamma"), ALU.mult).then_inc(s_yg, 1)
                if live(1):
                    wait_apart(dve, s_n[0], 2 * (p - 1) + 1, s_wv)
                    nc.vector.bn_aggr(mv[:, 1 - s, 0, :], st6[:, 1 - s, 0, :]).then_inc(s_n[0], 1)
                if live(1) or live(3):
                    norms = slice(0 if live(1) else 1, 2 if live(3) else 1)
                    if live(1):
                        dve.wait_ge(s_n[0], 2 * p)
                    if live(3):
                        dve.wait_ge(s_n[1], 2 * p - 4)
                    at_least(dve, s_r, p - 2)
                    nc.vector.tensor_scalar(ve[:, 1 - s, norms], mv[:, 1 - s, norms, 1], EPS, None, ALU.add).then_inc(s_ve, 1)
                if live(2):
                    dve.wait_ge(s_yg, p - 1)
                    at_least(dve, s_uu, p - 3)
                    at_least(dve, s_h[s], 16 * ((p - 2 - s) >> 1))
                    nc.vector.tensor_tensor(hh[:, s, :], yg[:, s, :], cst("beta"), ALU.add).then_inc(s_hh, 1)
                elif live(4):
                    dve.wait_ge(s_uu, p - 3)

            dve.wait_ge(s_pack, 16)
            nc.vector.tensor_scalar(al[:], cst("alog"), 88.0, None, ALU.min).then_inc(s_c, 1)
            steps(dve, step)
            c = [1]

            def then(ins):
                ins.then_inc(s_c, 1)
                c[0] += 1
                dve.wait_ge(s_c, c[0])

            dve.wait_ge(s_dtv, T)
            then(nc.vector.scalar_tensor_tensor(t1[:], xf, -1.0, xf, ALU.mult, ALU.max))
            dve.wait_ge(s_sc, 2)
            then(nc.vector.tensor_scalar(w[:], e[:], 1.0, None, ALU.add))
            then(nc.vector.tensor_scalar(sl[:], e[:], 1.0 / 7.0, None, ALU.mult))
            for coef in (-1.0 / 6.0, 1.0 / 5.0, -1.0 / 4.0, 1.0 / 3.0, -1.0 / 2.0, 1.0):
                then(nc.vector.scalar_tensor_tensor(sl[:], sl[:], coef, e[:], ALU.add, ALU.mult))
            dve.wait_ge(s_sc, 3)
            then(nc.vector.tensor_tensor(w[:], w[:], sl[:], ALU.subtract))
            then(nc.vector.scalar_tensor_tensor(w[:], e[:], 0.0625, w[:], ALU.is_gt, ALU.mult))
            then(nc.vector.tensor_tensor(sl[:], sl[:], w[:], ALU.add))
            dt_flat = dtv[:].rearrange("b t e -> b (t e)")
            then(nc.vector.scalar_tensor_tensor(dt_flat, xf, 0.0, sl[:], ALU.max, ALU.add))
            then(nc.vector.scalar_tensor_tensor(av[:], dtv[:], -1.0, al[:].unsqueeze(1).broadcast_to([B, T, 8]), ALU.mult, ALU.mult))
            avf = av[:].rearrange("b t e -> b (t e)")
            then(nc.vector.tensor_scalar(avf, avf, LONGEST_DECAY, None, ALU.max))

        @block.gpsimd
        def _(pool):
            def step(p, r, live, more):
                s = r % 2
                if live(1) or live(3):
                    norms = slice(0 if live(1) else 1, 2 if live(3) else 1)
                    pool.wait_ge(s_ve, p)
                    at_least(pool, s_yn, min(p - 2, T) if isinstance(p, int) else p - 2)
                    at_least(pool, s_uu, p - 4)
                    nc.gpsimd.tensor_tensor(rs[:, 1 - s, norms], ve[:, 1 - s, norms], mhalf[:, norms], ALU.pow).then_inc(s_r, 1)
                if live(6):
                    q = p - 6
                    pool.wait_ge(s_uc, q + 1)
                    out = u_t.rearrange("d (b t) -> d b t", t=T)
                    out = out[:, :, q] if isinstance(q, int) else out[:, :, bass.ds(q, 1)].rearrange("d b o -> d (b o)")
                    nc.gpsimd.tensor_copy(out, uc[:, s, :]).then_inc(s_ut, 1)

            nc.gpsimd.memset(mhalf[:], -0.5).then_inc(s_mh, 1)
            pool.wait_ge(s_mh, 1)
            steps(pool, step)
            pool.wait_ge(s_ut, T)


def stage_mamba(nc, u_t, pk, dt_dram, a_dram, h_dram, h1_dram, loads=()):
    with ExitStack() as ctx:
        def sb(name, shape, dt=F32):
            return ctx.enter_context(nc.sbuf_tensor("mb_" + name, shape, dt))

        def ps(name):
            return ctx.enter_context(nc.psum_tensor("mb_" + name, [128, 512], F32))

        def sem(name):
            return ctx.enter_context(nc.semaphore("mb_" + name))

        def cst(name, parts=128):
            return pk[0:parts, COLS[name][0]:COLS[name][1]]

        acc = sb("acc", [128, 2, 5, QT])
        xs = sb("xs", [128, 2, 4, QT])
        bcs = sb("bcs", [NS, 2, 4, QT])
        gz = sb("gz", [128, 2, 4, QT])
        dta = sb("dta", [PT, NP, 8])
        aa = sb("aa", [PT, NP, 8])
        a2 = sb("a2", [PT, 2, 2, 2, NH, T])
        ee = sb("ee", [PT, 2, 2, NH, T])
        gm = sb("gm", [PT, 2, 2, PT])
        tt = sb("tt", [PT, 2, 2, NH, PT])
        xd = sb("xd", [PT, 2, 8, HD])
        yv = sb("yv", [128, 4, QT])
        yg = sb("yg", [128, 2, 4, QT])
        sq = sb("sq", [128, 2, 4, QT])
        hq = sb("hq", [PT, 2, 2, D])
        ho = sb("ho", [PT, 2, 2, D])
        hm = sb("hm", [PT, 2, D])
        var = sb("var", [PT, 2, 2])
        rr = sb("rr", [PT, 2, 2])
        mhalf = sb("mhalf", [PT, 2])
        won = sb("won", [128, 4, D])
        psx = [ps("psx0"), ps("psx1")]
        psz, pss, pst, psg = ps("psz"), ps("pss"), ps("pst"), ps("psg")
        psy = [ps("psy0"), ps("psy1")]

        s_ld, s_k, s_mh = sem("ld"), sem("k"), sem("mh")
        s_xp = sem("xp")
        s_zp = sem("zp")
        s_t0 = sem("t0")
        s_dc = sem("dc")
        s_si = sem("si")
        s_gz = sem("gz")
        s_a2 = sem("a2")
        s_s = sem("s")
        s_e = sem("e")
        s_g = sem("g")
        s_gm = sem("gm")
        s_tt = sem("tt")
        s_xt = sem("xt")
        s_xd = sem("xd")
        s_y = sem("y")
        s_yv = sem("yv")
        s_yg = sem("yg")
        s_sq = sem("sq")
        s_o = sem("o")
        s_va = sem("va")
        s_rr = sem("rr")
        s_h = sem("h")
        s_hq = [sem("hq0"), sem("hq1")]
        s_st = [sem("st0"), sem("st1")]

        block = ctx.enter_context(nc.Block())

        FIRST = 6

        def steps(eng, turn):
            for t in range(FIRST):
                turn(t, t % 2, lambda k, t=t: 0 <= t - k < NQ)
            with eng.Fori(0, (NQ - FIRST) // 2) as i:
                for s in range(2):
                    turn(2 * i + FIRST + s, s, lambda k: True)
            for t in range(NQ, NQ + 3):
                turn(t, t % 2, lambda k, t=t: 0 <= t - k < NQ)

        def half(n, s):
            return (n - s) // 2 if isinstance(n, int) else (n - s) >> 1

        def rows(dram, n):
            v = dram.rearrange("(n j r) d -> n r j d", j=2, r=PT)
            return v[n] if isinstance(n, int) else v[bass.ds(n, 1)].rearrange("o r j d -> (o r) j d")

        flat = lambda a: a.rearrange("p k q -> p (k q)")
        GROUPS = ((0, 1), (2, 3), (4,))
        pair_cols = lambda j: slice(j * PT, (j + 1) * PT)

        @block.sync
        def _(sp):
            v = lambda a: a.rearrange("b (t e) -> (b t) e", e=8).rearrange("(p r) e -> r p e", r=PT)
            sp.dma_start(dta[:], v(dt_dram)).then_inc(s_ld, 16)
            sp.dma_start(aa[:], v(a_dram)).then_inc(s_ld, 16)

            def turn(t, s, live):
                if live(2):
                    n = t - 2
                    at_least(sp, s_h, 4 * n - 4)
                    sp.dma_start(hq[:, s], rows(h_dram, n)).then_inc(s_hq[s], 16)
                if live(0):
                    for dst, src, s_load in loads:
                        at = slice(t, t + 1) if isinstance(t, int) else bass.ds(t, 1)
                        sp.dma_start(dst(at), src(at)).then_inc(s_load, 16)
                if live(3):
                    n = t - 3
                    sp.wait_ge(s_h, 4 * n + 4)
                    sp.dma_start(rows(h1_dram, n), ho[:, 1 - s]).then_inc(s_st[1 - s], 16)

            steps(sp, turn)
            for s in range(2):
                sp.wait_ge(s_st[s], 16 * (NQ // 2))

        @block.tensor
        def _(pe):
            pe.wait_ge(s_k, 4)

            def in_proj(n, s, g):
                bank = psx[(3 * s + g) % 2]
                at_least(pe, s_dc, 18 * n + 6 * (g - 1))
                u = u_t[:, n * QT:(n + 1) * QT] if isinstance(n, int) else u_t[:, bass.ds(n * QT, QT)]
                for k in GROUPS[g]:
                    last = nc.tensor.matmul(bank[:, (k % 2) * QT:(k % 2 + 1) * QT], cst("wx")[:, k * 128:(k + 1) * 128],
                                            u, start=True, stop=True)
                last.then_inc(s_xp, 1)

            def in_proj_z(n, d):
                at_least(pe, s_gz, 2 * n + d)
                u = u_t[:, n * QT:(n + 1) * QT] if isinstance(n, int) else u_t[:, bass.ds(n * QT, QT)]
                for k in (2 * d, 2 * d + 1):
                    last = nc.tensor.matmul(psz[:, (k % 2) * QT:(k % 2 + 1) * QT], cst("wz")[:, k * 128:(k + 1) * 128],
                                            u, start=True, stop=True)
                last.then_inc(s_zp, 1)

            def exponents(n, s, j):
                m = 2 * n + j
                pe.wait_ge(s_a2, 2 * m + 2)
                at_least(pe, s_e, m)
                for d in range(2):
                    last = nc.tensor.matmul(pss[0:PT, d * 180:(d + 1) * 180], cst(("later_f", "later_b")[d], PT),
                                            a2[:, s, j, d].rearrange("k h i -> k (h i)"), start=True, stop=True)
                last.then_inc(s_s, 1)

            def transpose_x(n, s, j):
                m = 2 * n + j
                pe.wait_ge(s_si, 6 * n + 2)
                at_least(pe, s_xd, m)
                for k in range(4):
                    last = nc.tensor.transpose(pst[0:PT, k * 128:(k + 1) * 128], xs[:, s, k, pair_cols(j)], cst("ident"))
                last.then_inc(s_xt, 1)

            def b_times_c(n, s):
                pe.wait_ge(s_si, 6 * n + 6)
                at_least(pe, s_gm, n)
                at_least(pe, s_h, 4 * n - 4)
                for j in range(2):
                    for d in range(2):
                        c = pair_cols(j)
                        last = nc.tensor.matmul(psg[0:PT, (2 * j + d) * PT:(2 * j + d + 1) * PT], bcs[:, s, 2 * d, c], bcs[:, s, 2 * d + 1, c],
                                                start=True, stop=True)
                last.then_inc(s_g, 1)

            def scan(n, j):
                m = 2 * n + j
                if j == 0:
                    at_least(pe, s_yv, 4 * n)
                pe.wait_ge(s_tt, 2 * m + 2)
                pe.wait_ge(s_xd, m + 1)
                for e in range(8):
                    k = e // 2
                    last = nc.tensor.matmul(psy[k // 2][64 * (e % 2):64 * (e % 2) + 64, (k % 2) * QT + j * PT:(k % 2) * QT + (j + 1) * PT],
                                            xd[:, j, e, :], tt[:, j, e // 4, e % 4, :], start=True, stop=True)
                last.then_inc(s_y, 1)

            def out_proj(n, s, j, g_done):
                m = 2 * n + j
                c = pair_cols(j)
                pe.wait_ge(s_yg, n + 1)
                pe.wait_ge(s_sq, n + 1)
                at_least(pe, s_h, 2 * m)
                at_least(pe, s_gm, g_done)
                for d in range(2):
                    for k in (2 * d, 2 * d + 1):
                        nc.tensor.matmul(psg[0:PT, d * D:(d + 1) * D], yg[:, s, k, c], won[:, k, :],
                                         start=(k % 2 == 0), stop=(k % 2 == 1))
                    for k in (2 * d, 2 * d + 1):
                        last = nc.tensor.matmul(psg[0:PT, 2 * D + 2 * d:2 * D + 2 + 2 * d], sq[:, s, k, c], cst("ones"),
                                                start=(k % 2 == 0), stop=(k % 2 == 1))
                last.then_inc(s_o, 1)

            def turn(t, s, live):
                masked = min(t - 1, NQ) if isinstance(t, int) else t - 1
                if live(0):
                    in_proj(t, s, 0)
                if live(3):
                    out_proj(t - 3, 1 - s, 0, masked)
                if live(1):
                    exponents(t - 1, 1 - s, 0)
                if live(2):
                    scan(t - 2, 0)
                    scan(t - 2, 1)
                if live(0):
                    in_proj(t, s, 1)
                if live(1):
                    exponents(t - 1, 1 - s, 1)
                    transpose_x(t - 1, 1 - s, 0)
                if live(3):
                    out_proj(t - 3, 1 - s, 1, masked)
                if live(1):
                    transpose_x(t - 1, 1 - s, 1)
                if live(0):
                    in_proj_z(t, 0)
                if live(1):
                    b_times_c(t - 1, 1 - s)
                if live(0):
                    in_proj(t, s, 2)
                    in_proj_z(t, 1)

            steps(pe, turn)

        @block.scalar
        def _(act):
            def first_tap(n, s, g):
                act.wait_ge(s_xp, 3 * n + g + 1)
                at_least(act, s_si, 6 * n - 6)
                for k in GROUPS[g]:
                    nc.scalar.activation(acc[:, s, k, :], psx[(3 * s + g) % 2][:, (k % 2) * QT:(k % 2 + 1) * QT], ACT.Identity,
                                         bias=cst("cb")[:, k:k + 1], scale=cst("cw")[:, 4 * k + 3:4 * k + 4]).then_inc(s_t0, 1)

            def silu_z(n, s, d):
                act.wait_ge(s_zp, 2 * n + d + 1)
                at_least(act, s_yg, n - 1)
                nc.scalar.activation(flat(gz[:, s, 2 * d:2 * d + 2]), psz[:, 0:2 * QT], ACT.Silu).then_inc(s_gz, 1)

            def silu_x(n, s, g):
                act.wait_ge(s_dc, 18 * n + 6 * (g + 1))
                if g < 2:
                    at_least(act, s_yv, 4 * n - 4)
                    at_least(act, s_xt, 2 * n - 2)
                    lo, hi = GROUPS[g][0], GROUPS[g][-1] + 1
                    nc.scalar.activation(flat(xs[:, s, lo:hi, :]), flat(acc[:, s, lo:hi, :]), ACT.Silu).then_inc(s_si, 1)
                else:
                    at_least(act, s_g, n - 1)
                    for e in range(4):
                        nc.scalar.activation(bcs[:, s, e, :], acc[32 * e:32 * e + NS, s, 4, :], ACT.Silu).then_inc(s_si, 1)

            def decays(n, j):
                m = 2 * n + j
                act.wait_ge(s_s, m + 1)
                at_least(act, s_tt, 2 * m - 2)
                nc.scalar.activation(ee[:, j].rearrange("k d h i -> k (d h i)"), pss[0:PT, 0:360], ACT.Exp).then_inc(s_e, 1)

            def gate_squares(n, s):
                act.wait_ge(s_yg, n + 1)
                at_least(act, s_o, 2 * n - 2)
                nc.scalar.activation(flat(sq[:, s]), flat(yg[:, s]), ACT.Square).then_inc(s_sq, 1)

            def turn(t, s, live):
                if live(0):
                    first_tap(t, s, 0)
                if live(1):
                    decays(t - 1, 0)
                    decays(t - 1, 1)
                    silu_x(t - 1, 1 - s, 2)
                if live(0):
                    first_tap(t, s, 1)
                    silu_z(t, s, 0)
                    silu_x(t, s, 0)
                    silu_x(t, s, 1)
                if live(2):
                    gate_squares(t - 2, s)
                if live(0):
                    first_tap(t, s, 2)
                    silu_z(t, s, 1)

            steps(act, turn)

        @block.vector
        def _(dve):
            for k in range(4):
                nc.vector.tensor_scalar(won[:, k, :], cst("wo")[:, k * D:(k + 1) * D], cst("nw")[:, k:k + 1], None, ALU.mult).then_inc(s_k, 1)
            dve.wait_ge(s_ld, 32)

            def taps(n, s, g):
                parts = ([(0, 0, 128, False), (1, 0, 128, False)], [(2, 0, 128, True), (3, 0, 128, True)],
                         [(4, 0, 64, False), (4, 64, 128, True)])[g]
                by_batch = lambda ap: ap.rearrange("p (b t) -> p b t", t=T)
                dve.wait_ge(s_t0, 5 * n + (2, 4, 5)[g])
                for back in (1, 2, 3):
                    for j, (k, lo, hi, rev) in enumerate(parts):
                        w = cst("cw")[lo:hi, 4 * k + 3 - back:4 * k + 4 - back]
                        x = by_batch(psx[(3 * s + g) % 2][lo:hi, (k % 2) * QT:(k % 2 + 1) * QT])
                        a = by_batch(acc[lo:hi, s, k, :])
                        x, a = (x[:, :, back:], a[:, :, :T - back]) if rev else (x[:, :, :T - back], a[:, :, back:])
                        if back > 1:
                            dve.wait_ge(s_dc, 18 * n + 6 * g + 2 * (back - 1) + j - 1)
                        nc.vector.scalar_tensor_tensor(a, x, w, a, ALU.mult, ALU.add).then_inc(s_dc, 1)

            def dt_times_x(n, j):
                m = 2 * n + j
                dve.wait_ge(s_xt, m + 1)
                at_least(dve, s_y, m - 1)
                steps_dt = dta[:, m, :] if isinstance(m, int) else dta[:, bass.ds(m, 1), :].rearrange("r o e -> r (o e)")
                nc.vector.tensor_tensor(xd[:, j], pst[0:PT, :].rearrange("r (e q) -> r e q", e=8),
                                        steps_dt.unsqueeze(2).broadcast_to([PT, 8, HD]), ALU.mult).then_inc(s_xd, 1)

            def mask(n):
                dve.wait_ge(s_g, n + 1)
                at_least(dve, s_tt, 4 * n)
                masks = pk[0:PT, COLS["gmask_f"][0]:COLS["gmask_b"][1]].unsqueeze(1).broadcast_to([PT, 2, 2 * PT])
                nc.vector.tensor_tensor(gm[:].rearrange("r j d i -> r j (d i)"), psg[0:PT, 0:4 * PT].rearrange("r (j e) -> r j e", j=2),
                                        masks, ALU.mult).then_inc(s_gm, 1)

            def skip(n, s):
                dve.wait_ge(s_y, 2 * n + 2)
                at_least(dve, s_yg, n)
                for k in range(4):
                    nc.vector.scalar_tensor_tensor(yv[:, k, :], xs[:, s, k, :], cst("dcol")[:, k:k + 1],
                                                   psy[k // 2][:, (k % 2) * QT:(k % 2 + 1) * QT], ALU.mult, ALU.add).then_inc(s_yv, 1)

            def mean_square(n, j):
                m = 2 * n + j
                dve.wait_ge(s_o, m + 1)
                at_least(dve, s_rr, m - 1)
                sums = psg[0:PT, 2 * D:2 * D + 4].rearrange("r (d o) -> r d o", o=2)[:, :, 0]
                nc.vector.tensor_scalar(var[:, j, :], sums, 1.0 / DI, EPS, ALU.mult, ALU.add).then_inc(s_va, 1)

            def residual(n, s, j):
                m = 2 * n + j
                dve.wait_ge(s_rr, m + 1)
                if j == 0:
                    dve.wait_ge(s_hq[s], 16 * (half(n, s) + 1))
                    at_least(dve, s_st[s], 16 * half(n, s))
                nc.vector.scalar_tensor_tensor(hm[:, j, :], psg[0:PT, 0:D], rr[:, j, 0:1], hq[:, s, j, :],
                                               ALU.mult, ALU.add).then_inc(s_h, 1)
                dve.wait_ge(s_h, 2 * m + 1)
                nc.vector.scalar_tensor_tensor(ho[:, s, j, :], psg[0:PT, D:2 * D], rr[:, j, 1:2], hm[:, j, :],
                                               ALU.mult, ALU.add).then_inc(s_h, 1)

            def turn(t, s, live):
                if live(0):
                    taps(t, s, 0)
                if live(3):
                    mean_square(t - 3, 0)
                if live(2):
                    skip(t - 2, s)
                if live(3):
                    residual(t - 3, 1 - s, 0)
                if live(1):
                    dt_times_x(t - 1, 0)
                if live(3):
                    mean_square(t - 3, 1)
                    residual(t - 3, 1 - s, 1)
                if live(0):
                    taps(t, s, 1)
                if live(1):
                    mask(t - 1)
                    dt_times_x(t - 1, 1)
                if live(0):
                    taps(t, s, 2)

            steps(dve, turn)

        @block.gpsimd
        def _(pool):
            nc.gpsimd.memset(mhalf[:], -0.5).then_inc(s_mh, 1)
            pool.wait_ge(s_mh, 1)
            pool.wait_ge(s_ld, 32)

            def spread(n, s, j):
                m = 2 * n + j
                at_least(pool, s_s, m - 3)
                for d in range(2):
                    upto = cst(("upto_f", "upto_b")[d], PT).unsqueeze(1).broadcast_to([PT, NH, T])
                    av = aa[:, m, 4 * d:4 * d + 4] if isinstance(m, int) else aa[:, bass.ds(m, 1), 4 * d:4 * d + 4].rearrange("r o e -> r (o e)")
                    nc.gpsimd.tensor_tensor(a2[:, s, j, d], upto, av.unsqueeze(2).broadcast_to([PT, NH, T]), ALU.mult).then_inc(s_a2, 1)

            def weigh(n, j):
                m = 2 * n + j
                pool.wait_ge(s_e, m + 1)
                pool.wait_ge(s_gm, n + 1)
                at_least(pool, s_y, m - 1)
                for d in range(2):
                    o = tt[:, j, d].rearrange("r h (b i) -> r h b i", b=2)
                    x = ee[:, j, d].unsqueeze(2).broadcast_to([PT, NH, 2, T])
                    g = gm[:, j, d].rearrange("r (b i) -> r b i", b=2).unsqueeze(1).broadcast_to([PT, NH, 2, T])
                    nc.gpsimd.tensor_tensor(o, x, g, ALU.mult).then_inc(s_tt, 1)

            def root(n, j):
                m = 2 * n + j
                pool.wait_ge(s_va, m + 1)
                at_least(pool, s_h, 2 * m - 2)
                nc.gpsimd.tensor_tensor(rr[:, j, :], var[:, j, :], mhalf[:], ALU.pow).then_inc(s_rr, 1)

            def gate(n, s):
                pool.wait_ge(s_yv, 4 * n + 4)
                at_least(pool, s_o, 2 * n - 2)
                at_least(pool, s_sq, n - 1)
                pool.wait_ge(s_gz, 2 * n + 2)
                nc.gpsimd.tensor_tensor(flat(yg[:, s]), flat(yv[:]), flat(gz[:, s]), ALU.mult).then_inc(s_yg, 1)

            def turn(t, s, live):
                if live(3):
                    root(t - 3, 0)
                if live(2):
                    gate(t - 2, s)
                if live(3):
                    root(t - 3, 1)
                if live(0):
                    spread(t, s, 0)
                    spread(t, s, 1)
                if live(1):
                    weigh(t - 1, 0)
                    weigh(t - 1, 1)

            steps(pool, turn)


FT = 1024
FR = 128
FP = FT // FR
FE, FF = 8, 512
FG = 4


def stage_ffn(nc, pk, h1_dram, ew, ei, w1, w2):
    with ExitStack() as ctx:
        def sb(name, shape, dt=F32):
            return ctx.enter_context(nc.sbuf_tensor("ff_" + name, shape, dt))

        def ps(name):
            return ctx.enter_context(nc.psum_tensor("ff_" + name, [128, 512], F32))

        def sem(name):
            return ctx.enter_context(nc.semaphore("ff_" + name))

        ident = pk[:, COLS["ident"][0]:COLS["ident"][1]]
        NG = FP // FG
        GT = FG * FR
        KC = FF // 128
        hacc = sb("hacc", [FR, FP, D])
        st = sb("st", [FR, FP, 6])
        mv = sb("mv", [FR, FP, 2])
        ve = sb("ve", [FR, FP])
        rs = sb("rs", [FR, FP])
        mhalf = sb("mhalf", [FR, FP])
        uu = sb("uu", [FR, FP, D])
        ut = sb("ut", [D, FP * FR])
        wt = sb("wt", [FR, FP, 2])
        ix = sb("ix", [FR, FP, 2], I32)
        xf = sb("xf", [FR, FP, 2])
        part = sb("part", [FR, FE, FP, 2])
        comb = sb("comb", [FR, FE, FP])
        w1s = sb("w1s", [D, 2, FF])
        w2s = sb("w2s", [128, 2, KC, D])
        ht = sb("ht", [128, 2, KC, GT])
        psh = [ps(f"psh{c}") for c in range(KC)]
        pso = [ps("pso0"), ps("pso1")]
        psu = ps("psu")

        s_ld, s_z = sem("ld"), sem("z")
        s_v, s_r, s_u = sem("v"), sem("r"), sem("u")
        s_tu, s_ut = sem("tu"), sem("ut")
        s_w = [sem("w0"), sem("w1")]
        s_cb = sem("cb")
        s_h = sem("h")
        s_g = sem("g")
        s_o = sem("o")
        s_a = sem("a")
        s_st = sem("st")
        block = ctx.enter_context(nc.Block())
        h_rows = h1_dram[0:FT, :].rearrange("(p r) d -> r p d", r=FR)
        UNITS = 2 * NG

        def units(eng, unit):
            def turn(i):
                for k in range(UNITS):
                    unit(eng, i, k)
            turns(eng, FE // 2, turn)

        @block.sync
        def _(sp):
            sp.dma_start(hacc[:], h_rows).then_inc(s_ld, 16)
            for dst, src in ((wt, ew), (ix, ei)):
                sp.dma_start(dst[:], src[0:FT, :].rearrange("(p r) k -> r p k", r=FR)).then_inc(s_ld, 16)

            def load(i):
                for s in range(2):
                    e = 2 * i + s
                    at_least(sp, s_o, NG * (e - 1))
                    sp.dma_start(w1s[:, s, :], w1[bass.ds(e, 1)].rearrange("o d f -> (o d) f")).then_inc(s_w[s], 16)
                    sp.dma_start(w2s[:, s], w2[bass.ds(e, 1)].rearrange("o (c p) d -> (o p) c d", p=128)).then_inc(s_w[s], 16)
            turns(sp, FE // 2, load)
            sp.wait_ge(s_a, FE * FP)
            sp.dma_start(h_rows, hacc[:]).then_inc(s_st, 16)
            sp.wait_ge(s_st, 16)

        @block.gpsimd
        def _(pool):
            nc.gpsimd.memset(mhalf[:], -0.5).then_inc(s_z, 1)
            pool.wait_ge(s_z, 1)
            pool.wait_ge(s_v, 2)
            nc.gpsimd.tensor_tensor(rs[:], ve[:], mhalf[:], ALU.pow).then_inc(s_r, 1)

        @block.vector
        def _(dve):
            dve.wait_ge(s_ld, 16 * 3)
            for p in range(FP):
                last = nc.vector.bn_stats(st[:, p, :], hacc[:, p, :])
            last.then_inc(s_cb, 1)
            dve.wait_ge(s_cb, 1)
            for p in range(FP):
                last = nc.vector.bn_aggr(mv[:, p, :], st[:, p, :])
            last.then_inc(s_v, 1)
            dve.wait_ge(s_v, 1)
            nc.vector.tensor_scalar(ve[:], mv[:, :, 1], EPS, None, ALU.add).then_inc(s_v, 1)
            nc.vector.tensor_copy(xf[:], ix[:]).then_inc(s_cb, 1)
            dve.wait_ge(s_r, 1)
            for p in range(FP):
                nc.vector.tensor_scalar(uu[:, p, :], hacc[:, p, :], mv[:, p, 0:1], rs[:, p:p + 1], ALU.subtract, ALU.mult).then_inc(s_u, 1)
            dve.wait_ge(s_cb, 2)
            for e in range(FE):
                last = nc.vector.scalar_tensor_tensor(part[:, e], xf[:], float(e), wt[:], ALU.is_equal, ALU.mult)
            last.then_inc(s_cb, 1)
            dve.wait_ge(s_cb, 3)
            nc.vector.tensor_tensor(comb[:], part[:, :, :, 0], part[:, :, :, 1], ALU.add).then_inc(s_cb, 1)
            dve.wait_ge(s_cb, 4)
            dve.wait_ge(s_u, FP)

            def unit(dve, i, k):
                u, g = UNITS * i + k, k % NG
                dve.wait_ge(s_o, u + 1)
                at_least(dve, s_a, FG * u)
                for j in range(FG):
                    p = FG * g + j
                    cm = comb[:, bass.ds(2 * i + k // NG, 1), p]
                    nc.vector.scalar_tensor_tensor(hacc[:, p, :], pso[k % 2][0:FR, j * D:(j + 1) * D], cm, hacc[:, p, :],
                                                   ALU.mult, ALU.add).then_inc(s_a, 1)
            units(dve, unit)

        @block.scalar
        def _(act):
            for p in range(FP):
                act.wait_ge(s_tu, p + 1)
                nc.scalar.activation(ut[:, p * FR:(p + 1) * FR], psu[:, (p % 4) * 128:(p % 4) * 128 + FR], ACT.Copy).then_inc(s_ut, 1)

            def unit(act, i, k):
                u = UNITS * i + k
                for c in range(KC):
                    act.wait_ge(s_h, KC * u + c + 1)
                    if c == 0:
                        at_least(act, s_o, u - 1 if k else UNITS * i)
                    nc.scalar.activation(ht[:, k % 2, c, :], psh[c][:, 0:GT], ACT.Gelu).then_inc(s_g, 1)
            units(act, unit)

        @block.tensor
        def _(pe):
            for p in range(FP):
                pe.wait_ge(s_u, p + 1)
                if p >= 1:
                    pe.wait_ge(s_ut, p)
                nc.tensor.transpose(psu[:, (p % 4) * 128:(p % 4) * 128 + FR], uu[:, p, :], ident).then_inc(s_tu, 1)
            pe.wait_ge(s_ut, FP)

            def up(k, u, g):
                for c in range(KC):
                    at_least(pe, s_g, KC * (u - 1) + c + 1 if k else KC * u)
                    nc.tensor.matmul(psh[c][:, 0:GT], w1s[:, k // NG, c * 128:(c + 1) * 128], ut[:, g * GT:(g + 1) * GT],
                                     start=True, stop=True).then_inc(s_h, 1)

            def down(k, u):
                pe.wait_ge(s_g, KC * (u + 1))
                at_least(pe, s_a, FG * (u - 1) if k else FG * u)
                for j in range(FG):
                    for c in range(KC):
                        last = nc.tensor.matmul(pso[k % 2][0:FR, j * D:(j + 1) * D], ht[:, k % 2, c, j * FR:(j + 1) * FR],
                                                w2s[:, k // NG, c, :], start=(c == 0), stop=(c == KC - 1))
                last.then_inc(s_o, 1)

            def turn(i):
                for k in range(UNITS):
                    u = UNITS * i + k
                    if k % NG == 0:
                        pe.wait_ge(s_w[k // NG], 32 * (i + 1))
                    up(k, u, k % NG)
                    if k:
                        down(k - 1, u - 1)
                down(UNITS - 1, UNITS * i + UNITS - 1)
            turns(pe, FE // 2, turn)


E2, K2 = 32, 2
SLOTS = 128
NBL = -(-TOK * K2 // SLOTS) + E2 - 1
TINY = 1e-30
ROOM = -(-TOK // SLOTS) + 1
EMPTY = E2 * ROOM
XW = D + 1
SPARE = NBL * SLOTS


def stage_attention(nc, pk, h_in, h3_all, xs_dram, base, dm, ssum, s_sc):
    with ExitStack() as ctx:
        def sb(name, shape, dt=F32):
            return ctx.enter_context(nc.sbuf_tensor("at_" + name, shape, dt))

        def ps(name):
            return ctx.enter_context(nc.psum_tensor("at_" + name, [128, 512], F32))

        def sem(name):
            return ctx.enter_context(nc.semaphore("at_" + name))

        def cst(name, parts=128):
            return pk[0:parts, COLS[name][0]:COLS[name][1]]

        hq = sb("hq", [PT, 4, 2, D])
        st = sb("st", [PT, 2, 2, 2, 6])
        mv = sb("mv", [PT, 2, 2, 2, 2])
        ve = sb("ve", [PT, 2, 2, 2])
        rs = sb("rs", [PT, 2, 2, 2])
        mhalf = sb("mhalf", [PT, 2])
        uu = sb("uu", [PT, 2, 2, D])
        ut = sb("ut", [D, 2, QT])
        tqk = sb("tqk", [128, 2, QT])
        tv = sb("tv", [PT, 2, D])
        qk = sb("qk", [128, 2, 2, QT])
        vv = sb("vv", [PT, 2, 2, D + 2])
        ee = sb("ee", [PT, 2, 2, PT])
        pp = sb("pp", [PT, 2, 2, PT])
        den = sb("den", [PT, 2, 2])
        rd = sb("rd", [PT, 2, 2])
        xc = sb("xc", [PT, 2, 2, D])
        copies = sb("copies", [PT, 4, 2, 2, XW])
        oh = sb("oh", [PT, 2, 2, 2, E2])
        cnt = sb("cnt", [PT, 2, 2, E2])
        nxt = sb("nxt", [PT, 2, E2])
        prod = sb("prod", [PT, 4, E2])
        posf = sb("posf", [PT, 4])
        pos = [sb(f"pos{s}", [PT, 4], I32) for s in range(2)]
        xt = sb("xt", [D, 2, QT])
        lg = sb("lg", [PT, 2, 2, E2])
        m8 = sb("m8", [PT, 2, 2, 8])
        i8 = sb("i8", [PT, 2, 2, 8], U32)
        f8 = sb("f8", [PT, 2, 2, 8])
        ld = sb("ld", [PT, 2, 2, E2])
        le = sb("le", [PT, 2, 2, E2])
        psu, psqk, psv, pss, pso, psx, psl = (ps(n) for n in ("psu", "psqk", "psv", "pss", "pso", "psx", "psl"))
        psc = ps("psc")

        s_k = sem("k")
        s_hq = [sem(f"hq{k}") for k in range(4)]
        s_va = sem("va")
        s_ra = sem("ra")
        s_u = sem("u")
        s_tu, s_ut = sem("tu"), sem("ut")
        s_pq, s_pv = sem("pq"), sem("pv")
        s_tq, s_tv = sem("tq"), sem("tv")
        s_q, s_vv = sem("q"), sem("vv")
        s_s, s_e, s_p, s_o = sem("s"), sem("e"), sem("p"), sem("o")
        s_d = sem("d")
        s_h = sem("h")
        s_vb = sem("vb")
        s_rb = sem("rb")
        s_x = sem("x")
        s_xa = sem("xa")
        s_pc = sem("pc")
        s_b = sem("b")
        s_tx, s_xt, s_l = sem("tx"), sem("xt"), sem("l")
        s_m = sem("m")
        s_le = sem("le")
        s_wv, s_wp = sem("wv"), sem("wp")

        block = ctx.enter_context(nc.Block())

        FIRST = 8
        LAST = 7
        MS = 12

        def steps(eng, turn):
            for t in range(FIRST):
                turn(t, t % 4, lambda k, t=t: 0 <= t - k < NQ)
            with eng.Fori(0, (NQ - FIRST) // 4) as i:
                for r in range(4):
                    turn(4 * i + FIRST + r, r, lambda k: True)
            for t in range(NQ, NQ + LAST):
                turn(t, t % 4, lambda k, t=t: 0 <= t - k < NQ)

        def rounds(n, r, of):
            shift = {2: 1, 4: 2}[of]
            return (n - r) >> shift

        def rows(dram, n):
            v = dram.rearrange("(n j r) d -> n r j d", j=2, r=PT)
            return v[n] if isinstance(n, int) else v[bass.ds(n, 1)].rearrange("o r j d -> (o r) j d")

        def pair_rows(a, n):
            return a[:, 2 * n:2 * n + 2] if isinstance(n, int) else a[:, bass.ds(2 * n, 2)]

        flat = lambda a: a.rearrange("p k q -> p (k q)")
        pair_cols = lambda j: slice(j * PT, (j + 1) * PT)

        @block.sync
        def _(sp):
            def load(n, r):
                at_least(sp, s_h, 2 * n - 6)
                sp.dma_start(hq[:, r], rows(h_in, n)).then_inc(s_hq[r], 16)

            def turn(t, r, live):
                if live(-1):
                    load(t + 1, (r + 1) % 4)

            load(0, 0)
            for t in range(FIRST):
                turn(t, t % 4, lambda k, t=t: 0 <= t - k < NQ)
            with sp.Fori(0, (NQ - FIRST) // 4 - 1) as i:
                for r in range(4):
                    turn(4 * i + FIRST + r, r, lambda k: True)
            for t in range(NQ - 4, NQ):
                turn(t, t % 4, lambda k, t=t: 0 <= t - k < NQ)
            for s in range(4):
                sp.wait_ge(s_sc[s], 64 * (NQ // 4))

        @block.tensor
        def _(pe):
            def transpose_u(n, s):
                pe.wait_ge(s_u, 2 * n + 2)
                at_least(pe, s_ut, n)
                for j in range(2):
                    last = nc.tensor.transpose(psu[:, pair_cols(j)], uu[:, s, j, :], cst("ident", PT)[:, 0:PT])
                last.then_inc(s_tu, 1)

            def project(n, s):
                pe.wait_ge(s_ut, n + 1)
                at_least(pe, s_tq, n)
                for k, w in enumerate(("wq", "wk")):
                    last = nc.tensor.matmul(psqk[:, k * QT:(k + 1) * QT], cst(w), ut[:, s, :], start=True, stop=True)
                last.then_inc(s_pq, 1)
                at_least(pe, s_tv, n)
                for j in range(2):
                    last = nc.tensor.matmul(psv[0:PT, j * D:(j + 1) * D], ut[:, s, pair_cols(j)], cst("wv"), start=True, stop=True)
                last.then_inc(s_pv, 1)

            def scores(n, s):
                pe.wait_ge(s_q, n + 1)
                at_least(pe, s_e, n)
                for j in range(2):
                    c = pair_cols(j)
                    last = nc.tensor.matmul(pss[0:PT, c], qk[:, s, 1, c], qk[:, s, 0, c], start=True, stop=True)
                last.then_inc(s_s, 1)

            def weighted_sum(n, s):
                pe.wait_ge(s_p, n + 1)
                pe.wait_ge(s_vv, n + 1)
                at_least(pe, s_h, 2 * n)
                for j in range(2):
                    last = nc.tensor.matmul(pso[0:PT, j * (D + 2):(j + 1) * (D + 2)], pp[:, s, j, :], vv[:, s, j, :], start=True, stop=True)
                last.then_inc(s_o, 1)

            def transpose_x(n, s):
                pe.wait_ge(s_x, 2 * n + 2)
                at_least(pe, s_xt, n)
                for j in range(2):
                    last = nc.tensor.transpose(psx[:, pair_cols(j)], xc[:, s, j, :], cst("ident", PT)[:, 0:PT])
                last.then_inc(s_tx, 1)

            def logits(n, s):
                pe.wait_ge(s_xt, n + 1)
                at_least(pe, s_m, MS * n - 10)
                for j in range(2):
                    last = nc.tensor.matmul(psl[0:PT, j * E2:(j + 1) * E2], xt[:, s, pair_cols(j)], cst("wgate"), start=True, stop=True)
                last.then_inc(s_l, 1)

            def counts(n, s):
                pe.wait_ge(s_m, MS * n + 11)
                at_least(pe, s_b, 5 * (n - 1) + 2)
                c = lambda j: psc[0:PT, j * E2:(j + 1) * E2]
                nc.tensor.matmul(c(0), cst("tri", PT), cnt[:, s, 0, :], start=True, stop=True)
                nc.tensor.matmul(c(1), cst("tri", PT), cnt[:, s, 1, :], start=True, stop=False)
                nc.tensor.matmul(c(1), cst("onem", PT)[:, 0:PT], cnt[:, s, 0, :], start=False, stop=True)
                for j in range(2):
                    last = nc.tensor.matmul(psc[:, 2 * E2:3 * E2], cst("onem", PT), cnt[:, s, j, :], start=(j == 0), stop=(j == 1))
                last.then_inc(s_pc, 1)

            def turn(t, r, live):
                s = r % 2
                if live(2):
                    scores(t - 2, s)
                if live(6):
                    counts(t - 6, s)
                if live(1):
                    transpose_u(t - 1, 1 - s)
                if live(4):
                    transpose_x(t - 4, s)
                if live(1):
                    project(t - 1, 1 - s)
                if live(4):
                    logits(t - 4, s)
                if live(2):
                    weighted_sum(t - 2, s)

            steps(pe, turn)

        @block.scalar
        def _(act):
            def turn(t, r, live):
                s = r % 2
                if live(1):
                    n = t - 1
                    act.wait_ge(s_tu, n + 1)
                    at_least(act, s_pv, n - 1)
                    nc.scalar.activation(ut[:, 1 - s, :], psu[:, 0:QT], ACT.Copy).then_inc(s_ut, 1)
                if live(2):
                    n = t - 2
                    act.wait_ge(s_s, n + 1)
                    at_least(act, s_p, n - 1)
                    nc.scalar.activation(flat(ee[:, s]), pss[0:PT, 0:2 * PT], ACT.Exp, scale=float(D) ** -0.5).then_inc(s_e, 1)
                if live(4):
                    n = t - 4
                    act.wait_ge(s_tx, n + 1)
                    at_least(act, s_l, n - 1)
                    nc.scalar.activation(xt[:, s, :], psx[:, 0:QT], ACT.Copy).then_inc(s_xt, 1)
                if live(1):
                    n = t - 1
                    act.wait_ge(s_pq, n + 1)
                    at_least(act, s_q, n)
                    nc.scalar.activation(flat(tqk[:]), psqk[:, 0:2 * QT], ACT.Tanh, scale=0.5).then_inc(s_tq, 1)
                    act.wait_ge(s_pv, n + 1)
                    at_least(act, s_vv, n)
                    nc.scalar.activation(flat(tv[:]), psv[0:PT, 0:2 * D], ACT.Tanh, scale=0.5).then_inc(s_tv, 1)
                if live(4):
                    n = t - 4
                    at_least(act, s_sc[r], 64 * rounds(n, r, 4))
                    nc.scalar.activation(copies[:, r, :, :, 0:D], xc[:, s].unsqueeze(1).broadcast_to([PT, 2, 2, D]), ACT.Copy).then_inc(s_xa, 1)
                    ids = cst("tokid", PT).rearrange("r (k m) -> r k m", k=2)
                    ids = ids[:, :, 2 * n:2 * n + 2] if isinstance(n, int) else ids[:, :, bass.ds(2 * n, 2)]
                    nc.scalar.activation(copies[:, r, :, :, D], ids, ACT.Copy).then_inc(s_xa, 1)
                if live(5):
                    n = t - 5
                    act.wait_ge(s_m, MS * n + 6)
                    at_least(act, s_m, MS * (n - 1))
                    nc.scalar.activation(le[:, 1 - s], ld[:, 1 - s], ACT.Exp).then_inc(s_le, 1)

            steps(act, turn)

        @block.vector
        def _(dve):
            for s in range(2):
                for j in range(2):
                    nc.vector.memset(vv[:, s, j, D:D + 2], 1.0).then_inc(s_k, 1)
            nc.vector.tensor_scalar(base, cst("iota32"), float(ROOM * SLOTS), None, ALU.mult).then_inc(s_k, 1)

            def stats(x, which, s, s_v):
                for j in range(2):
                    nc.vector.bn_stats(st[:, which, s, j, :], x(j)).then_inc(s_v, 1)

            def mean_var(which, n, s, s_v):
                for j in range(2):
                    wait_apart(dve, s_v, 5 * n + j + 1, s_wv)
                    nc.vector.bn_aggr(mv[:, which, s, j, :], st[:, which, s, j, :]).then_inc(s_v, 1)

            def add_eps(which, n, s, s_v):
                dve.wait_ge(s_v, 5 * n + 4)
                nc.vector.tensor_scalar(ve[:, which, s, :], mv[:, which, s, :, 1], EPS, None, ALU.add).then_inc(s_v, 1)

            def normed(x, which, s, out, s_out):
                for j in range(2):
                    nc.vector.tensor_scalar(out[:, j, :], x(j), mv[:, which, s, j, 0:1], rs[:, which, s, j:j + 1],
                                            ALU.subtract, ALU.mult).then_inc(s_out, 1)

            def turn(t, r, live):
                s = r % 2
                o = pso[0:PT, 0:2 * (D + 2)].rearrange("r (j c) -> r j c", j=2)
                n, q, e = t, t - 3, t - 5
                s1 = 1 - s
                h3 = lambda j: h3_all[:, q + q + j, :] if isinstance(q, int) else h3_all[:, bass.ds(2 * q + j, 1), :].rearrange("r o d -> r (o d)")
                c = t - 6
                if live(0):
                    dve.wait_ge(s_hq[r], 16 * (rounds(n, r, 4) + 1))
                    at_least(dve, s_u, 2 * n - 2)
                    stats(lambda j: hq[:, r, j, :], 0, s, s_va)
                if live(3):
                    dve.wait_ge(s_o, q + 1)
                    at_least(dve, s_h, 2 * q - 2)
                    nc.vector.tensor_scalar(den[:, s1, :], o[:, :, D], TINY, None, ALU.max).then_inc(s_d, 1)
                if live(5):
                    dve.wait_ge(s_l, e + 1)
                    at_least(dve, s_le, e - 1)
                    bg = cst("bgate", PT).unsqueeze(1).broadcast_to([PT, 2, E2])
                    nc.vector.tensor_tensor(lg[:, s1], psl[0:PT, 0:2 * E2].rearrange("r (j e) -> r j e", j=2), bg, ALU.add).then_inc(s_m, 1)
                if live(0):
                    mean_var(0, n, s, s_va)
                if live(6):
                    dve.wait_ge(s_pc, c + 1)
                    nc.vector.tensor_tensor(nxt[:], psc[0:PT, 0:2 * E2].rearrange("r (j e) -> r j e", j=2),
                                            base[0:PT, :].unsqueeze(1).broadcast_to([PT, 2, E2]), ALU.add).then_inc(s_b, 1)
                if live(3):
                    dve.wait_ge(s_d, 2 * q + 1)
                    nc.vector.reciprocal(rd[:, s1, :], den[:, s1, :]).then_inc(s_d, 1)
                if live(5):
                    wait_apart(dve, s_m, MS * e + 1, s_wv)
                    for j in range(2):
                        nc.vector.max(m8[:, s1, j, :], lg[:, s1, j, :]).then_inc(s_m, 1)
                if live(6):
                    dve.wait_ge(s_b, 5 * c + 1)
                    nc.vector.tensor_tensor(base, base, psc[:, 2 * E2:3 * E2], ALU.add).then_inc(s_b, 1)
                    nc.vector.tensor_tensor(prod[:].rearrange("r (k j) e -> r k (j e)", k=2), oh[:, s].rearrange("r k j e -> r k (j e)"),
                                            nxt[:].rearrange("r j e -> r (j e)").unsqueeze(1).broadcast_to([PT, 2, 2 * E2]), ALU.mult).then_inc(s_b, 1)
                if live(0):
                    add_eps(0, n, s, s_va)
                if live(3):
                    dve.wait_ge(s_d, 2 * q + 2)
                    for j in range(2):
                        nc.vector.scalar_tensor_tensor(h3(j), o[:, j, 0:D], rd[:, s1, j:j + 1], hq[:, (r - 3) % 4, j, :], ALU.mult, ALU.add).then_inc(s_h, 1)
                if live(5):
                    wait_apart(dve, s_m, MS * e + 3, s_wv)
                    for j in range(2):
                        nc.vector.max_index(i8[:, s1, j, :], m8[:, s1, j, :], lg[:, s1, j, :]).then_inc(s_m, 1)
                    nc.vector.tensor_tensor(ld[:, s1], lg[:, s1], m8[:, s1, :, 0:1].broadcast_to([PT, 2, E2]), ALU.subtract).then_inc(s_m, 1)
                if live(2):
                    dve.wait_ge(s_e, t - 1)
                    at_least(dve, s_o, t - 3)
                    nc.vector.tensor_tensor(pp[:, s], ee[:, s], cst("amask", PT).unsqueeze(1).broadcast_to([PT, 2, PT]), ALU.mult).then_inc(s_p, 1)
                if live(3):
                    wait_apart(dve, s_h, 2 * q + 2, s_wv)
                    stats(h3, 1, s1, s_vb)
                if live(5):
                    dve.wait_ge(s_m, MS * e + 5)
                    nc.vector.tensor_copy(f8[:, s1], i8[:, s1]).then_inc(s_m, 1)
                if live(0):
                    dve.wait_ge(s_ra, n + 1)
                    at_least(dve, s_tu, n - 1)
                    normed(lambda j: hq[:, r, j, :], 0, s, uu[:, s], s_u)
                if live(3):
                    mean_var(1, q, s1, s_vb)
                if live(5):
                    dve.wait_ge(s_m, MS * e + 7)
                    io = cst("iota32", PT).unsqueeze(1).broadcast_to([PT, 2, E2])
                    for k in range(2):
                        nc.vector.tensor_tensor(oh[:, s1, k], io, f8[:, s1, :, k:k + 1].broadcast_to([PT, 2, E2]), ALU.is_equal).then_inc(s_m, 1)
                if live(3):
                    add_eps(1, q, s1, s_vb)
                if live(5):
                    nc.vector.tensor_tensor(pair_rows(dm, e), m8[:, s1, :, 1], m8[:, s1, :, 0], ALU.subtract).then_inc(s_m, 1)
                    dve.wait_ge(s_m, MS * e + 9)
                    nc.vector.tensor_tensor(cnt[:, s1], oh[:, s1, 0], oh[:, s1, 1], ALU.add).then_inc(s_m, 1)
                if live(6):
                    dve.wait_ge(s_b, 5 * c + 3)
                    nc.vector.tensor_reduce(posf[:], prod[:], AX_X, ALU.add).then_inc(s_b, 1)
                if live(1):
                    dve.wait_ge(s_tq, t)
                    at_least(dve, s_s, t - 2)
                    nc.vector.tensor_scalar(qk[:, s1], tqk[:], 0.5, 0.5, ALU.mult, ALU.add).then_inc(s_q, 1)
                    dve.wait_ge(s_tv, t)
                    at_least(dve, s_o, t - 2)
                    nc.vector.tensor_scalar(vv[:, s1, :, 0:D], tv[:], 0.5, 0.5, ALU.mult, ALU.add).then_inc(s_vv, 1)
                if live(6):
                    dve.wait_ge(s_b, 5 * c + 4)
                    if not isinstance(c, int) or c >= 2:
                        dve.wait_ge(s_sc[r], 64 * rounds(t - 8, r, 4) + 64)
                    nc.vector.tensor_copy(pos[s][:], posf[:]).then_inc(s_b, 1)
                if live(3):
                    dve.wait_ge(s_rb, q + 1)
                    at_least(dve, s_tx, q - 1)
                    at_least(dve, s_xa, 2 * q - 2)
                    normed(h3, 1, s1, xc[:, s1], s_x)
                if live(5):
                    dve.wait_ge(s_le, e + 1)
                    nc.vector.tensor_reduce(pair_rows(ssum, e), le[:, s1], AX_X, ALU.add).then_inc(s_m, 1)

            steps(dve, turn)

        @block.gpsimd
        def _(pool):
            nc.gpsimd.memset(mhalf[:], -0.5).then_inc(s_k, 1)
            pool.wait_ge(s_k, 6)

            def root(which, n, s, s_v, s_out, s_r):
                pool.wait_ge(s_v, 5 * n + 5)
                at_least(pool, s_out, 2 * n - 2)
                nc.gpsimd.tensor_tensor(rs[:, which, s, :], ve[:, which, s, :], mhalf[:], ALU.pow).then_inc(s_r, 1)

            def turn(t, r, live):
                s = r % 2

                def send(*which):
                    if live(7):
                        if 0 in which:
                            pool.wait_ge(s_b, 5 * (t - 7) + 5)
                            wait_apart(pool, s_xa, 2 * (t - 7) + 2, s_wp)
                        for k in which:
                            pool.indirect_dma_start(xs_dram, bass.IndirectOffsetOnAxis(ap=pos[1 - s][:, k:k + 1], axis=0),
                                                    copies[:, (r + 1) % 4, k // 2, k % 2, :], None).then_inc(s_sc[(r + 1) % 4], 16)

                send(0, 1)
                if live(0):
                    root(0, t, s, s_va, s_u, s_ra)
                send(2)
                if live(3):
                    root(1, t - 3, 1 - s, s_vb, s_x, s_rb)
                send(3)

            steps(pool, turn)


F2 = 256
FC = F2 // 128
WB = 2 * F2 + D
PLACE, UP_DOWN, NEXT = 0, 128, 256
NROWS = NEXT + E2
UP, DOWN = 1, 4


def stage_plan(nc, pk, base, slot_rows, bias_in, bias_dram, xs_dram, s_bias):
    with ExitStack() as ctx:
        def sb(name, shape, dt=F32):
            return ctx.enter_context(nc.sbuf_tensor("pl_" + name, shape, dt))

        def sem(name):
            return ctx.enter_context(nc.semaphore("pl_" + name))

        def cst(name, parts=128):
            return pk[0:parts, COLS[name][0]:COLS[name][1]]

        n_e = sb("ne", [128, E2])
        n_i = sb("ni", [128, E2], I32)
        nb_i = sb("nbi", [128, E2], I32)
        en = [sb(f"en{k}", [128, E2]) for k in range(2)]
        nb = sb("nb", [128, E2])
        le = sb("le", [128, E2])
        first = sb("first", [128, E2])
        ebf = sb("ebf", [128, 1])
        fbf = sb("fbf", [128, 1])
        abf = sb("abf", [128, 1])
        up_down = sb("up_down", [1, 128])
        open_slots = sb("open_slots", [SLOTS, XW])
        bf = sb("bf", [E2, WB])
        bh = [sb(f"bh{k}", [E2, WB], BF16) for k in range(3)]
        br = [sb(f"br{k}", [E2, WB]) for k in range(2)]
        psr = ctx.enter_context(nc.psum_tensor("pl_psr", [128, 512], F32))

        s_ld = sem("ld")
        s_c = sem("c")
        s_z = sem("z")
        s_ee, s_ea = sem("ee"), sem("ea")
        s_row = sem("row")
        s_b = sem("b")
        s_tail = [sem(f"tail{k}") for k in range(2)]
        block = ctx.enter_context(nc.Block())

        def fill(eng, k):
            eng.wait_ge(s_z, 3)
            with eng.Fori(0, E2 // 2) as i:
                row = eng.value_load(slot_rows[0:1, bass.ds(2 * i + NEXT + k, 1)], min_val=0, max_val=EMPTY * SLOTS - SLOTS)
                eng.dma_start(xs_dram[bass.ds(row, SLOTS), :], open_slots[:]).then_inc(s_tail[k], 16)
            eng.wait_ge(s_tail[k], 16 * (E2 // 2))

        @block.sync
        def _(sp):
            for lo, src in zip((0, F2, 2 * F2), bias_in):
                sp.dma_start(bf[:, lo:lo + src.shape[1]], src).then_inc(s_ld, 16)
            fill(sp, 0)
            sp.wait_ge(s_b, 6)
            for k in range(3):
                sp.dma_start(bias_dram[:, k, :], bh[k][:]).then_inc(s_bias, 16)
            sp.dma_start(xs_dram[EMPTY * SLOTS:(EMPTY + 1) * SLOTS, :], open_slots[:]).then_inc(s_bias, 16)
            sp.wait_ge(s_bias, 64)

        @block.scalar
        def _(act):
            fill(act, 1)

        @block.tensor
        def _(pe):
            pe.wait_ge(s_ee, 1)
            nc.tensor.matmul(psr[0:1, 0:128], ebf[:], cst("ident"), start=True, stop=True)
            pe.wait_ge(s_ea, 1)
            nc.tensor.matmul(psr[0:1, 128:256], abf[:], cst("ident"), start=True, stop=True).then_inc(s_row, 1)

        @block.gpsimd
        def _(pool):
            nc.gpsimd.memset(open_slots[:, 0:D], 0.0).then_inc(s_z, 1)
            nc.gpsimd.memset(open_slots[:, D:XW], -1.0).then_inc(s_z, 1)
            pool.wait_ge(s_ld, 48)
            nc.gpsimd.tensor_copy(bh[0][:], bf[:]).then_inc(s_b, 1)
            pool.wait_ge(s_b, 1)
            nc.gpsimd.tensor_tensor(br[0][:], bf[:], bh[0][:], ALU.subtract).then_inc(s_b, 1)
            pool.wait_ge(s_b, 2)
            nc.gpsimd.tensor_copy(bh[1][:], br[0][:]).then_inc(s_b, 1)
            pool.wait_ge(s_b, 3)
            nc.gpsimd.tensor_tensor(br[1][:], br[0][:], bh[1][:], ALU.subtract).then_inc(s_b, 1)
            pool.wait_ge(s_b, 4)
            nc.gpsimd.tensor_copy(bh[2][:], br[1][:]).then_inc(s_b, 2)

        @block.vector
        def _(dve):
            c = [0]

            def then(ins):
                ins.then_inc(s_c, 1)
                c[0] += 1
                dve.wait_ge(s_c, c[0])

            nc.vector.tensor_copy(slot_rows[0:1, NEXT:NEXT + E2], base[0:1, :]).then_inc(s_z, 1)
            then(nc.vector.scalar_tensor_tensor(n_e[:], cst("iota32"), -float(ROOM * SLOTS), base, ALU.mult, ALU.add))
            then(nc.vector.tensor_scalar(n_e[:], n_e[:], float(SLOTS - 1), None, ALU.add))
            then(nc.vector.tensor_copy(n_i[:], n_e[:]))
            then(nc.vector.tensor_scalar(nb_i[:], n_i[:], SLOTS.bit_length() - 1, None, ALU.logical_shift_right))
            then(nc.vector.tensor_copy(nb[:], nb_i[:]))
            a, b = nb, en[0]
            other = en[1]
            step = 1
            while step < E2:
                then(nc.vector.tensor_copy(b[:, :step], a[:, :step]))
                then(nc.vector.tensor_tensor(b[:, step:], a[:, step:], a[:, :E2 - step], ALU.add))
                a, b = b, (other if b is en[0] else en[0])
                step *= 2
            then(nc.vector.tensor_scalar(le[:], a[:], cst("bcol"), None, ALU.is_le))
            then(nc.vector.tensor_reduce(ebf[:], le[:], AX_X, ALU.add))
            then(nc.vector.tensor_tensor(first[:], le[:], nb[:], ALU.mult))
            then(nc.vector.tensor_reduce(fbf[:], first[:], AX_X, ALU.add))
            then(nc.vector.scalar_tensor_tensor(abf[:], ebf[:], float(ROOM), cst("bcol"), ALU.mult, ALU.add))
            then(nc.vector.tensor_tensor(abf[:], abf[:], fbf[:], ALU.subtract))
            then(nc.vector.tensor_scalar(abf[:], abf[:], float(EMPTY), None, ALU.min))
            nc.vector.tensor_scalar(ebf[:], ebf[:], float(E2 - 1), None, ALU.min).then_inc(s_ee, 1)
            dve.wait_ge(s_ee, 1)
            nc.vector.scalar_tensor_tensor(abf[:], abf[:], float(E2), ebf[:], ALU.mult, ALU.add).then_inc(s_ea, 1)
            dve.wait_ge(s_row, 1)
            then(nc.vector.tensor_copy(slot_rows[0:1, PLACE:PLACE + 128], psr[0:1, 128:256]))
            then(nc.vector.memset(up_down[:, 0:UP], 0.0))
            then(nc.vector.tensor_copy(up_down[:, UP:], psr[0:1, 0:128 - UP]))
            then(nc.vector.scalar_tensor_tensor(up_down[:, DOWN:], psr[0:1, 0:128 - DOWN], float(E2), up_down[:, DOWN:], ALU.mult, ALU.add))
            then(nc.vector.tensor_copy(slot_rows[0:1, UP_DOWN:UP_DOWN + 128], up_down[:]))


def stage_experts(nc, pk, h3_all, slot_rows, dm, ssum, wgu, wd, bias_dram, xs_dram, ys_dram, out_dram, s_w, n_w, s_st):
    with ExitStack() as ctx:
        def sb(name, shape, dt=F32):
            return ctx.enter_context(nc.sbuf_tensor("ex_" + name, shape, dt))

        def ps(name):
            return ctx.enter_context(nc.psum_tensor("ex_" + name, [128, 512], F32))

        def sem(name):
            return ctx.enter_context(nc.semaphore("ex_" + name))

        def cst(name, parts=128):
            return pk[0:parts, COLS[name][0]:COLS[name][1]]

        RING = 4
        CP = 8
        xb = sb("xb", [SLOTS, RING, XW])
        rows_to = [sb(f"rows_to{k}", [SLOTS, 1], I32) for k in range(RING)]
        bb = sb("bb", [3, RING, 2 * F2], BF16)
        bdown = sb("bdown", [3, E2, D], BF16)
        one3 = sb("one3", [3, SLOTS], BF16)
        spares = sb("spares", [SLOTS, 128])
        xt = sb("xt", [D, 2, SLOTS])
        sg = sb("sg", [SLOTS, 2, F2])
        hh = sb("hh", [SLOTS, 2, F2])
        ht = sb("ht", [128, 2, FC, SLOTS])
        yb = sb("yb", [SLOTS, RING, D])
        pw = sb("pw", [PT, 2, NP])
        pw2 = sb("pw2", [PT, NP])
        yy = sb("yy", [PT, 2, 2, CP, D])
        ha = sb("ha", [PT, 2, CP, D])
        ho = sb("ho", [PT, 2, CP, D])
        psx = ps("psx")
        psg = [ps("psg0"), ps("psg1")]
        psh = [ps("psh0"), ps("psh1")]
        psy = [ps("psy0"), ps("psy1")]

        s_k = sem("k")
        s_x = [sem(f"x{k}") for k in range(RING)]
        s_tx, s_xt, s_g, s_sg, s_hh, s_th, s_ht, s_y, s_yb = (sem(n) for n in ("tx", "xt", "g", "sg", "hh", "th", "ht", "y", "yb"))
        s_to = sem("to")
        s_pw = sem("pw")
        s_wp, s_ws = sem("wp"), sem("ws")
        s_yy = [sem(f"yy{k}") for k in range(2)]
        s_bd = sem("bd")
        s_bi = [sem(f"bi{k}") for k in range(RING)]
        s_a = sem("a")
        s_out = [sem(f"out{k}") for k in range(2)]

        block = ctx.enter_context(nc.Block())
        PEEL = 8
        TURNS = (NBL - DOWN - PEEL) // RING
        REST = PEEL + RING * TURNS

        def steps(eng, step):
            for n in range(PEEL):
                step(eng, n, n % RING, n)
            with eng.Fori(0, TURNS) as i:
                for k in range(RING):
                    step(eng, RING * i + PEEL + k, (PEEL + k) % RING, None)
            for n in range(REST, NBL + DOWN):
                step(eng, n, n % RING, n)

        def live(known, back):
            return known is None or 0 <= known - back < NBL

        def rows(dram, n):
            v = dram.rearrange("(n s) d -> n s d", s=SLOTS)
            return v[n] if isinstance(n, int) else v[bass.ds(n, 1)].rearrange("o s d -> (o s) d")

        def of_block(eng, at, n, most):
            return eng.value_load(slot_rows[0:1, at + n:at + n + 1] if isinstance(n, int) else slot_rows[0:1, bass.ds(n + at, 1)], min_val=0, max_val=most)

        def halves(both, most):
            high = nc.s_assert_within(both >> (E2.bit_length() - 1), 0, most,
                                      skip_runtime_bounds_check_because="both is at most most * E2 + E2 - 1")
            return high, both & (E2 - 1)

        results = ys_dram[SPARE:SPARE + 2 * TOK].rearrange("(k p r) d -> r k p d", k=2, r=PT)
        outs = out_dram.rearrange("(p r) d -> r p d", r=PT)

        @block.gpsimd
        def _(pool):
            nc.gpsimd.memset(one3[:], 1.0).then_inc(s_k, 1)

            def step(pool, n, s, known):
                if live(known, DOWN):
                    b, r = n - DOWN, (s - DOWN) % RING
                    pool.wait_ge(s_to, b + 1)
                    wait_apart(pool, s_yb, b + 1, s_wp)
                    pool.indirect_dma_start(ys_dram, bass.IndirectOffsetOnAxis(ap=rows_to[r][:], axis=0), yb[:, r, :], None).then_inc(s_st[r], 16)

            steps(pool, step)
            for r in range(RING):
                pool.wait_ge(s_st[r], 16 * ((NBL + RING - 1 - r) // RING))
            pool.sem_inc(s_k, 1)

        @block.sync
        def _(sp):
            def load(m, s):
                place, e = halves(of_block(sp, PLACE, m, EMPTY * E2 + E2 - 1), EMPTY)
                sp.dma_start(xb[:, s, :], rows(xs_dram, place)).then_inc(s_x[s], 16)
                if not isinstance(m, int) or m >= RING:
                    wait_apart(sp, s_g, m - RING + 1, s_ws)
                sp.dma_start(bb[:, s, :], bias_dram[bass.ds(e, 1), :, 0:2 * F2].rearrange("o k w -> (o k) w")).then_inc(s_bi[s], 16)

            for m in range(3):
                load(m, m)
            sp.dma_start(bdown[:], bias_dram[:, :, 2 * F2:].rearrange("e k w -> k e w")).then_inc(s_bd, 16)

            def step(sp, n, s, known):
                if known is None or known + 3 < NBL:
                    at_least(sp, s_tx, n)
                    at_least(sp, s_to, n)
                    load(n + 3, (s + 3) % RING)

            steps(sp, step)
            sp.wait_ge(s_k, 2)

            def load_results(q, s):
                for k in range(K2):
                    src = results[:, k, q * CP:(q + 1) * CP, :] if isinstance(q, int) else results[:, k, bass.ds(q * CP, CP), :]
                    sp.dma_start(yy[:, s, k], src).then_inc(s_yy[s], 16)

            for q in range(2):
                load_results(q, q)

            def turn(i, more):
                for s in range(2):
                    q = 2 * i + s
                    sp.wait_ge(s_a, 2 * CP * (q + 1))
                    dst = outs[:, q * CP:(q + 1) * CP, :] if isinstance(q, int) else outs[:, bass.ds(q * CP, CP), :]
                    sp.dma_start(dst, ho[:, s]).then_inc(s_out[s], 16)
                    if more:
                        load_results(q + 2, s)

            with sp.Fori(0, NP // CP // 2 - 1) as i:
                turn(i, True)
            turn(NP // CP // 2 - 1, False)
            for s in range(2):
                sp.wait_ge(s_out[s], 16 * (NP // CP // 2))

        @block.tensor
        def _(pe):
            pe.wait_ge(s_w, n_w)
            pe.wait_ge(s_k, 1)
            pe.wait_ge(s_bd, 16)

            def step(pe, n, s, known):
                up_down = of_block(pe, UP_DOWN, n, E2 * E2 - 1)
                down, up = halves(up_down, E2 - 1)
                if live(known, 0):
                    pe.wait_ge(s_x[s], 16 * (((n - s) >> 2) + 1))
                    at_least(pe, s_xt, n)
                    nc.tensor.transpose(psx[:, 0:SLOTS], xb[:, s, 0:D], cst("ident")).then_inc(s_tx, 1)
                if live(known, 3):
                    b, r = n - 3, (s - 3) % RING
                    pe.wait_ge(s_hh, b + 1)
                    at_least(pe, s_ht, b - 1)
                    for c in range(FC):
                        last = nc.tensor.transpose(psh[r % 2][:, c * SLOTS:(c + 1) * SLOTS], hh[:, r % 2, c * 128:(c + 1) * 128], cst("ident"))
                    last.then_inc(s_th, 1)
                if live(known, DOWN):
                    b, r = n - DOWN, (s - DOWN) % RING
                    pe.wait_ge(s_ht, b + 1)
                    at_least(pe, s_yb, b - 1)
                    nc.tensor.matmul(psy[r % 2][:, 0:D], one3[:], bdown[:, bass.ds(down, 1), :].rearrange("p o d -> p (o d)"), start=True, stop=False)
                    for c in range(FC):
                        last = nc.tensor.matmul(psy[r % 2][:, 0:D], ht[:, r % 2, c, :], wd[:, bass.ds(down, 1), c, :].rearrange("p o d -> p (o d)"), start=False, stop=(c == FC - 1))
                    last.then_inc(s_y, 1)
                if live(known, UP):
                    b, r = n - UP, (s - UP) % RING
                    pe.wait_ge(s_xt, b + 1)
                    pe.wait_ge(s_bi[r], 16 * (((b - r) >> 2) + 1))
                    at_least(pe, s_hh, b - 1)
                    nc.tensor.matmul(psg[r % 2][:], one3[:], bb[:, r, :], start=True, stop=False)
                    nc.tensor.matmul(psg[r % 2][:], xt[:, r % 2, :], wgu[:, bass.ds(up, 1), :].rearrange("p o f -> p (o f)"), start=False, stop=True).then_inc(s_g, 1)

            steps(pe, step)

        @block.scalar
        def _(act):
            nc.scalar.activation(pw[:, 1, :], dm, ACT.Exp).then_inc(s_pw, 1)

            def step(act, n, s, known):
                if live(known, 0):
                    act.wait_ge(s_tx, n + 1)
                    at_least(act, s_g, n - 1)
                    nc.scalar.activation(xt[:, s % 2, :], psx[:, 0:SLOTS], ACT.Copy).then_inc(s_xt, 1)
                if live(known, 3):
                    b, r = n - 3, (s - 3) % 2
                    act.wait_ge(s_th, b + 1)
                    at_least(act, s_y, b - 1)
                    nc.scalar.activation(ht[:, r].rearrange("p c s -> p (c s)"), psh[r][:, 0:FC * SLOTS], ACT.Copy).then_inc(s_ht, 1)
                if live(known, UP):
                    b, r = n - UP, (s - UP) % 2
                    act.wait_ge(s_g, b + 1)
                    at_least(act, s_hh, b - 1)
                    nc.scalar.activation(sg[:, r, :], psg[r][:, 0:F2], ACT.Silu).then_inc(s_sg, 1)

            steps(act, step)

        @block.vector
        def _(dve):
            nc.vector.reciprocal(pw[:, 0, :], ssum).then_inc(s_pw, 1)
            nc.vector.tensor_scalar(spares[:], cst("block0"), cst("bcol"), None, ALU.add).then_inc(s_pw, 1)
            dve.wait_ge(s_pw, 3)
            nc.vector.tensor_tensor(pw2[:], pw[:, 1, :], pw[:, 0, :], ALU.mult).then_inc(s_pw, 1)

            def step(dve, n, s, known):
                if live(known, DOWN):
                    b, r = n - DOWN, (s - DOWN) % RING
                    dve.wait_ge(s_y, b + 1)
                    at_least(dve, s_st[r], 16 * ((b - r) >> 2))
                    nc.vector.tensor_copy(yb[:, r, :], psy[r % 2][:, 0:D]).then_inc(s_yb, 1)
                if live(known, UP):
                    b, r = n - UP, (s - UP) % 2
                    dve.wait_ge(s_sg, b + 1)
                    at_least(dve, s_th, b - 1)
                    nc.vector.tensor_tensor(hh[:, r, :], sg[:, r, :], psg[r][:, F2:2 * F2], ALU.mult).then_inc(s_hh, 1)
                if live(known, UP):
                    b, r = n - UP, (s - UP) % RING
                    dve.wait_ge(s_tx, b + 1)
                    at_least(dve, s_st[r], 16 * ((b - r) >> 2))
                    spare = spares[:, b:b + 1] if isinstance(n, int) else spares[:, bass.ds(b, 1)]
                    nc.vector.tensor_tensor(rows_to[r][:], xb[:, r, D:XW], spare, ALU.max).then_inc(s_to, 1)

            steps(dve, step)
            dve.wait_ge(s_pw, 4)

            def turn(i):
                for s in range(2):
                    q = 2 * i + s
                    dve.wait_ge(s_yy[s], 32 * (i + 1))
                    at_least(dve, s_out[s], 16 * i)
                    for j in range(CP):
                        p = q * CP + j
                        h3 = h3_all[:, bass.ds(p, 1), :].rearrange("r o d -> r (o d)")
                        nc.vector.scalar_tensor_tensor(ha[:, s, j, :], yy[:, s, 0, j, :], pw[:, 0, bass.ds(p, 1)], h3,
                                                       ALU.mult, ALU.add).then_inc(s_a, 1)
                    for j in range(CP):
                        p = q * CP + j
                        dve.wait_ge(s_a, 2 * CP * q + j + 1)
                        nc.vector.scalar_tensor_tensor(ho[:, s, j, :], yy[:, s, 1, j, :], pw2[:, bass.ds(p, 1)], ha[:, s, j, :],
                                                       ALU.mult, ALU.add).then_inc(s_a, 1)

            turns(dve, NP // CP // 2, turn)


def bass_audio_tower_kernel(nc, x, small, e_w, e_i, w1, w2, wg, wu, wd_, bg, bu, bd, out):
    def dram(name, shape, dt=F32):
        return nc.dram_tensor(name, shape, dt, kind="Internal").ap()

    h0, h1 = (dram(n, [TOK, D]) for n in ("h0", "h1"))
    dt_dram, a_dram = (dram(n, [B, T * 8]) for n in ("steps_dt", "steps_a"))
    xs_dram = dram("slots_x", [(EMPTY + 1) * SLOTS, XW])
    ys_dram = dram("results", [SPARE + K2 * TOK, D])
    bias_dram = dram("bias_parts", [E2, 3, WB], BF16)

    with ExitStack() as ctx:
        def sb(name, shape, dt=F32):
            return ctx.enter_context(nc.sbuf_tensor(name, shape, dt))

        s_pack, s_bias, s_w = (ctx.enter_context(nc.semaphore(n)) for n in ("s_pack", "s_bias", "s_w"))
        s_sent, s_back = ([ctx.enter_context(nc.semaphore(f"{n}{k}")) for k in range(4)] for n in ("s_sent", "s_back"))
        pk = sb("pk", [128, NPACK])
        wgu = sb("wgu", [D, E2, 2 * F2])
        wd = sb("wd", [128, E2, FC, D])
        loads = [
            (lambda e: wgu[:, e, 0:F2], lambda e: wg[e].rearrange("o d f -> d o f"), s_w),
            (lambda e: wgu[:, e, F2:2 * F2], lambda e: wu[e].rearrange("o d f -> d o f"), s_w),
            (lambda e: wd[:, e].rearrange("p o c d -> p (o c) d"), lambda e: wd_[e].rearrange("o (c p) d -> p (o c) d", p=128), s_w),
        ]
        with nc.sbuf_tensor("u_t", [D, TOK], F32) as u_t:
            stage_patches(nc, x, u_t[:], dt_dram, a_dram, h0, pk, s_pack, small)
            stage_mamba(nc, u_t[:], pk, dt_dram, a_dram, h0, h1, loads)
        stage_ffn(nc, pk, h1, e_w, e_i, w1, w2)
        slot_rows = sb("slot_rows", [1, NROWS], I32)
        base = sb("base", [128, E2])
        dm = sb("dm", [PT, NP])
        ssum = sb("ssum", [PT, NP])
        with nc.sbuf_tensor("h3_all", [PT, NP, D], F32) as h3_all:
            stage_attention(nc, pk, h1, h3_all[:], xs_dram, base[:], dm[:], ssum[:], s_sent)
            stage_plan(nc, pk, base[:], slot_rows, (bg, bu, bd), bias_dram, xs_dram, s_bias)
            stage_experts(nc, pk, h3_all[:], slot_rows, dm[:], ssum[:], wgu[:], wd[:], bias_dram, xs_dram, ys_dram,
                          out.rearrange("b t d -> (b t) d"), s_w, 16 * len(loads) * NQ, s_back)
def pack(i):
    f = np.float32
    r = np.arange(PT); b, t = r // T, r % T
    same = b[:, None] == b[None]
    tt = np.arange(T)
    p = {}
    p["ident"] = np.eye(128)
    p["later_f"] = same & (t[:, None] > t[None]); p["later_b"] = same & (t[:, None] < t[None])
    p["upto_f"] = t[:, None] <= tt[None]; p["upto_b"] = t[:, None] >= tt[None]
    p["gmask_f"] = same & (t[:, None] <= t[None]); p["gmask_b"] = same & (t[:, None] >= t[None])
    p["amask"] = same & (t[:, None] < t[None])
    p["tri"] = r[:, None] < r[None]
    p["iota32"] = np.broadcast_to(np.arange(32), (128, 32))
    token = SPARE + np.arange(NP)[None, :] * PT + r[:, None]
    p["tokid"] = np.stack([token, token + TOK], 1).reshape(PT, 2 * NP)
    p["block0"] = np.broadcast_to(np.arange(128) * SLOTS, (128, 128))
    p["bcol"] = np.arange(128)[:, None]
    p["ones"] = np.ones((128, 2)); p["onem"] = np.ones((128, 128))
    p["tokw"] = i["L0_tok_W"].reshape(64, 2, 8, 128).transpose(1, 2, 0, 3).reshape(8, 128, 128).transpose(1, 0, 2).reshape(128, 1024)
    p["tokb"] = i["L0_tok_b"][:, None]
    row = lambda a: np.broadcast_to(a[None], (128, a.size))
    p["gamma"] = row(i["L0_tok_gamma"]); p["beta"] = row(i["L0_tok_beta"])
    m = lambda d, n: np.asarray(i[f"L0_attn_{d}_{n}"])
    wi = {d: m(d, "in_proj_w") for d in ("fwd", "bwd")}
    both = lambda n: np.concatenate([m("fwd", n), m("bwd", n)])
    p["wdt"] = np.concatenate([wi["fwd"][544:], wi["bwd"][544:]]).T
    p["dtb"] = row(both("dt_bias")); p["alog"] = row(both("A_log"))
    p["wz"] = np.concatenate([wi["fwd"][:256], wi["bwd"][:256]]).T
    def tiles(a):
        n = a["fwd"].shape[1]
        bc = np.zeros((128, n), f)
        bc[0:16], bc[32:48], bc[64:80], bc[96:112] = a["fwd"][256:272], a["fwd"][272:], a["bwd"][256:272], a["bwd"][272:]
        return [a["fwd"][:128], a["fwd"][128:256], a["bwd"][:128], a["bwd"][128:256], bc]
    p["wx"] = np.concatenate([w.T for w in tiles({d: wi[d][256:544] for d in wi})], 1)
    p["cw"] = np.stack(tiles({d: m(d, "conv_w")[:, 0] for d in wi}), 1).reshape(128, 20)
    p["cb"] = np.stack(tiles({d: m(d, "conv_b")[:, None] for d in wi}), 1).reshape(128, 5)
    p["dcol"] = np.repeat(both("Dp"), 64).reshape(4, 128).T
    p["wo"] = np.concatenate([m("fwd", "out_proj_w"), m("bwd", "out_proj_w")], 1).T.reshape(4, 128, 128).transpose(1, 0, 2).reshape(128, 512)
    p["nw"] = both("norm_w").reshape(4, 128).T
    p["wq"], p["wk"], p["wv"] = i["L1_attn_Wq"], i["L1_attn_Wv"], i["L1_attn_Wk"]
    p["wgate"] = i["L1_ffn_Wgate"]; p["bgate"] = row(i["L1_ffn_bgate"])
    out = np.zeros((128, NPACK), f)
    for n, a in p.items():
        c = COLS[n]; a = np.asarray(a); out[:a.shape[0], c[0]:c[1]] = a
    return out


_L = "L1_ffn_"
_AS_THEY_ARE = ["L0_ffn_expert_weights", "L0_ffn_expert_indices", "L0_ffn_w1", "L0_ffn_w2",
                _L + "Wg", _L + "Wu", _L + "Wd", _L + "bg", _L + "bu", _L + "bd"]


def kernel(**inputs):
    import concourse.bacc as bacc
    from concourse.bass_utils import run_bass_kernel_spmd as run

    nc = bacc.Bacc("TRN2", target_bir_lowering=False, num_devices=1)
    arrays, args = {}, []
    given = {n: np.ascontiguousarray(a) for n, a in inputs.items()}
    for name, a in [("x", given["x"]), ("small", pack(given))] + [(n, given[n]) for n in _AS_THEY_ARE]:
        arrays[f"in_{name}"] = a
        args.append(nc.dram_tensor(f"in_{name}", a.shape, mybir.dt.from_np(a.dtype), kind="ExternalInput").ap())
    out = nc.dram_tensor("out", (B, T, D), F32, kind="ExternalOutput").ap()
    bass_audio_tower_kernel(nc, *args, out)
    return run(nc, [arrays], core_ids=[0]).results[0]["out"]
```
